# Optimizing a Trainium2 kernel written in Bass

```python
import numpy as np
import jax
import jax.numpy as jnp

def _softmax(x, axis=-1):
    return jax.nn.softmax(x, axis=axis)

def _gelu(x):
    return jax.nn.gelu(x, approximate=True)

def _silu(x):
    return jax.nn.silu(x)

def _sigmoid(x):
    return jax.nn.sigmoid(x)

def _layernorm(x, axis=-1, eps=1e-05):
    m = jnp.mean(x, axis=axis, keepdims=True)
    v = jnp.var(x, axis=axis, keepdims=True)
    return (x - m) / jnp.sqrt(v + eps)

def _scatter_add(tgt, idx, src, axis=0):
    return tgt.at[idx].add(src)

def _segment_sum(src, seg, n):
    return jax.ops.segment_sum(src, seg, n)
kernel_name = 'mk_lm_tower_d2_tok_ids256_r4_019969'

def setup_inputs(seed: int=0):
    np.random.seed(seed)
    _w = jnp.asarray

    def _rec_inputs():
        import jax
        import jax.numpy as jnp
        _rk = jax.random.key(seed)
        x = jax.random.randint(jax.random.fold_in(_rk, 1), (64, 256), 0, 64, jnp.int32)
        return x
    x = _rec_inputs()

    def _L0_tok_setup():
        import jax, jax.numpy as jnp
        import numpy as np
        PRIME = 31
        VOCAB = 125000
        NGRAM_SIZES = (2, 3, 4)

        def _ngram_hash(byte_ids, n):
            T = byte_ids.shape[1]
            powers = PRIME ** jnp.arange(n - 1, -1, -1, dtype=jnp.int64) % VOCAB
            windows = jnp.stack([byte_ids[:, i:T - n + 1 + i] for i in range(n)], axis=-1)
            return (windows.astype(jnp.int64) * powers).sum(axis=-1) % VOCAB
        key = jax.random.key(seed)
        k0, k1, k2, k3 = jax.random.split(key, 4)
        byte_ids = jax.random.randint(k0, (8, 1024), 0, 64, dtype=jnp.int64)
        emb_2 = jax.random.normal(k1, (VOCAB, 64), dtype=jnp.float32)
        emb_3 = jax.random.normal(k2, (VOCAB, 64), dtype=jnp.float32)
        emb_4 = jax.random.normal(k3, (VOCAB, 64), dtype=jnp.float32)
        return {'byte_ids': byte_ids, 'emb_2': emb_2, 'emb_3': emb_3, 'emb_4': emb_4}
    _L0_tok_all = _L0_tok_setup()
    _L0_tok_in = {k: v for k, v in _L0_tok_all.items() if k in ('emb_2', 'emb_3', 'emb_4')}
    del _L0_tok_all

    def _L0_attn_setup():
        import jax, jax.numpy as jnp
        import numpy as np
        import math
        PI = math.pi

        def _encode_phase(x, w1, b1, w2, b2):
            h = jnp.tanh(jnp.einsum('bld,ed->ble', x, w1) + b1)
            return jnp.tanh(jnp.einsum('bld,kd->blk', h, w2) + b2) * PI
        key = jax.random.key(seed)
        ks = jax.random.split(key, 12)
        B, L, D, K = (2, 512, 64, 32)
        s = 0.02
        return {'x': jax.random.normal(ks[0], (B, L, D), dtype=jnp.float32), 'kw1': jax.random.normal(ks[1], (D, D), dtype=jnp.float32) * s, 'kb1': jnp.zeros((D,), dtype=jnp.float32), 'kw2': jax.random.normal(ks[2], (K, D), dtype=jnp.float32) * s, 'kb2': jnp.zeros((K,), dtype=jnp.float32), 'qw1': jax.random.normal(ks[3], (D, D), dtype=jnp.float32) * s, 'qb1': jnp.zeros((D,), dtype=jnp.float32), 'qw2': jax.random.normal(ks[4], (K, D), dtype=jnp.float32) * s, 'qb2': jnp.zeros((K,), dtype=jnp.float32), 'vw': jax.random.normal(ks[5], (D, D), dtype=jnp.float32) * s, 'vb': jnp.zeros((D,), dtype=jnp.float32)}
    _L0_attn_all = _L0_attn_setup()
    _L0_attn_in = {k: v for k, v in _L0_attn_all.items() if k in ('kw1', 'kb1', 'kw2', 'kb2', 'qw1', 'qb1', 'qw2', 'qb2', 'vw', 'vb')}
    del _L0_attn_all

    def _L0_ffn_setup():
        import jax, jax.numpy as jnp
        import numpy as np
        B, N, D = (16, 1024, 64)
        NUM_EXPERTS, TOP_K, HEADS = (4, 2, 4)
        N_EDGES = 262144
        LN_EPS = 1e-05

        def _layernorm(x, g, b):
            mu = x.mean(-1, keepdims=True)
            var = ((x - mu) ** 2).mean(-1, keepdims=True)
            return (x - mu) * jax.lax.rsqrt(var + LN_EPS) * g + b

        def _forward(x, edge_index, W_gat, att_src, att_dst, b_gat, ln_gamma, ln_beta, W1, b1, W2, b2):
            Bc, Nc, Dc = x.shape
            M = Bc * Nc
            x_flat = x.reshape(M, Dc)
            h = (x_flat @ W_gat).reshape(M, HEADS, NUM_EXPERTS)
            loops = jnp.arange(M, dtype=edge_index.dtype)
            src = jnp.concatenate([edge_index[0], loops])
            dst = jnp.concatenate([edge_index[1], loops])
            a_src = (h * att_src).sum(-1)
            a_dst = (h * att_dst).sum(-1)
            e = jax.nn.leaky_relu(a_src[src] + a_dst[dst], negative_slope=0.2)
            e_max = jax.ops.segment_max(e, dst, num_segments=M)
            ee = jnp.exp(e - e_max[dst])
            denom = jax.ops.segment_sum(ee, dst, num_segments=M)
            alpha = ee / (denom[dst] + 1e-16)
            msg = h[src] * alpha[:, :, None]
            agg = jax.ops.segment_sum(msg, dst, num_segments=M).reshape(M, HEADS * NUM_EXPERTS) + b_gat
            scores = _layernorm(agg, ln_gamma, ln_beta).reshape(M, HEADS, NUM_EXPERTS).mean(1)
            scores = scores.reshape(Bc, Nc, NUM_EXPERTS)
            topk_s, topk_i = jax.lax.top_k(scores, TOP_K)
            w = jax.nn.softmax(topk_s, axis=-1)
            out = jnp.zeros_like(x)
            for ei in range(NUM_EXPERTS):
                g = jnp.where(topk_i == ei, w, 0.0).sum(-1)
                hh = jax.nn.gelu(x @ W1[ei] + b1[ei], approximate=False)
                out = out + g[..., None] * (hh @ W2[ei] + b2[ei])
            return out
        key = jax.random.key(seed)
        ks = jax.random.split(key, 8)
        s = 0.05
        return {'x': jax.random.normal(ks[0], (B, N, D), jnp.float32), 'W_gat': jax.random.normal(ks[1], (D, HEADS * NUM_EXPERTS), jnp.float32) * s, 'att_src': jax.random.normal(ks[2], (HEADS, NUM_EXPERTS), jnp.float32) * s, 'att_dst': jax.random.normal(ks[3], (HEADS, NUM_EXPERTS), jnp.float32) * s, 'b_gat': jnp.zeros((HEADS * NUM_EXPERTS,), jnp.float32), 'ln_gamma': jnp.ones((HEADS * NUM_EXPERTS,), jnp.float32), 'ln_beta': jnp.zeros((HEADS * NUM_EXPERTS,), jnp.float32), 'W1': jax.random.normal(ks[4], (NUM_EXPERTS, D, 2 * D), jnp.float32) * s, 'b1': jnp.zeros((NUM_EXPERTS, 2 * D), jnp.float32), 'W2': jax.random.normal(ks[5], (NUM_EXPERTS, 2 * D, D), jnp.float32) * s, 'b2': jnp.zeros((NUM_EXPERTS, D), jnp.float32), 'edge_index': jax.random.randint(ks[6], (2, N_EDGES), 0, B * N, jnp.int32)}
    _L0_ffn_all = _L0_ffn_setup()
    _L0_ffn_in = {k: v for k, v in _L0_ffn_all.items() if k in ('W_gat', 'att_src', 'att_dst', 'b_gat', 'ln_gamma', 'ln_beta', 'W1', 'b1', 'W2', 'b2', 'edge_index')}
    del _L0_ffn_all

    def _L1_attn_setup():
        import jax, jax.numpy as jnp
        import numpy as np
        MIDC = 64
        HEADS = 16
        HEADC = MIDC // HEADS
        EPS = 1e-05

        def _layernorm(x, w, b):
            mean = jnp.mean(x, axis=-1, keepdims=True)
            std = jnp.std(x, axis=-1, keepdims=True, ddof=1)
            return w * (x - mean) / (std + EPS) + b
        key = jax.random.key(seed)
        ks = jax.random.split(key, 3)
        B, HW = (8, 4096)
        x = jax.random.normal(ks[0], (B, HW, MIDC), dtype=jnp.float32)
        W_qkv = jax.random.normal(ks[1], (3 * MIDC, MIDC), dtype=jnp.float32) * 0.02
        b_qkv = jnp.zeros((3 * MIDC,), dtype=jnp.float32)
        kln_w = jnp.ones((HEADS, 1, HEADC), dtype=jnp.float32)
        kln_b = jnp.zeros((HEADS, 1, HEADC), dtype=jnp.float32)
        vln_w = jnp.ones((HEADS, 1, HEADC), dtype=jnp.float32)
        vln_b = jnp.zeros((HEADS, 1, HEADC), dtype=jnp.float32)
        W_proj = jax.random.normal(ks[2], (MIDC, MIDC), dtype=jnp.float32) * 0.02
        b_proj = jnp.zeros((MIDC,), dtype=jnp.float32)
        return {'x': x, 'W_qkv': W_qkv, 'b_qkv': b_qkv, 'kln_w': kln_w, 'kln_b': kln_b, 'vln_w': vln_w, 'vln_b': vln_b, 'W_proj': W_proj, 'b_proj': b_proj}
    _L1_attn_all = _L1_attn_setup()
    _L1_attn_in = {k: v for k, v in _L1_attn_all.items() if k in ('W_qkv', 'b_qkv', 'kln_w', 'kln_b', 'vln_w', 'vln_b', 'W_proj', 'b_proj')}
    del _L1_attn_all

    def _L1_ffn_setup():
        import jax, jax.numpy as jnp
        import numpy as np
        B, S, D = (8, 1024, 64)
        H = 4 * D
        CAPACITY = 0.5
        key = jax.random.key(seed)
        ks = jax.random.split(key, 6)
        x = jax.random.normal(ks[0], (B, S, D), dtype=jnp.float32)
        attention_mask = jnp.zeros((B, 1, 1, S), dtype=jnp.float32)
        wr = jax.random.normal(ks[1], (D, 1), dtype=jnp.float32) * 0.02
        br = jnp.zeros((1,), dtype=jnp.float32)
        w1 = jax.random.normal(ks[2], (D, H), dtype=jnp.float32) * 0.02
        b1 = jnp.zeros((H,), dtype=jnp.float32)
        w2 = jax.random.normal(ks[3], (H, D), dtype=jnp.float32) * 0.02
        b2 = jnp.zeros((D,), dtype=jnp.float32)
        return {'x': x, 'attention_mask': attention_mask, 'wr': wr, 'br': br, 'w1': w1, 'b1': b1, 'w2': w2, 'b2': b2}
    _L1_ffn_all = _L1_ffn_setup()
    _L1_ffn_in = {k: v for k, v in _L1_ffn_all.items() if k in ('attention_mask', 'wr', 'br', 'w1', 'b1', 'w2', 'b2')}
    del _L1_ffn_all
    return {'x': x, 'L0_tok_emb_2': _L0_tok_in['emb_2'], 'L0_tok_emb_3': _L0_tok_in['emb_3'], 'L0_tok_emb_4': _L0_tok_in['emb_4'], 'L0_attn_kw1': _L0_attn_in['kw1'], 'L0_attn_kb1': _L0_attn_in['kb1'], 'L0_attn_kw2': _L0_attn_in['kw2'], 'L0_attn_kb2': _L0_attn_in['kb2'], 'L0_attn_qw1': _L0_attn_in['qw1'], 'L0_attn_qb1': _L0_attn_in['qb1'], 'L0_attn_qw2': _L0_attn_in['qw2'], 'L0_attn_qb2': _L0_attn_in['qb2'], 'L0_attn_vw': _L0_attn_in['vw'], 'L0_attn_vb': _L0_attn_in['vb'], 'L0_ffn_W_gat': _L0_ffn_in['W_gat'], 'L0_ffn_att_src': _L0_ffn_in['att_src'], 'L0_ffn_att_dst': _L0_ffn_in['att_dst'], 'L0_ffn_b_gat': _L0_ffn_in['b_gat'], 'L0_ffn_ln_gamma': _L0_ffn_in['ln_gamma'], 'L0_ffn_ln_beta': _L0_ffn_in['ln_beta'], 'L0_ffn_W1': _L0_ffn_in['W1'], 'L0_ffn_b1': _L0_ffn_in['b1'], 'L0_ffn_W2': _L0_ffn_in['W2'], 'L0_ffn_b2': _L0_ffn_in['b2'], 'L0_ffn_edge_index': _L0_ffn_in['edge_index'], 'L1_attn_W_qkv': _L1_attn_in['W_qkv'], 'L1_attn_b_qkv': _L1_attn_in['b_qkv'], 'L1_attn_kln_w': _L1_attn_in['kln_w'], 'L1_attn_kln_b': _L1_attn_in['kln_b'], 'L1_attn_vln_w': _L1_attn_in['vln_w'], 'L1_attn_vln_b': _L1_attn_in['vln_b'], 'L1_attn_W_proj': _L1_attn_in['W_proj'], 'L1_attn_b_proj': _L1_attn_in['b_proj'], 'L1_ffn_attention_mask': _L1_ffn_in['attention_mask'], 'L1_ffn_wr': _L1_ffn_in['wr'], 'L1_ffn_br': _L1_ffn_in['br'], 'L1_ffn_w1': _L1_ffn_in['w1'], 'L1_ffn_b1': _L1_ffn_in['b1'], 'L1_ffn_w2': _L1_ffn_in['w2'], 'L1_ffn_b2': _L1_ffn_in['b2']}

def reference(x, L0_tok_emb_2, L0_tok_emb_3, L0_tok_emb_4, L0_attn_kw1, L0_attn_kb1, L0_attn_kw2, L0_attn_kb2, L0_attn_qw1, L0_attn_qb1, L0_attn_qw2, L0_attn_qb2, L0_attn_vw, L0_attn_vb, L0_ffn_W_gat, L0_ffn_att_src, L0_ffn_att_dst, L0_ffn_b_gat, L0_ffn_ln_gamma, L0_ffn_ln_beta, L0_ffn_W1, L0_ffn_b1, L0_ffn_W2, L0_ffn_b2, L0_ffn_edge_index, L1_attn_W_qkv, L1_attn_b_qkv, L1_attn_kln_w, L1_attn_kln_b, L1_attn_vln_w, L1_attn_vln_b, L1_attn_W_proj, L1_attn_b_proj, L1_ffn_attention_mask, L1_ffn_wr, L1_ffn_br, L1_ffn_w1, L1_ffn_b1, L1_ffn_w2, L1_ffn_b2):
    import jax
    import jax.numpy as jnp

    def _L0_tok_ref(byte_ids, emb_2, emb_3, emb_4):
        import jax, jax.numpy as jnp
        import numpy as np
        PRIME = 31
        VOCAB = 125000
        NGRAM_SIZES = (2, 3, 4)

        def _ngram_hash(byte_ids, n):
            T = byte_ids.shape[1]
            powers = PRIME ** jnp.arange(n - 1, -1, -1, dtype=jnp.int64) % VOCAB
            windows = jnp.stack([byte_ids[:, i:T - n + 1 + i] for i in range(n)], axis=-1)
            return (windows.astype(jnp.int64) * powers).sum(axis=-1) % VOCAB
        tables = {2: emb_2, 3: emb_3, 4: emb_4}
        B, T = byte_ids.shape
        D = emb_2.shape[1]
        out = jnp.zeros((B, T, D), dtype=emb_2.dtype)
        for n in NGRAM_SIZES:
            idx = _ngram_hash(byte_ids, n)
            gathered = tables[n][idx]
            out = out + jnp.pad(gathered, ((0, 0), (n - 1, 0), (0, 0)))
        return out / (len(NGRAM_SIZES) + 1)

    def _L0_attn_ref(x, kw1, kb1, kw2, kb2, qw1, qb1, qw2, qb2, vw, vb):
        import jax, jax.numpy as jnp
        import numpy as np
        import math
        PI = math.pi

        def _encode_phase(x, w1, b1, w2, b2):
            h = jnp.tanh(jnp.einsum('bld,ed->ble', x, w1) + b1)
            return jnp.tanh(jnp.einsum('bld,kd->blk', h, w2) + b2) * PI
        B, L, D = x.shape
        key_phase = _encode_phase(x, kw1, kb1, kw2, kb2)
        query_phase = _encode_phase(x, qw1, qb1, qw2, qb2)
        K = key_phase.shape[-1]
        value = jnp.einsum('bld,ed->ble', x, vw) + vb
        cos_k = jnp.cos(key_phase)[..., None]
        sin_k = jnp.sin(key_phase)[..., None]
        v_exp = value[:, :, None, :]
        mem_real = jnp.cumsum(cos_k * v_exp, axis=1)
        mem_imag = jnp.cumsum(sin_k * v_exp, axis=1)
        cos_q = jnp.cos(query_phase)[..., None]
        sin_q = jnp.sin(query_phase)[..., None]
        retrieved = jnp.sum(mem_real * cos_q + mem_imag * sin_q, axis=2)
        positions = jnp.arange(1, L + 1, dtype=x.dtype)
        norm = jnp.sqrt(positions * K)[None, :, None]
        return retrieved / norm

    def _L0_ffn_ref(x, W_gat, att_src, att_dst, b_gat, ln_gamma, ln_beta, W1, b1, W2, b2, edge_index):
        import jax, jax.numpy as jnp
        import numpy as np
        B, N, D = (16, 1024, 64)
        NUM_EXPERTS, TOP_K, HEADS = (4, 2, 4)
        N_EDGES = 262144
        LN_EPS = 1e-05

        def _layernorm(x, g, b):
            mu = x.mean(-1, keepdims=True)
            var = ((x - mu) ** 2).mean(-1, keepdims=True)
            return (x - mu) * jax.lax.rsqrt(var + LN_EPS) * g + b

        def _forward(x, edge_index, W_gat, att_src, att_dst, b_gat, ln_gamma, ln_beta, W1, b1, W2, b2):
            Bc, Nc, Dc = x.shape
            M = Bc * Nc
            x_flat = x.reshape(M, Dc)
            h = (x_flat @ W_gat).reshape(M, HEADS, NUM_EXPERTS)
            loops = jnp.arange(M, dtype=edge_index.dtype)
            src = jnp.concatenate([edge_index[0], loops])
            dst = jnp.concatenate([edge_index[1], loops])
            a_src = (h * att_src).sum(-1)
            a_dst = (h * att_dst).sum(-1)
            e = jax.nn.leaky_relu(a_src[src] + a_dst[dst], negative_slope=0.2)
            e_max = jax.ops.segment_max(e, dst, num_segments=M)
            ee = jnp.exp(e - e_max[dst])
            denom = jax.ops.segment_sum(ee, dst, num_segments=M)
            alpha = ee / (denom[dst] + 1e-16)
            msg = h[src] * alpha[:, :, None]
            agg = jax.ops.segment_sum(msg, dst, num_segments=M).reshape(M, HEADS * NUM_EXPERTS) + b_gat
            scores = _layernorm(agg, ln_gamma, ln_beta).reshape(M, HEADS, NUM_EXPERTS).mean(1)
            scores = scores.reshape(Bc, Nc, NUM_EXPERTS)
            topk_s, topk_i = jax.lax.top_k(scores, TOP_K)
            w = jax.nn.softmax(topk_s, axis=-1)
            out = jnp.zeros_like(x)
            for ei in range(NUM_EXPERTS):
                g = jnp.where(topk_i == ei, w, 0.0).sum(-1)
                hh = jax.nn.gelu(x @ W1[ei] + b1[ei], approximate=False)
                out = out + g[..., None] * (hh @ W2[ei] + b2[ei])
            return out
        return _forward(x, edge_index, W_gat, att_src, att_dst, b_gat, ln_gamma, ln_beta, W1, b1, W2, b2)

    def _L1_attn_ref(x, W_qkv, b_qkv, kln_w, kln_b, vln_w, vln_b, W_proj, b_proj):
        import jax, jax.numpy as jnp
        import numpy as np
        MIDC = 64
        HEADS = 16
        HEADC = MIDC // HEADS
        EPS = 1e-05

        def _layernorm(x, w, b):
            mean = jnp.mean(x, axis=-1, keepdims=True)
            std = jnp.std(x, axis=-1, keepdims=True, ddof=1)
            return w * (x - mean) / (std + EPS) + b
        B, HW, C = x.shape
        bias = x
        qkv = jnp.einsum('bnc,oc->bno', x, W_qkv) + b_qkv
        qkv = qkv.reshape(B, HW, HEADS, 3 * HEADC).transpose(0, 2, 1, 3)
        q, k, v = jnp.split(qkv, 3, axis=-1)
        k = _layernorm(k, kln_w, kln_b)
        v = _layernorm(v, vln_w, vln_b)
        kv = jnp.einsum('bhnd,bhne->bhde', k, v) / HW
        out = jnp.einsum('bhnd,bhde->bhne', q, kv)
        out = out.transpose(0, 2, 1, 3).reshape(B, HW, C)
        ret = out + bias
        proj = jnp.einsum('bnc,oc->bno', ret, W_proj) + b_proj
        return jax.nn.gelu(proj, approximate=False) + bias

    def _L1_ffn_ref(x, attention_mask, wr, br, w1, b1, w2, b2):
        import jax, jax.numpy as jnp
        import numpy as np
        B, S, D = (8, 1024, 64)
        H = 4 * D
        CAPACITY = 0.5
        b, s, d = x.shape
        weights = (jnp.einsum('bsd,do->bso', x, wr) + br)[..., 0]
        k = max(1, int(CAPACITY * s))
        kk = k - 1 if k > 1 else 1
        _, idx = jax.lax.top_k(weights, k)
        sel_idx = idx[:, :kk]
        sel = jnp.take_along_axis(x, sel_idx[:, :, None], axis=1)
        h = jax.nn.gelu(jnp.einsum('bkd,dh->bkh', sel, w1) + b1)
        y = jnp.einsum('bkh,hd->bkd', h, w2) + b2
        w_sel = jnp.take_along_axis(weights, sel_idx, axis=1)
        y = y * w_sel[..., None]
        batch_idx = jnp.arange(b)[:, None]
        processed = jnp.zeros_like(x).at[batch_idx, sel_idx].set(y)
        return processed + x
    h = _L0_tok_ref(x, L0_tok_emb_2, L0_tok_emb_3, L0_tok_emb_4)
    h = h + _L0_attn_ref(_layernorm(h, axis=-1), L0_attn_kw1, L0_attn_kb1, L0_attn_kw2, L0_attn_kb2, L0_attn_qw1, L0_attn_qb1, L0_attn_qw2, L0_attn_qb2, L0_attn_vw, L0_attn_vb)
    h = h + _L0_ffn_ref(_layernorm(h, axis=-1), L0_ffn_W_gat, L0_ffn_att_src, L0_ffn_att_dst, L0_ffn_b_gat, L0_ffn_ln_gamma, L0_ffn_ln_beta, L0_ffn_W1, L0_ffn_b1, L0_ffn_W2, L0_ffn_b2, L0_ffn_edge_index)
    h = h + _L1_attn_ref(_layernorm(h, axis=-1), L1_attn_W_qkv, L1_attn_b_qkv, L1_attn_kln_w, L1_attn_kln_b, L1_attn_vln_w, L1_attn_vln_b, L1_attn_W_proj, L1_attn_b_proj)
    h = h + _L1_ffn_ref(_layernorm(h, axis=-1), L1_ffn_attention_mask, L1_ffn_wr, L1_ffn_br, L1_ffn_w1, L1_ffn_b1, L1_ffn_w2, L1_ffn_b2)
    return h

_drawn_inputs = setup_inputs


def setup_inputs(seed=0):
    import zlib

    import numpy as np

    out = dict(_drawn_inputs(seed))
    spreads = {'L0_attn_kb1': (0.0, 0.8),
     'L0_attn_kb2': (0.0, 0.1),
     'L0_attn_qb1': (0.0, 0.8),
     'L0_attn_qb2': (0.0, 0.1),
     'L0_attn_vb': (0.0, 0.1),
     'L0_ffn_b_gat': (0.0, 0.8),
     'L0_ffn_ln_gamma': (1.0, 0.6),
     'L0_ffn_ln_beta': (0.0, 0.8),
     'L0_ffn_b1': (0.0, 0.8),
     'L0_ffn_b2': (0.0, 0.647),
     'L1_attn_b_qkv': (0.0, 0.8),
     'L1_attn_kln_w': (1.0, 0.6),
     'L1_attn_kln_b': (0.0, 0.8),
     'L1_attn_vln_w': (1.0, 0.6),
     'L1_attn_vln_b': (0.0, 0.8),
     'L1_attn_b_proj': (0.0, 0.8),
     'L1_ffn_b1': (0.0, 0.8),
     'L1_ffn_b2': (0.0, 0.8)}
    factors = {'L0_attn_kw1': 8.0,
     'L0_attn_kw2': 8.0,
     'L0_attn_qw1': 8.0,
     'L0_attn_qw2': 8.0,
     'L0_ffn_W_gat': 8.0,
     'L0_ffn_att_src': 8.0,
     'L0_ffn_att_dst': 8.0,
     'L0_ffn_W1': 3.811,
     'L0_ffn_W2': 3.385,
     'L1_attn_W_qkv': 8.0,
     'L1_attn_W_proj': 4.161,
     'L1_ffn_wr': 8.0,
     'L1_ffn_w1': 8.0,
     'L1_ffn_w2': 8.0}
    for name, (base, spread) in spreads.items():
        noise = np.random.default_rng([zlib.crc32(name.encode()), seed]).standard_normal(out[name].shape)
        drawn = base * np.exp(spread * noise) if base else spread * noise
        out[name] = jnp.asarray(drawn.astype(out[name].dtype))
    for name, factor in factors.items():
        out[name] = (out[name] * factor).astype(out[name].dtype)
    return out
```

```python
from contextlib import ExitStack

import concourse.bass as bass
from concourse import mybir

ALU = mybir.AluOpType
ACT = mybir.ActivationFunctionType
AX = mybir.AxisListType
F32 = mybir.dt.float32
BF16 = mybir.dt.bfloat16
I32 = mybir.dt.int32
U32 = mybir.dt.uint32

P = 128
B, T, D = 64, 256, 64
M = B * T
TILES = M // P
GT = 8
GB = GT // 2
GROUPS = TILES // GT
VOCAB, PRIME = 125000, 31
EPS = 1e-5
K = 32
EDGES = 262144
COLS = EDGES // P
NODE_COLS = M // P
ALL_COLS = COLS + NODE_COLS
EXPERTS, HEADS = 4, 4
HID = 2 * D
KEY_BASE = 1 << 29
ROW = 24
BIG = 1e30
H1, C1 = 16, 4
F2 = 4 * D
KEEP = T // 2 - 1


def columns(spec):
    at, n = {}, 0
    for name, width in spec:
        at[name] = (n, width)
        n += width
    return at, n


CONST, CONST_N = columns([
    ("ident", 128), ("causal", 384), ("rnorm", 2), ("emb_scale", 6), ("fold", 1), ("sin_scale", 1),
    ("sin_bias", 1), ("eps", 1), ("iota", 128), ("bit_sign", 7), ("before", 128), ("ties", 512),
    ("own_head", 64), ("zero", 1), ("flip", 7), ("all_but_last", 128), ("slice_end", 1), ("ones", 1),
])
WEIGHT, WEIGHT_N = columns([
    ("kq_w1", 128), ("kq_w2", 64), ("v_w", 64), ("kq_b1", 1), ("k_b2", 1), ("q_b2", 1), ("v_b", 64),
    ("w_gat", 16), ("att_src", 16), ("att_dst", 16), ("b_gat", 16), ("gamma", 16), ("beta", 16),
    ("e_w1", EXPERTS * HID), ("e_b1", EXPERTS), ("e_w2", EXPERTS * D), ("e_b2", EXPERTS * D),
    ("q_w", 64), ("q_b", 1), ("kv_w", 128), ("kv_b", 128), ("kv_ln_w", 128), ("kv_ln_b", 128),
    ("proj_w", 64), ("proj_b", 64), ("route_w", 64), ("route_b", 1),
    ("m_w1", F2), ("m_b1", 2), ("m_w2", 2 * D), ("m_b2", 64),
])


class Chain:

    def __init__(self, eng, sem):
        self.eng, self.sem, self.base, self.n = eng, sem, 0, 0

    def step(self, ins):
        ins.then_inc(self.sem, 1)
        self.n += 1

    def settle(self):
        self.eng.wait_ge(self.sem, self.base + self.n)

    def turn(self, i, per_turn):
        self.start, self.per_turn = self.n if isinstance(self.base, int) else None, per_turn
        self.base, self.n = i * per_turn + self.start, 0

    def end(self, turns):
        assert self.n == self.per_turn, (self.n, self.per_turn)
        self.base, self.n = 0, self.start + turns * self.per_turn


def pause(eng, sem, value, spent):
    eng.wait_ge(sem, value)
    eng.sem_inc(spent, 1)


def spread(ap, n):
    return ap.unsqueeze(len(ap.shape)).broadcast_to(list(ap.shape) + [n])


def repeat(ap, n):
    s = list(ap.shape)
    return ap.unsqueeze(1).broadcast_to([s[0], n] + s[1:])


def clear(nc, sems):
    with nc.Block() as block:
        @block.gpsimd
        def _(pool):
            for s in sems:
                pool.sem_clear(s)


def embed_and_sort(nc, mem, ids, tables, edges, consts, weights, sorted_keys):
    c, w, h, e34 = mem["c"], mem["w"], mem["h"], mem["e34"]
    with ExitStack() as ctx:
        sb = lambda name, shape, dt: ctx.enter_context(nc.sbuf_tensor(name, shape, dt))
        sems = []

        def sem(name):
            sems.append(ctx.enter_context(nc.semaphore(name)))
            return sems[-1]

        idf = sb("idf", [B, T + 3], F32)
        idi = sb("idi", [B, T], I32)
        hashes = sb("hashes", [B, 3, T], F32)
        quot = sb("quot", [B, 3, T], I32)
        quotf = sb("quotf", [B, 3, T], F32)
        rows = sb("rows", [P, TILES, 3], I32)
        rows_now = sb("rows_now", [P, 2, GT * 3], I32)
        ring = sb("ring", [P, 2, 3, GT, D], F32)
        ends = sb("ends", [P, 2, COLS], I32)
        keys = [sb("keys0", [P, COLS], F32), sb("keys1", [P, COLS], F32)]
        nodes = sb("nodes", [P, COLS], I32)
        nodes2 = sb("nodes2", [P, COLS], I32)
        tops = [sb("tops0", [P, P], F32), sb("tops1", [P, P], F32)]
        turned = ctx.enter_context(nc.psum_tensor("turned", [P, COLS], F32))
        idx_t = ctx.enter_context(nc.psum_tensor("idx_t", [P, 6, B], F32))

        s_const, s_ids, s_edges = sem("s_const"), sem("s_ids"), sem("s_edges")
        s_dve = sem("s_dve1")
        s_pool = sem("s_pool1")
        s_hash = sem("s_hash")
        s_idx_t = sem("s_idx_t")
        s_rows = sem("s_rows")
        s_landed = [sem("s_landed0"), sem("s_landed1")]
        s_drained = [sem("s_drained0"), sem("s_drained1")]
        s_spent = sem("s_spent1")
        s_turn_go, s_turned = sem("s_turn_go"), sem("s_turned")
        s_iota = sem("s_iota")
        s_tops, s_tops_back, s_sorted = sem("s_tops"), sem("s_tops_back"), sem("s_sorted")
        s_tops_w, s_low_w = sem("s_tops_w"), sem("s_low_w")

        ident = mem["C"]("ident")
        kept = {"k": keys, "t": tops}
        PHASES = [("k", top) for top in range(1, 19)] + [("k", 18), ("t", 14)]
        top_dram = mem["top_dram"]

        final, final_top = (sum(range(1, 19)) + 1 + 18) % 2, 14 % 2

        stage = ExitStack()
        block = stage.enter_context(nc.Block())

        @block.sync
        def _(sp):
            sp.dma_start(idi[:], ids).then_inc(s_ids, 16)
            sp.dma_start(c[:], consts).then_inc(s_const, 16)
            sp.dma_start(ends[:], edges.rearrange("two (p c) -> p two c", p=P)).then_inc(s_edges, 16)
            sp.dma_start(w[:], weights).then_inc(mem["s_weights"], 16)
            sp.wait_ge(s_tops, 1)
            sp.dma_start(top_dram.rearrange("(p c) -> p c", p=8), nodes2[120:128, :].bitcast(F32)).then_inc(s_tops_w, 16)
            sp.wait_ge(s_tops_w, 16)
            sp.dma_start(tops[0][:], top_dram.rearrange("(p c) -> p c", p=P)).then_inc(s_tops_back, 16)
            sp.wait_ge(s_sorted, 2)
            sp.dma_start(sorted_keys[0:EDGES].rearrange("(p c) -> p c", p=P), keys[final][:]).then_inc(s_low_w, 16)
            sp.dma_start(sorted_keys[EDGES:].rearrange("(p c) -> p c", p=P), tops[final_top][:]).then_inc(s_low_w, 16)
            sp.wait_ge(s_low_w, 32)
            sp.wait_ge(mem["s_weights"], 16)

        @block.gpsimd
        def _(pool):
            nc.gpsimd.iota(nodes[:], pattern=[[-1, COLS]], base=EDGES - 1, channel_multiplier=-COLS).then_inc(s_iota, 1)
            pool.wait_ge(s_rows, 1)
            with pool.Fori(0, GROUPS // 2) as i:
                for r in range(2):
                    pause(pool, s_drained[r], i * 6 + 6, s_spent)
                    nc.gpsimd.tensor_copy(rows_now[:, r, :], rows[:].rearrange("p t n -> p (t n)")[:, bass.ds((i * 2 + r) * (GT * 3), GT * 3)]).then_inc(s_pool, 1)
                    pause(pool, s_pool, i * 2 + r + 1, s_spent)
                    for t in range(GT):
                        for n in range(3):
                            pool.indirect_dma_start(
                                out=ring[:, r, n, t, :], out_offset=None, in_=tables[n],
                                in_offset=bass.IndirectOffsetOnAxis(ap=rows_now[:, r, t * 3 + n:t * 3 + n + 1].bitcast(U32), axis=0),
                            ).then_inc(s_landed[r], 16)

        @block.scalar
        def _(act):
            act.wait_ge(s_const, 16)
            for r in range(2):
                act.sem_inc(s_drained[r], 6)
            with act.Fori(0, GROUPS // 2) as i:
                for r in range(2):
                    pause(act, s_landed[r], (i + 1) * (GT * 3 * 16), s_spent)
                    for n in range(3):
                        for half in range(2):
                            to = h[:] if n == 0 else e34[:, n - 1]
                            to = to.rearrange("p (g b two) d -> p g b two d", b=GB, two=2)[:, bass.ds(i * 2 + r, 1), :, half, :]
                            nc.scalar.activation(
                                to.rearrange("p g b d -> p (g b) d"),
                                ring[:, r, n].rearrange("p (b two) d -> p b two d", two=2)[:, :, half, :],
                                ACT.Copy, scale=mem["C"]("emb_scale")[:, n * 2 + half:n * 2 + half + 1],
                            ).then_inc(s_drained[r], 1)

        @block.vector
        def _(dve):
            ch = Chain(dve, s_dve)
            v = nc.vector
            ch.step(v.memset(idf[:, 0:3], 0.0))
            dve.wait_ge(s_ids, 16)
            ch.step(v.tensor_copy(idf[:, 3:], idi[:]))
            ch.settle()
            for n in range(3):
                power = float(PRIME ** (n + 1) % VOCAB)
                before = idf[:, 3:] if n == 0 else hashes[:, n - 1, :]
                ch.step(v.scalar_tensor_tensor(out=hashes[:, n, :], in0=idf[:, 2 - n:2 - n + T], scalar=power, in1=before, op0=ALU.mult, op1=ALU.add))
                ch.settle()
            ch.step(v.tensor_scalar(quot[:], hashes[:], 1.0 / VOCAB, None, ALU.mult)); ch.settle()
            ch.step(v.tensor_copy(quotf[:], quot[:])); ch.settle()
            ch.step(v.scalar_tensor_tensor(out=hashes[:], in0=quotf[:], scalar=-float(VOCAB), in1=hashes[:], op0=ALU.mult, op1=ALU.add)); ch.settle()
            ch.step(v.tensor_scalar(quotf[:], hashes[:], 0.0, float(VOCAB), ALU.is_lt, ALU.mult)); ch.settle()
            ch.step(v.tensor_tensor(hashes[:], hashes[:], quotf[:], ALU.add)); ch.settle()
            ch.step(v.tensor_scalar(quotf[:], hashes[:], float(VOCAB), -float(VOCAB), ALU.is_ge, ALU.mult)); ch.settle()
            v.tensor_tensor(hashes[:], hashes[:], quotf[:], ALU.add).then_inc(s_hash, 1)
            dve.wait_ge(s_idx_t, 1)
            v.tensor_copy(rows[:].rearrange("p (b two) n -> p n two b", two=2),
                          idx_t[:].rearrange("p (n two) b -> p n two b", two=2)).then_inc(s_rows, 1)

            dve.wait_ge(s_edges, 16)
            ki = keys[0][:].bitcast(I32)
            ch.step(v.tensor_scalar(ends[:, 1], ends[:, 1], 15, KEY_BASE | (1 << 14), ALU.logical_shift_left, ALU.bitwise_or)); ch.settle()
            ch.step(v.tensor_tensor(ki, ends[:, 1], ends[:, 0], ALU.bitwise_or))
            dve.wait_ge(s_iota, 1)
            ch.step(v.tensor_scalar(nodes[:], nodes[:], float(M), None, ALU.min)); ch.settle()
            ch.step(v.tensor_scalar(nodes2[:], nodes[:], float(M), None, ALU.add)); ch.settle()
            ch.step(v.tensor_scalar(nodes2[:], nodes2[:], 15, None, ALU.logical_shift_left)); ch.settle()
            ch.step(v.tensor_tensor(nodes2[:], nodes2[:], nodes[:], ALU.bitwise_or)); ch.settle()
            dve.wait_ge(s_const, 16)

            now = [0]
            turns = [0]

            def exchange(arr, step, lo_from=None):
                pairs = lambda t: t.rearrange("p (n two d) -> p n two d", two=2, d=step)
                a = pairs(kept[arr][now[0]][:])
                left, right = a[:, :, 0, :], a[:, :, 1, :]
                o = pairs(kept[arr][1 - now[0]][:])
                if lo_from is not None:
                    left = pairs(lo_from)[:, :, 0, :]
                    ch.step(v.tensor_copy(right, pairs(lo_from)[:, :, 1, :]))
                    ch.settle()
                ch.step(v.tensor_tensor(o[:, :, 0, :], left, right, ALU.min))
                ch.step(v.tensor_tensor(o[:, :, 1, :], left, right, ALU.max))
                ch.settle()
                now[0] = 1 - now[0]

            def turn(arr):
                turns[0] += 1
                dve.sem_inc(s_turn_go, 1)
                dve.wait_ge(s_turned, turns[0])
                return turned[:, 0:COLS if arr == "k" else P]

            def merge(top, arr="k"):
                low = 11 if arr == "k" else 7
                j = top - 1
                if top > low:
                    src = turn(arr)
                    while j >= low:
                        exchange(arr, 1 << (j - low), src)
                        src = None
                        j -= 1
                    while j >= 7:
                        exchange(arr, 1 << j)
                        j -= 1
                    src = turn(arr)
                    while j >= 0:
                        exchange(arr, 1 << j, src)
                        src = None
                        j -= 1
                else:
                    while j >= 0:
                        exchange(arr, 1 << j)
                        j -= 1

            def negate(ap, by):
                ch.step(v.tensor_scalar(ap, ap, by, None, ALU.mult))

            for k in range(1, 19):
                cur = kept["k"][now[0]]
                if k == 1:
                    negate(cur[:].rearrange("p (n a d) -> p n a d", a=2, d=2)[:, :, 1, :], -1.0)
                elif k <= 10:
                    q = cur[:].rearrange("p (n a b d) -> p n a b d", a=2, b=2, d=1 << (k - 1))
                    negate(q[:, :, 0, 1, :], -1.0)
                    negate(q[:, :, 1, 0, :], -1.0)
                elif k == 11:
                    negate(cur[:, 0:COLS // 2], mem["C"]("bit_sign")[:, 0:1])
                    negate(cur[:, COLS // 2:], mem["C"]("flip")[:, 0:1])
                elif k < 18:
                    negate(cur[:], mem["C"]("flip")[:, k - 11:k - 10])
                else:
                    negate(cur[:], mem["C"]("bit_sign")[:, 6:7])
                ch.settle()
                merge(k)
            cur, oth = kept["k"][now[0]], kept["k"][1 - now[0]]
            n2 = nodes2[:].bitcast(F32)
            ch.step(v.tensor_copy(oth[0:96, :], cur[0:96, :]))
            ch.step(v.tensor_tensor(oth[96:P, :], cur[96:P, :], n2[96:P, :], ALU.min))
            ch.settle()
            v.tensor_tensor(n2[96:P, :], cur[96:P, :], n2[96:P, :], ALU.max).then_inc(s_tops, 1)
            now[0] = 1 - now[0]
            merge(18)
            assert now[0] == final
            dve.sem_inc(s_sorted, 1)
            now[0] = 0
            dve.wait_ge(s_tops_back, 16)
            merge(14, "t")
            assert now[0] == final_top
            dve.sem_inc(s_sorted, 1)

        @block.tensor
        def _(pe):
            pe.wait_ge(s_const, 16)
            pe.wait_ge(s_hash, 1)
            for n in range(3):
                for half in range(2):
                    mm = pe.transpose(idx_t[:, n * 2 + half, :], hashes[:, n, half * P:half * P + P], ident[0:B, 0:B])
            mm.then_inc(s_idx_t, 1)
            turns, done = 0, 0
            for n, (arr, top) in enumerate(PHASES):
                if n == 18:
                    done += 1
                if arr == "t":
                    done = 0
                if arr == "k" and top <= 11:
                    done += top
                    continue
                for exchanges in (top - 7, 7):
                    turns += 1
                    pe.wait_ge(s_turn_go, turns)
                    for b in range((COLS if arr == "k" else P) // P):
                        mm = pe.transpose(turned[:, b * P:b * P + P], kept[arr][done % 2][:, b * P:b * P + P], ident)
                    mm.then_inc(s_turned, 1)
                    done += exchanges
        stage.close()
        clear(nc, sems)


def layernorm_stats(nc, mem, ctx, name, first=None):
    h, xc, rstd = mem["h"], mem["xc"], mem["rstd"]
    with ExitStack() as ctx:
        sem = lambda n: ctx.enter_context(nc.semaphore(n + name))
        sq = ctx.enter_context(nc.sbuf_tensor("sq" + name, [P, 2, TILES // 4, D], F32))
        s_dve, s_xc, s_sq, s_var, s_std = sem("ln_dve"), sem("ln_xc"), sem("ln_sq"), sem("ln_var"), sem("ln_std")
        s_read = sem("ln_read")
        block = ctx.enter_context(nc.Block())
        Q = TILES // 4

        @block.vector
        def _(dve):
            ch = Chain(dve, s_dve)
            v = nc.vector
            if first is not None:
                first(v, ch)
            mean = mem["mean"]
            for q in range(4):
                t = slice(q * Q, q * Q + Q)
                ch.step(v.tensor_reduce(mean[:, t], h[:, t], AX.X, ALU.add)); ch.settle()
                ch.step(v.tensor_scalar(mean[:, t], mean[:, t], 1.0 / D, None, ALU.mult)); ch.settle()
                v.tensor_tensor(xc[:, t], h[:, t], spread(mean[:, t], D), ALU.subtract).then_inc(s_xc, 1)
                if q:
                    dve.wait_ge(s_sq, q)
                    v.tensor_reduce(rstd[:, (q - 1) * Q:q * Q], sq[:, (q - 1) % 2], AX.X, ALU.add).then_inc(s_read, 1)
            dve.wait_ge(s_sq, 4)
            v.tensor_reduce(rstd[:, 3 * Q:], sq[:, 1], AX.X, ALU.add).then_inc(s_read, 1)
            dve.wait_ge(s_std, 1)
            v.reciprocal(rstd[:], rstd[:])

        @block.scalar
        def _(act):
            for q in range(4):
                act.wait_ge(s_xc, q + 1)
                if q >= 2:
                    act.wait_ge(s_read, q - 1)
                nc.scalar.activation(sq[:, q % 2], xc[:, q * Q:q * Q + Q], ACT.Square).then_inc(s_sq, 1)
            act.wait_ge(s_read, 4)
            nc.scalar.activation(rstd[:], rstd[:], ACT.Sqrt, scale=1.0 / D, bias=mem["C"]("eps")).then_inc(s_std, 1)


def phase_attention(nc, mem):
    h, xc, rstd, C, W = mem["h"], mem["xc"], mem["rstd"], mem["C"], mem["W"]
    N = GT * P
    with ExitStack() as ctx:
        sb = lambda name, shape, dt: ctx.enter_context(nc.sbuf_tensor(name, shape, dt))
        ps = lambda name, shape: ctx.enter_context(nc.psum_tensor(name, shape, F32))
        sem = lambda name: ctx.enter_context(nc.semaphore(name))
        x = sb("a0_x", [P, GT, D], F32)
        xt = sb("a0_xt", [D, N], F32)
        hid = sb("a0_hid", [P, N], F32)
        val = sb("a0_val", [P, GT, D], F32)
        u = sb("a0_u", [D, 2, N], F32)
        fold = sb("a0_fold", [D, 2, N], F32)
        phi = sb("a0_phi", [D, 2, N], F32)
        sm = sb("a0_sm", [P, GB, 384], F32)
        ret = sb("a0_ret", [P, GT, D], F32)
        wide = ps("a0_wide", [P, 4, 512])
        p_v, p_o = ps("a0_pv", [P, GT, D]), ps("a0_po", [P, GT, D])
        s_dve, s_x, s_xt_p, s_xt, s_hid_p, s_hid, s_v, s_ph, s_u, s_fold, s_phi, s_sc, s_sm, s_out, s_done, s_spent = (
            sem("a0_" + n) for n in ("dve", "x", "xtp", "xt", "hidp", "hid", "v", "ph", "u", "fold", "phi", "sc", "sm", "out", "done", "spent"))
        block = ctx.enter_context(nc.Block())
        wf = wide[:].rearrange("p a n -> p (a n)")

        @block.vector
        def _(dve):
            ch = Chain(dve, s_dve)
            v = nc.vector
            with dve.Fori(0, GROUPS) as i:
                g = bass.ds(i * GT, GT)
                if_first = i + 1
                v.tensor_tensor(x[:], xc[:, g], spread(rstd[:, g], D), ALU.mult).then_inc(s_x, 1)
                pause(dve, s_v, i + 1, s_spent)
                v.tensor_tensor(val[:], p_v[:], repeat(W("v_b"), GT), ALU.add).then_inc(s_dve, 1)
                pause(dve, s_u, i * 2 + 2, s_spent)
                v.scalar_tensor_tensor(out=fold[:], in0=u[:], scalar=C("fold")[0:D], in1=u[:], op0=ALU.mult, op1=ALU.max).then_inc(s_fold, 1)
                pause(dve, s_sc, i + 1, s_spent)
                v.tensor_tensor(sm[:], wide[:, :, 0:384], repeat(C("causal"), GB), ALU.mult).then_inc(s_sm, 1)
                pause(dve, s_out, i + 1, s_spent)
                v.tensor_tensor(ret[:].rearrange("p (b two) d -> p b two d", two=2), p_o[:].rearrange("p (b two) d -> p b two d", two=2),
                                repeat(spread(C("rnorm"), D), GB), ALU.mult).then_inc(s_done, 1)
                pause(dve, s_done, i * 2 + 1, s_spent)
                v.tensor_tensor(h[:, g], h[:, g], ret[:], ALU.add).then_inc(s_done, 1)
            dve.wait_ge(s_done, 2 * GROUPS)

        @block.tensor
        def _(pe):
            with pe.Fori(0, GROUPS) as i:
                pause(pe, s_x, i + 1, s_spent)
                for t in range(GT):
                    mm = pe.transpose(wf[0:D, t * P:t * P + P], x[:, t, :], C("ident"))
                mm.then_inc(s_xt_p, 1)
                pause(pe, s_xt, i + 1, s_spent)
                for n in range(2):
                    mm = pe.matmul(wide[:, 2 + n, :], W("kq_w1")[0:D], xt[:, n * 512:n * 512 + 512], start=True, stop=True)
                mm.then_inc(s_hid_p, 1)
                for t in range(GT):
                    mm = pe.matmul(p_v[:, t, :], xt[:, t * P:t * P + P], W("v_w")[0:D], start=True, stop=True)
                mm.then_inc(s_v, 1)
                pause(pe, s_hid, i + 1, s_spent)
                for kq in range(2):
                    for n in range(2):
                        mm = pe.matmul(wide[0:D, kq * 2 + n, :], W("kq_w2")[kq * D:kq * D + D], hid[kq * D:kq * D + D, n * 512:n * 512 + 512], start=True, stop=True)
                    mm.then_inc(s_ph, 1)
                pause(pe, s_phi, i + 1, s_spent)
                for b in range(GB):
                    pe.matmul(wide[:, b, 0:256], phi[:, 0, b * T:b * T + P], phi[:, 1, b * T:b * T + T], start=True, stop=True)
                    mm = pe.matmul(wide[:, b, 256:384], phi[:, 0, b * T + P:b * T + T], phi[:, 1, b * T + P:b * T + T], start=True, stop=True)
                mm.then_inc(s_sc, 1)
                pause(pe, s_sm, i + 1, s_spent)
                for b in range(GB):
                    pe.matmul(p_o[:, 2 * b, :], sm[:, b, 0:P], val[:, 2 * b, :], start=True, stop=True)
                    pe.matmul(p_o[:, 2 * b + 1, :], sm[:, b, P:2 * P], val[:, 2 * b, :], start=True, stop=False)
                    mm = pe.matmul(p_o[:, 2 * b + 1, :], sm[:, b, 2 * P:3 * P], val[:, 2 * b + 1, :], start=False, stop=True)
                mm.then_inc(s_out, 1)

        @block.scalar
        def _(act):
            a = nc.scalar
            with act.Fori(0, GROUPS) as i:
                pause(act, s_xt_p, i + 1, s_spent)
                a.activation(xt[:], wf[0:D, 0:N], ACT.Copy).then_inc(s_xt, 1)
                pause(act, s_hid_p, i + 1, s_spent)
                a.activation(hid[:], wf[:, N:2 * N], ACT.Tanh, bias=W("kq_b1")).then_inc(s_hid, 1)
                for kq in range(2):
                    pause(act, s_ph, i * 2 + kq + 1, s_spent)
                    a.activation(u[:, kq], wf[0:D, kq * N:kq * N + N], ACT.Tanh, bias=W("q_b2" if kq else "k_b2")[0:D]).then_inc(s_u, 1)
                pause(act, s_fold, i + 1, s_spent)
                a.activation(phi[:], fold[:], ACT.Sin, scale=C("sin_scale")[0:D], bias=C("sin_bias")[0:D]).then_inc(s_phi, 1)


CH = 32
CHUNKS = ALL_COLS // CH
OH = 16


def node_table(nc, mem, table_dram):
    xc, rstd, C, W = mem["xc"], mem["rstd"], mem["C"], mem["W"]
    with ExitStack() as ctx:
        sb = lambda name, shape, dt: ctx.enter_context(nc.sbuf_tensor(name, shape, dt))
        sem = lambda name: ctx.enter_context(nc.semaphore("nt_" + name))
        x = sb("nt_x", [P, 2, GT, D], F32)
        xt = sb("nt_xt", [D, 2, GT * P], F32)
        tab = sb("nt_tab", [P, TILES, ROW], F32)
        att = sb("nt_att", [P, 2, TILES, 16], F32)
        p_xt = ctx.enter_context(nc.psum_tensor("nt_pxt", [D, 2, GT * P], F32))
        p_h = ctx.enter_context(nc.psum_tensor("nt_ph", [P, 2, 512], F32))
        s_x, s_xt_p, s_xt, s_h_p, s_h, s_dve, s_tab, s_out, s_spent = (sem(n) for n in ("x", "xtp", "xt", "hp", "h", "dve", "tab", "out", "spent"))
        block = ctx.enter_context(nc.Block())

        @block.vector
        def _(dve):
            v = nc.vector
            with dve.Fori(0, GROUPS // 2) as i:
                for r in range(2):
                    pause(dve, s_xt_p, i * 2 + r + 1, s_spent)
                    v.tensor_tensor(x[:, r], xc[:, bass.ds((i * 2 + r) * GT, GT)], spread(rstd[:, bass.ds((i * 2 + r) * GT, GT)], D), ALU.mult).then_inc(s_x, 1)
            ch = Chain(dve, s_dve)
            dve.wait_ge(s_h, GROUPS + 2)
            for n, name in enumerate(("att_src", "att_dst")):
                ch.step(v.tensor_tensor(att[:, n], tab[:, :, 0:16], repeat(W(name), TILES), ALU.mult))
            ch.settle()
            for n in range(2):
                v.tensor_reduce(tab[:, :, 16 + 4 * n:20 + 4 * n], att[:, n].rearrange("p t (h e) -> p t h e", e=EXPERTS), AX.X, ALU.add).then_inc(s_tab, 1)

        @block.tensor
        def _(pe):
            pe.sem_inc(s_xt_p, 2)
            pe.sem_inc(s_h, 2)
            with pe.Fori(0, GROUPS // 2) as i:
                for r in range(2):
                    pause(pe, s_x, i * 2 + r + 1, s_spent)
                    pause(pe, s_h, i * 2 + r + 1, s_spent)
                    for t in range(GT):
                        mm = pe.transpose(p_xt[:, r, t * P:t * P + P], x[:, r, t, :], C("ident"))
                    mm.then_inc(s_xt_p, 1)
                    pause(pe, s_xt, i * 2 + r + 1, s_spent)
                    for t in range(GT):
                        mm = pe.matmul(p_h[:, r, t * 16:t * 16 + 16], xt[:, r, t * P:t * P + P], W("w_gat")[0:D], start=True, stop=True)
                    mm.then_inc(s_h_p, 1)

        @block.scalar
        def _(act):
            with act.Fori(0, GROUPS // 2) as i:
                for r in range(2):
                    pause(act, s_xt_p, i * 2 + r + 3, s_spent)
                    nc.scalar.activation(xt[:, r], p_xt[:, r], ACT.Copy).then_inc(s_xt, 1)
                    pause(act, s_h_p, i * 2 + r + 1, s_spent)
                    nc.scalar.activation(tab[:, bass.ds((i * 2 + r) * GT, GT), 0:16], p_h[:, r, 0:GT * 16].rearrange("p (t f) -> p t f", f=16), ACT.Copy).then_inc(s_h, 1)

        @block.sync
        def _(sp):
            sp.wait_ge(s_tab, 2)
            sp.dma_start(table_dram.rearrange("(t p) r -> p t r", p=P), tab[:]).then_inc(s_out, 16)
            sp.wait_ge(s_out, 16)


def edge_stream(nc, mem, sorted_keys, table_dram, state_dram):
    C = mem["C"]
    with ExitStack() as ctx:
        sb = lambda name, shape, dt: ctx.enter_context(nc.sbuf_tensor(name, shape, dt))
        sem = lambda name: ctx.enter_context(nc.semaphore("es_" + name))
        key = sb("es_key", [P, ALL_COLS], I32)
        src = sb("es_src", [P, ALL_COLS], I32)
        tmp = sb("es_tmp", [P, ALL_COLS], I32)
        keep = sb("es_keep", [P, ALL_COLS], F32)
        starts = sb("es_starts", [P, ALL_COLS], F32)
        drop = sb("es_drop", [P, ALL_COLS], F32)
        hi = sb("es_hi", [P, ALL_COLS], BF16)
        lo = sb("es_lo", [P, ALL_COLS], BF16)
        iota = sb("es_iota", [P, P], BF16)
        hot = sb("es_hot", [P, 2, 2, OH, P], BF16)
        now = sb("es_now", [P, 2, CH], I32)
        row0 = sb("es_row0", [P, ROW], F32)
        got = sb("es_got", [P, 2, CH, ROW], F32)
        a_self = sb("es_aself", [P, 4, CH], F32)
        a_dst = sb("es_adst", [P, 2, 4, CH], F32)
        e = sb("es_e", [P, 4, CH], F32)
        diff = sb("es_diff", [P, 2, CH, 4], F32)
        ex = sb("es_ex", [P, 2, CH, 4], F32)
        msg = sb("es_msg", [P, CH, 16], F32)
        st = sb("es_st", [P, 2, CH + 1, ROW], F32)
        counts = ctx.enter_context(nc.psum_tensor("es_counts", [P, P], F32))
        s_keys, s_dve, s_pool, s_src, s_row0, s_diff, s_ex, s_state, s_stored0, s_stored1, s_spent, s_hot, s_used = (
            sem(n) for n in ("keys", "dve", "pool", "src", "row0", "diff", "ex", "state", "stored0", "stored1", "spent", "hot", "used"))
        s_landed, s_free, s_stored = [sem("landed0"), sem("landed1")], [sem("free0"), sem("free1")], [s_stored0, s_stored1]
        block = ctx.enter_context(nc.Block())
        HOTS = CH // OH

        @block.sync
        def _(sp):
            sp.dma_start(key[:], sorted_keys.rearrange("(p c) -> p c", p=P).bitcast(I32)).then_inc(s_keys, 16)
            states = state_dram.rearrange("(p c) r -> p c r", p=P)
            for r in range(2):
                sp.sem_inc(s_stored[r], 16)
            with sp.Fori(0, CHUNKS // 2) as i:
                for r in range(2):
                    pause(sp, s_state, i * 2 + r + 1, s_spent)
                    sp.dma_start(states[:, bass.ds((i * 2 + r) * CH, CH), :], st[:, r, 1:, :]).then_inc(s_stored[r], 16)
            for r in range(2):
                sp.wait_ge(s_stored[r], 16 * (CHUNKS // 2 + 1))

        @block.gpsimd
        def _(pool):
            pool.wait_ge(s_src, 1)
            pool.indirect_dma_start(out=row0[:], out_offset=None, in_=table_dram,
                                    in_offset=bass.IndirectOffsetOnAxis(ap=mem["first"][:, 0:1].bitcast(U32), axis=0)).then_inc(s_row0, 16)
            for r in range(2):
                pool.sem_inc(s_free[r], 1)
            with pool.Fori(0, CHUNKS // 2) as i:
                for r in range(2):
                    pause(pool, s_free[r], i + 1, s_spent)
                    nc.gpsimd.tensor_copy(now[:, r, :], src[:, bass.ds((i * 2 + r) * CH, CH)]).then_inc(s_pool, 1)
                    pause(pool, s_pool, i * 2 + r + 1, s_spent)
                    for k in range(CH):
                        pool.indirect_dma_start(out=got[:, r, k, :], out_offset=None, in_=table_dram,
                                                in_offset=bass.IndirectOffsetOnAxis(ap=now[:, r, k:k + 1].bitcast(U32), axis=0)).then_inc(s_landed[r], 16)

        @block.scalar
        def _(act):
            with act.Fori(0, CHUNKS) as i:
                pause(act, s_diff, i + 1, s_spent)
                nc.scalar.activation(ex[:], diff[:], ACT.Exp).then_inc(s_ex, 1)

        @block.tensor
        def _(pe):
            pe.wait_ge(s_src, 1)
            pe.matmul(counts[:], hot[:, 0, 0, 0, :], hot[:, 0, 1, 0, :], start=True, stop=False, skip_group_check=True).then_inc(s_used, 2)
            with pe.Fori(0, CHUNKS // 2) as i:
                for n in range(2 * HOTS):
                    pause(pe, s_hot, i * (2 * HOTS) + n + 1, s_spent)
                    for k in range(OH):
                        mm = pe.matmul(counts[:], hot[:, n % 2, 0, k, :], hot[:, n % 2, 1, k, :], start=False, stop=False, skip_group_check=True)
                    mm.then_inc(s_used, 1)
            pe.matmul(counts[:], hot[:, 0, 0, 0, :], mem["zeros"][:], start=False, stop=True, skip_group_check=True).then_inc(s_used, 1)

        @block.vector
        def _(dve):
            ch = Chain(dve, s_dve)
            v = nc.vector
            dve.wait_ge(s_keys, 16)
            ch.step(v.tensor_scalar(src[:], key[:], M - 1, None, ALU.bitwise_and))
            ch.step(v.tensor_scalar(mem["first"][:], key[:, 0:1], 15, M - 1, ALU.logical_shift_right, ALU.bitwise_and))
            ch.step(v.tensor_copy(iota[:], C("iota")))
            ch.step(v.memset(mem["zeros"][:], 0.0))
            ch.step(v.memset(hot[:, 0, :, 0, :], 0.0))
            ch.settle()
            dve.sem_inc(s_src, 1)
            for to, shift in ((hi, 22), (lo, 15)):
                ch.step(v.tensor_scalar(tmp[:], key[:], shift, P - 1, ALU.logical_shift_right, ALU.bitwise_and)); ch.settle()
                ch.step(v.tensor_copy(to[:], tmp[:])); ch.settle()
            ch.step(v.tensor_scalar(tmp[:], key[:], 14, 1, ALU.logical_shift_right, ALU.bitwise_and)); ch.settle()
            ch.step(v.tensor_copy(keep[:], tmp[:])); ch.settle()
            ch.step(v.tensor_scalar(starts[:], keep[:], -1.0, 1.0, ALU.mult, ALU.add)); ch.settle()
            ch.step(v.tensor_scalar(drop[:], starts[:], -BIG, None, ALU.mult))
            ch.step(v.tensor_reduce(mem["has_start"][:], starts[:], AX.X, ALU.max))
            ch.step(v.tensor_copy(mem["first_keep"][:], keep[:, 0:1]))
            ch.step(v.memset(st[:, 1, CH, 0:4], -BIG))
            ch.step(v.memset(st[:, 1, CH, 4:ROW], 0.0))
            dve.wait_ge(s_row0, 16)
            ch.step(v.tensor_copy(a_dst[:, 1, :, CH - 1], row0[:, 20:24]))
            ch.settle()
            PER = 2 * 38
            with dve.Fori(0, CHUNKS // 2) as i:
                ch.turn(i, PER)
                for r in range(2):
                    cols = bass.ds((i * 2 + r) * CH, CH)
                    for n in range(HOTS):
                        at = bass.ds((i * 2 + r) * CH + n * OH, OH)
                        pause(dve, s_used, (i * 2 + r) * HOTS + n + 1, s_spent)
                        v.tensor_tensor(hot[:, n % 2, 0], repeat(iota[:], OH), spread(hi[:, at], P), ALU.is_equal)
                        v.tensor_tensor(hot[:, n % 2, 1], repeat(iota[:], OH), spread(lo[:, at], P), ALU.is_equal).then_inc(s_hot, 1)
                    pause(dve, s_landed[r], (i + 1) * (16 * CH), s_spent)
                    g = got[:, r]
                    ch.step(v.tensor_tensor(a_self[:], g[:, :, 20:24].rearrange("p c k -> p k c"), repeat(starts[:, cols], 4), ALU.mult)); ch.settle()
                    for k in range(4):
                        ch.step(v.tensor_tensor_scan(a_dst[:, r, k], keep[:, cols], a_self[:, k], a_dst[:, 1 - r, k, CH - 1:CH], ALU.mult, ALU.add))
                    ch.settle()
                    ch.step(v.tensor_tensor(e[:], g[:, :, 16:20].rearrange("p c k -> p k c"), a_dst[:, r], ALU.add)); ch.settle()
                    ch.step(v.scalar_tensor_tensor(out=e[:], in0=e[:], scalar=0.2, in1=e[:], op0=ALU.mult, op1=ALU.max)); ch.settle()
                    pause(dve, s_stored[r], (i + 1) * 16, s_spent)
                    ch.step(v.tensor_copy(st[:, r, 0, :], st[:, 1 - r, CH, :]))
                    ch.settle()
                    for k in range(4):
                        ch.step(v.tensor_tensor_scan(st[:, r, 1:, k], drop[:, cols], e[:, k], st[:, r, 0, k:k + 1], ALU.add, ALU.max))
                    ch.settle()
                    ch.step(v.tensor_tensor(diff[:, 0], st[:, r, 0:CH, 0:4], st[:, r, 1:, 0:4], ALU.subtract))
                    ch.step(v.tensor_tensor(diff[:, 1], e[:].rearrange("p k c -> p c k"), st[:, r, 1:, 0:4], ALU.subtract))
                    ch.settle()
                    v.tensor_tensor(diff[:, 0], diff[:, 0], spread(drop[:, cols], 4), ALU.add).then_inc(s_diff, 1)
                    pause(dve, s_ex, i * 2 + r + 1, s_spent)
                    for k in range(4):
                        ch.step(v.tensor_tensor_scan(st[:, r, 1:, 4 + k], ex[:, 0, :, k], ex[:, 1, :, k], st[:, r, 0, 4 + k:5 + k], ALU.mult, ALU.add))
                    for k in range(4):
                        ch.step(v.tensor_tensor(msg[:, :, 4 * k:4 * k + 4], g[:, :, 4 * k:4 * k + 4], spread(ex[:, 1, :, k], 4), ALU.mult))
                    ch.settle()
                    dve.sem_inc(s_free[r], 1)
                    for j in range(16):
                        ch.step(v.tensor_tensor_scan(st[:, r, 1:, 8 + j], ex[:, 0, :, j // 4], msg[:, :, j], st[:, r, 0, 8 + j:9 + j], ALU.mult, ALU.add))
                    ch.settle()
                    dve.sem_inc(s_state, 1)
                ch.end(CHUNKS // 2)
            ch.step(v.tensor_copy(mem["last"][:], st[:, 1, CH, :]))
            dve.wait_ge(s_used, 2 + CHUNKS * HOTS + 1)
            ch.step(v.tensor_copy(mem["counts"][:], counts[:]))
            ch.settle()


def join_runs(nc, mem, state_dram, end_dram):
    C = mem["C"]
    with ExitStack() as ctx:
        sb = lambda name, shape, dt: ctx.enter_context(nc.sbuf_tensor("jr_" + name, shape, dt))
        ps = lambda name, shape: ctx.enter_context(nc.psum_tensor("jr_" + name, shape, F32))
        sem = lambda name: ctx.enter_context(nc.semaphore("jr_" + name))
        total, prefix, end_f, end_i = sb("total", [P, 1], F32), sb("prefix", [P, 1], F32), sb("endf", [P, P], F32), sb("endi", [P, P], I32)
        pos, pos_f, bad, to, row = sb("pos", [P, 1], I32), sb("posf", [P, 1], F32), sb("bad", [P, 1], F32), sb("to", [P, 1], I32), sb("row", [P, ROW], F32)
        wide = sb("wide", [P, 4, 16], F32)
        tr = sb("tr", [16, 4, P], F32)
        car = sb("car", [16, 3, P + 1], F32)
        df = sb("df", [16, 2, P], F32)
        fx = sb("fx", [16, 2, P], F32)
        ws = sb("ws", [16, 2, P], F32)
        cin = sb("cin", [P, 3, 16], F32)
        mine = sb("mine", [P, 3, 16], F32)
        d2, x2, mix, mix2, new = sb("d2", [P, 2, 16], F32), sb("x2", [P, 2, 16], F32), sb("mix", [P, 2, 16], F32), sb("mix2", [P, 2, 16], F32), sb("new", [P, ROW], F32)
        m16 = sb("m16", [P, 16], F32)
        p_pre, p_tr, p_back, p_end = ps("ppre", [P, 1]), ps("ptr", [16, 4, P]), ps("pback", [P, 3, 16]), ps("pend", [P, P])
        s_dve, s_total, s_pre, s_end, s_end_t, s_endd, s_pos, s_posok, s_row, s_wide, s_tr, s_ex, s_exd, s_car, s_back, s_ex2, s_ex2d, s_new, s_scat = (
            sem(n) for n in ("dve", "total", "pre", "end", "endt", "endd", "pos", "posok", "row", "wide", "tr", "ex", "exd", "car", "back", "ex2", "ex2d", "new", "scat"))
        block = ctx.enter_context(nc.Block())

        @block.vector
        def _(dve):
            ch = Chain(dve, s_dve)
            v = nc.vector
            counts = mem["counts"]
            v.tensor_reduce(total[:], counts[:], AX.X, ALU.add).then_inc(s_total, 1)
            dve.wait_ge(s_pre, 1)
            ch.step(v.tensor_copy(prefix[:], p_pre[:])); ch.settle()
            ch.step(v.tensor_scalar(prefix[:], prefix[:], -1.0, None, ALU.add)); ch.settle()
            ch.step(v.memset(end_f[:], 1.0)); ch.settle()
            ch.step(v.tensor_tensor_scan(end_f[:], end_f[:], counts[:], prefix[:], ALU.mult, ALU.add)); ch.settle()
            v.tensor_copy(end_i[:], end_f[:]).then_inc(s_end, 1)
            dve.wait_ge(s_end_t, 1)
            ch.step(v.tensor_copy(mem["node_end"][:], p_end[:]))
            last = mem["last"]
            ch.step(v.tensor_copy(wide[:, 0].rearrange("p (h e) -> p h e", e=4), spread(last[:, 0:4], 4)))
            ch.step(v.tensor_copy(wide[:, 1].rearrange("p (h e) -> p h e", e=4), spread(last[:, 4:8], 4)))
            ch.step(v.tensor_copy(wide[:, 2], last[:, 8:24]))
            ch.step(v.tensor_copy(wide[:, 3], mem["has_start"][:, 0:1].broadcast_to([P, 16]))); ch.settle()
            dve.sem_inc(s_wide, 1)
            dve.wait_ge(s_tr, 1)
            ch.step(v.tensor_copy(tr[:], p_tr[:]))
            ch.step(v.memset(car[:, 0, 0:1], -BIG))
            ch.step(v.memset(car[:, 1:, 0:1], 0.0)); ch.settle()
            ch.step(v.tensor_scalar(tr[:, 3], tr[:, 3], -BIG, None, ALU.mult)); ch.settle()
            ch.step(v.tensor_tensor_scan(car[:, 0, 1:], tr[:, 3], tr[:, 0], car[:, 0, 0:1], ALU.add, ALU.max)); ch.settle()
            ch.step(v.tensor_tensor(df[:, 0], car[:, 0, 0:P], car[:, 0, 1:], ALU.subtract))
            ch.step(v.tensor_tensor(df[:, 1], tr[:, 0], car[:, 0, 1:], ALU.subtract)); ch.settle()
            v.tensor_tensor(df[:, 0], df[:, 0], tr[:, 3], ALU.add).then_inc(s_ex, 1)
            dve.wait_ge(s_exd, 1)
            for k in range(2):
                ch.step(v.tensor_tensor(ws[:, k], fx[:, 1], tr[:, 1 + k], ALU.mult))
            ch.settle()
            for k in range(2):
                ch.step(v.tensor_tensor_scan(car[:, 1 + k, 1:], fx[:, 0], ws[:, k], car[:, 1 + k, 0:1], ALU.mult, ALU.add))
            ch.settle()
            dve.sem_inc(s_car, 1)
            dve.wait_ge(s_pos, 16)
            ch.step(v.tensor_copy(pos_f[:], pos[:])); ch.settle()
            ch.step(v.tensor_tensor(bad[:], pos_f[:], C("slice_end"), ALU.is_ge)); ch.settle()
            ch.step(v.tensor_tensor(bad[:], bad[:], mem["first_keep"][:], ALU.is_ge)); ch.settle()
            ch.step(v.scalar_tensor_tensor(out=pos_f[:], in0=bad[:], scalar=float(1 << 20), in1=pos_f[:], op0=ALU.mult, op1=ALU.add)); ch.settle()
            ch.step(v.tensor_copy(to[:], pos_f[:]))
            dve.wait_ge(s_back, 1)
            ch.step(v.tensor_copy(cin[:], p_back[:]))
            dve.wait_ge(s_row, 16)
            for k in range(2):
                ch.step(v.tensor_copy(mine[:, k].rearrange("p (h e) -> p h e", e=4), spread(row[:, 4 * k:4 * k + 4], 4)))
            ch.step(v.tensor_copy(mine[:, 2], row[:, 8:24])); ch.settle()
            ch.step(v.tensor_tensor(m16[:], cin[:, 0], mine[:, 0], ALU.max)); ch.settle()
            ch.step(v.tensor_tensor(d2[:, 0], cin[:, 0], m16[:], ALU.subtract))
            ch.step(v.tensor_tensor(d2[:, 1], mine[:, 0], m16[:], ALU.subtract)); ch.settle()
            dve.sem_inc(s_ex2, 1)
            dve.wait_ge(s_ex2d, 1)
            ch.step(v.tensor_tensor(mix[:], cin[:, 1:], repeat(x2[:, 0], 2), ALU.mult))
            ch.step(v.tensor_tensor(mix2[:], mine[:, 1:], repeat(x2[:, 1], 2), ALU.mult)); ch.settle()
            ch.step(v.tensor_tensor(mix[:], mix[:], mix2[:], ALU.add)); ch.settle()
            ch.step(v.tensor_copy(new[:, 0:4], m16[:].rearrange("p (h e) -> p h e", e=4)[:, :, 0]))
            ch.step(v.tensor_copy(new[:, 4:8], mix[:, 0].rearrange("p (h e) -> p h e", e=4)[:, :, 0]))
            ch.step(v.tensor_copy(new[:, 8:24], mix[:, 1])); ch.settle()
            dve.sem_inc(s_new, 1)

        @block.tensor
        def _(pe):
            pe.wait_ge(s_total, 1)
            pe.matmul(p_pre[:], C("before"), total[:], start=True, stop=True).then_inc(s_pre, 1)
            pe.wait_ge(s_end, 1)
            pe.transpose(p_end[:], end_f[:], C("ident")).then_inc(s_end_t, 1)
            pe.wait_ge(s_wide, 1)
            for k in range(4):
                mm = pe.transpose(p_tr[:, k], wide[:, k], C("ident"))
            mm.then_inc(s_tr, 1)
            pe.wait_ge(s_car, 1)
            for k in range(3):
                mm = pe.transpose(p_back[:, k], car[:, k, 0:P], C("ident")[0:16, 0:16])
            mm.then_inc(s_back, 1)

        @block.scalar
        def _(act):
            act.wait_ge(s_ex, 1)
            nc.scalar.activation(fx[:], df[:], ACT.Exp).then_inc(s_exd, 1)
            act.wait_ge(s_ex2, 1)
            nc.scalar.activation(x2[:], d2[:], ACT.Exp).then_inc(s_ex2d, 1)

        @block.gpsimd
        def _(pool):
            pool.wait_ge(s_end, 1)
            pool.dma_start(end_dram.rearrange("(p c) one -> p (c one)", p=P), end_i[:].bitcast(F32)).then_inc(s_endd, 16)
            pool.wait_ge(s_endd, 16)
            at = lambda t: bass.IndirectOffsetOnAxis(ap=t[:, 0:1].bitcast(U32), axis=0)
            pool.indirect_dma_start(out=pos[:].bitcast(F32), out_offset=None, in_=end_dram, in_offset=at(mem["first"])).then_inc(s_pos, 16)
            pool.wait_ge(s_pos, 16)
            pool.indirect_dma_start(out=row[:], out_offset=None, in_=state_dram, in_offset=at(pos)).then_inc(s_row, 16)
            pool.wait_ge(s_new, 1)
            pool.indirect_dma_start(out=state_dram, out_offset=at(to), in_=new[:], in_offset=None,
                                    bounds_check=EDGES + M - 1, oob_is_err=False).then_inc(s_scat, 16)
            pool.wait_ge(s_scat, 16)


def gate(nc, mem, state_dram, gates):
    C, W = mem["C"], mem["W"]
    RG = 16
    with ExitStack() as ctx:
        sb = lambda name, shape, dt: ctx.enter_context(nc.sbuf_tensor("gt_" + name, shape, dt))
        sem = lambda name: ctx.enter_context(nc.semaphore("gt_" + name))
        now = sb("now", [P, 2, RG], I32)
        ring = sb("ring", [P, 2, RG, ROW], F32)
        ns = sb("ns", [P, TILES, ROW], F32)
        den = sb("den", [P, TILES, 4], F32)
        agg, sq = sb("agg", [P, TILES, 16], F32), sb("sq", [P, TILES, 16], F32)
        mu, sd = sb("mu", [P, TILES], F32), sb("sd", [P, TILES], F32)
        sc = sb("sc", [P, TILES, 4], F32)
        best = sb("best", [P, 2, TILES], F32)
        pick = sb("pick", [P, 2, 4, TILES], F32)
        found, t, w1 = sb("found", [P, TILES], F32), sb("t", [P, TILES], F32), sb("w1", [P, 2, TILES], F32)
        s_pool, s_spent, s_dve, s_ns, s_var, s_std, s_t, s_exp = (sem(n) for n in ("pool", "spent", "dve", "ns", "var", "std", "t", "exp"))
        s_landed, s_free = [sem("landed0"), sem("landed1")], [sem("free0"), sem("free1")]
        block = ctx.enter_context(nc.Block())

        @block.gpsimd
        def _(pool):
            for r in range(2):
                pool.sem_inc(s_free[r], 1)
            with pool.Fori(0, TILES // RG // 2) as i:
                for r in range(2):
                    pause(pool, s_free[r], i + 1, s_spent)
                    nc.gpsimd.tensor_copy(now[:, r], mem["node_end"][:, bass.ds((i * 2 + r) * RG, RG)]).then_inc(s_pool, 1)
                    pause(pool, s_pool, i * 2 + r + 1, s_spent)
                    for k in range(RG):
                        pool.indirect_dma_start(out=ring[:, r, k, :], out_offset=None, in_=state_dram,
                                                in_offset=bass.IndirectOffsetOnAxis(ap=now[:, r, k:k + 1].bitcast(U32), axis=0)).then_inc(s_landed[r], 16)

        @block.scalar
        def _(act):
            with act.Fori(0, TILES // RG // 2) as i:
                for r in range(2):
                    pause(act, s_landed[r], (i + 1) * (16 * RG), s_spent)
                    nc.scalar.activation(ns[:, bass.ds((i * 2 + r) * RG, RG), :], ring[:, r], ACT.Copy).then_inc(s_free[r], 1)
            act.wait_ge(s_var, 1)
            nc.scalar.activation(sd[:], sd[:], ACT.Sqrt, scale=1.0 / 16, bias=C("eps")).then_inc(s_std, 1)
            act.wait_ge(s_t, 1)
            nc.scalar.activation(t[:], t[:], ACT.Exp).then_inc(s_exp, 1)

        @block.vector
        def _(dve):
            ch = Chain(dve, s_dve)
            v = nc.vector

            def do(ins):
                ch.step(ins)
                ch.settle()

            for r in range(2):
                dve.wait_ge(s_free[r], 1 + TILES // RG // 2)
            four = lambda a: a.rearrange("p t (h e) -> p t h e", e=4)
            do(v.tensor_scalar(den[:], ns[:, :, 4:8], 1e-16, None, ALU.add))
            do(v.reciprocal(den[:], den[:]))
            do(v.tensor_tensor(four(agg[:]), four(ns[:, :, 8:24]), spread(den[:], 4), ALU.mult))
            do(v.tensor_tensor(agg[:], agg[:], repeat(W("b_gat"), TILES), ALU.add))
            do(v.tensor_reduce(mu[:], agg[:], AX.X, ALU.add))
            do(v.tensor_scalar(mu[:], mu[:], 1.0 / 16, None, ALU.mult))
            do(v.tensor_tensor(agg[:], agg[:], spread(mu[:], 16), ALU.subtract))
            do(v.tensor_tensor(sq[:], agg[:], agg[:], ALU.mult))
            v.tensor_reduce(sd[:], sq[:], AX.X, ALU.add).then_inc(s_var, 1)
            dve.wait_ge(s_std, 1)
            do(v.reciprocal(sd[:], sd[:]))
            do(v.tensor_tensor(agg[:], agg[:], spread(sd[:], 16), ALU.mult))
            do(v.tensor_tensor(agg[:], agg[:], repeat(W("gamma"), TILES), ALU.mult))
            do(v.tensor_tensor(agg[:], agg[:], repeat(W("beta"), TILES), ALU.add))
            do(v.tensor_reduce(sc[:], agg[:].rearrange("p t (h e) -> p t e h", e=4), AX.X, ALU.add))
            do(v.tensor_scalar(sc[:], sc[:], 0.25, None, ALU.mult))
            for n in range(2):
                do(v.tensor_reduce(best[:, n], sc[:], AX.X, ALU.max))
                for ex in range(4):
                    do(v.tensor_tensor(pick[:, n, ex], sc[:, :, ex], best[:, n], ALU.is_equal))
                do(v.tensor_copy(found[:], pick[:, n, 0]))
                for ex in range(1, 4):
                    do(v.tensor_tensor(w1[:, 0], pick[:, n, ex], found[:], ALU.is_gt))
                    do(v.tensor_tensor(found[:], found[:], pick[:, n, ex], ALU.max))
                    do(v.tensor_copy(pick[:, n, ex], w1[:, 0]))
                if n == 0:
                    do(v.scalar_tensor_tensor(out=sc[:], in0=pick[:, 0].rearrange("p e t -> p t e"), scalar=-BIG, in1=sc[:], op0=ALU.mult, op1=ALU.add))
            v.tensor_tensor(t[:], best[:, 1], best[:, 0], ALU.subtract).then_inc(s_t, 1)
            dve.wait_ge(s_exp, 1)
            do(v.tensor_scalar(w1[:, 0], t[:], 1.0, None, ALU.add))
            do(v.reciprocal(w1[:, 0], w1[:, 0]))
            do(v.tensor_tensor(w1[:, 1], t[:], w1[:, 0], ALU.mult))
            for n in range(2):
                do(v.tensor_tensor(pick[:, n], pick[:, n], repeat(w1[:, n], 4), ALU.mult))
            do(v.tensor_tensor(gates[:], pick[:, 0].rearrange("p e t -> p t e"), pick[:, 1].rearrange("p e t -> p t e"), ALU.add))


def experts(nc, mem, gates):
    h, xc, rstd, C, W = mem["h"], mem["xc"], mem["rstd"], mem["C"], mem["W"]
    N = GT * P
    with ExitStack() as ctx:
        sb = lambda name, shape, dt: ctx.enter_context(nc.sbuf_tensor("ex_" + name, shape, dt))
        ps = lambda name, shape: ctx.enter_context(nc.psum_tensor("ex_" + name, shape, F32))
        sem = lambda name: ctx.enter_context(nc.semaphore("ex_" + name))
        x, xt, hid = sb("x", [P, GT, D], F32), sb("xt", [D, N], F32), sb("hid", [P, 2, N], F32)
        y = sb("y", [P, 2, GT, D], F32)
        p_xt, p_hid, p_y = ps("pxt", [D, N]), ps("phid", [P, 2, N]), ps("py", [P, 2, GT, D])
        s_x, s_xt_p, s_xt, s_hid_p, s_hid, s_y_p, s_y, s_dve, s_spent = (sem(n) for n in ("x", "xtp", "xt", "hidp", "hid", "yp", "y", "dve", "spent"))
        block = ctx.enter_context(nc.Block())

        @block.vector
        def _(dve):
            ch = Chain(dve, s_dve)
            v = nc.vector
            with dve.Fori(0, GROUPS) as i:
                g = bass.ds(i * GT, GT)
                ch.turn(i, 2 * EXPERTS)
                pause(dve, s_xt_p, i + 1, s_spent)
                v.tensor_tensor(x[:], xc[:, g], spread(rstd[:, g], D), ALU.mult).then_inc(s_x, 1)
                for e in range(EXPERTS):
                    pause(dve, s_y_p, i * EXPERTS + e + 3, s_spent)
                    v.tensor_tensor(y[:, e % 2], p_y[:, e % 2], repeat(W("e_b2")[:, e * D:e * D + D], GT), ALU.add).then_inc(s_y, 1)
                    pause(dve, s_y, i * EXPERTS + e + 3, s_spent)
                    ch.step(v.tensor_tensor(y[:, e % 2], y[:, e % 2], spread(gates[:, g, e], D), ALU.mult)); ch.settle()
                    ch.step(v.tensor_tensor(h[:, g], h[:, g], y[:, e % 2], ALU.add)); ch.settle()
                ch.end(GROUPS)

        @block.tensor
        def _(pe):
            pe.sem_inc(s_xt_p, 1)
            pe.sem_inc(s_y_p, 2)
            pe.sem_inc(s_y, 2)
            with pe.Fori(0, GROUPS) as i:
                pause(pe, s_x, i + 1, s_spent)
                for t in range(GT):
                    mm = pe.transpose(p_xt[:, t * P:t * P + P], x[:, t, :], C("ident"))
                mm.then_inc(s_xt_p, 1)
                pause(pe, s_xt, i + 1, s_spent)
                for e in range(EXPERTS + 1):
                    if e < EXPERTS:
                        if e >= 2:
                            pause(pe, s_hid, i * EXPERTS + e - 1, s_spent)
                        for n in range(2):
                            mm = pe.matmul(p_hid[:, e % 2, n * 512:n * 512 + 512], W("e_w1")[0:D, e * HID:e * HID + HID], xt[:, n * 512:n * 512 + 512], start=True, stop=True)
                        mm.then_inc(s_hid_p, 1)
                    if e:
                        o = e - 1
                        pause(pe, s_hid, i * EXPERTS + o + 1, s_spent)
                        pause(pe, s_y, i * EXPERTS + o + 1, s_spent)
                        for t in range(GT):
                            mm = pe.matmul(p_y[:, o % 2, t, :], hid[:, o % 2, t * P:t * P + P], W("e_w2")[:, o * D:o * D + D], start=True, stop=True)
                        mm.then_inc(s_y_p, 1)

        @block.scalar
        def _(act):
            with act.Fori(0, GROUPS) as i:
                pause(act, s_xt_p, i + 2, s_spent)
                nc.scalar.activation(xt[:], p_xt[:], ACT.Copy).then_inc(s_xt, 1)
                for e in range(EXPERTS):
                    pause(act, s_hid_p, i * EXPERTS + e + 1, s_spent)
                    pause(act, s_y_p, i * EXPERTS + e + 1, s_spent)
                    nc.scalar.activation(hid[:, e % 2], p_hid[:, e % 2], ACT.Gelu, bias=W("e_b1")[:, e:e + 1]).then_inc(s_hid, 1)


def graph_experts(nc, mem, sorted_keys, table_dram, state_dram, end_dram):
    with ExitStack() as ctx:
        sb = lambda name, shape, dt: ctx.enter_context(nc.sbuf_tensor(name, shape, dt))
        mem.update(zeros=sb("zeros", [P, P], BF16), first=sb("first", [P, 1], I32), has_start=sb("has_start", [P, 1], F32),
                   first_keep=sb("first_keep", [P, 1], F32), last=sb("last", [P, ROW], F32), counts=sb("counts", [P, P], F32),
                   node_end=sb("node_end", [P, TILES], I32))
        gates = sb("gates", [P, TILES, EXPERTS], F32)
        node_table(nc, mem, table_dram)
        edge_stream(nc, mem, sorted_keys, table_dram, state_dram)
        join_runs(nc, mem, state_dram, end_dram)
        gate(nc, mem, state_dram, gates)
        experts(nc, mem, gates)


def head_attention(nc, mem):
    h, xc, rstd, C, W = mem["h"], mem["xc"], mem["rstd"], mem["C"], mem["W"]
    N = GT * P
    NG = 2 * H1
    with ExitStack() as ctx:
        sb = lambda name, shape, dt=F32: ctx.enter_context(nc.sbuf_tensor("a1_" + name, shape, dt))
        ps = lambda name, shape: ctx.enter_context(nc.psum_tensor("a1_" + name, shape, F32))
        sem = lambda name: ctx.enter_context(nc.semaphore("a1_" + name))
        x, xt, qt = sb("x", [P, GT, D]), sb("xt", [D, N]), sb("qt", [D, N])
        kv, sq = sb("kv", [P, GT * NG, C1]), sb("sq", [P, GT * NG, C1])
        mu, sd = sb("mu", [P, GT * NG]), sb("sd", [P, GT * NG])
        kvm, rt = sb("kvm", [D, GB, D]), sb("rt", [D, N])
        pj, gj = sb("pj", [P, GT, D]), sb("gj", [P, GT, D])
        p_xt, p_q, p_kv, p_kvm, p_p = ps("pxt", [D, N]), ps("pq", [D, N]), ps("pkv", [P, GT, 2 * D]), ps("pkvm", [D, GB, D]), ps("pp", [P, GT, D])
        s_x, s_xt_p, s_xt, s_q_p, s_q, s_kv_p, s_var, s_std, s_kv, s_kvm_p, s_kvm, s_o, s_rt, s_p, s_pj, s_gj, s_dve, s_spent = (
            sem(n) for n in ("x", "xtp", "xt", "qp", "q", "kvp", "var", "std", "kv", "kvmp", "kvm", "o", "rt", "p", "pj", "gj", "dve", "spent"))
        block = ctx.enter_context(nc.Block())
        flat = lambda t: t[:].rearrange("p (t g) c -> p t (g c)", t=GT)

        @block.vector
        def _(dve):
            ch = Chain(dve, s_dve)
            v = nc.vector

            def do(ins):
                ch.step(ins)
                ch.settle()

            with dve.Fori(0, GROUPS) as i:
                g = bass.ds(i * GT, GT)
                ch.turn(i, 11)
                v.tensor_tensor(x[:], xc[:, g], spread(rstd[:, g], D), ALU.mult).then_inc(s_x, 1)
                pause(dve, s_kv_p, i + 1, s_spent)
                do(v.tensor_tensor(flat(kv), p_kv[:], repeat(W("kv_b"), GT), ALU.add))
                do(v.tensor_reduce(mu[:], kv[:], AX.X, ALU.add))
                do(v.tensor_scalar(mu[:], mu[:], 1.0 / C1, None, ALU.mult))
                do(v.tensor_tensor(kv[:], kv[:], spread(mu[:], C1), ALU.subtract))
                do(v.tensor_tensor(sq[:], kv[:], kv[:], ALU.mult))
                v.tensor_reduce(sd[:], sq[:], AX.X, ALU.add).then_inc(s_var, 1)
                pause(dve, s_std, i + 1, s_spent)
                do(v.tensor_scalar(sd[:], sd[:], EPS, None, ALU.add))
                do(v.reciprocal(sd[:], sd[:]))
                do(v.tensor_tensor(kv[:], kv[:], spread(sd[:], C1), ALU.mult))
                do(v.tensor_tensor(flat(kv), flat(kv), repeat(W("kv_ln_w"), GT), ALU.mult))
                v.tensor_tensor(flat(kv), flat(kv), repeat(W("kv_ln_b"), GT), ALU.add).then_inc(s_kv, 1)
                pause(dve, s_kvm_p, i + 1, s_spent)
                v.tensor_tensor(kvm[:], p_kvm[:], repeat(C("own_head")[0:D], GB), ALU.mult).then_inc(s_kvm, 1)
                pause(dve, s_o, i + 1, s_spent)
                v.tensor_tensor(rt[:], p_q[:], xt[:], ALU.add).then_inc(s_rt, 1)
                pause(dve, s_p, i + 1, s_spent)
                v.tensor_tensor(pj[:], p_p[:], repeat(W("proj_b"), GT), ALU.add).then_inc(s_pj, 1)
                do(v.tensor_tensor(x[:], h[:, g], x[:], ALU.add))
                pause(dve, s_gj, i + 1, s_spent)
                do(v.tensor_tensor(h[:, g], x[:], gj[:], ALU.add))
                ch.end(GROUPS)

        @block.tensor
        def _(pe):
            with pe.Fori(0, GROUPS) as i:
                pause(pe, s_x, i + 1, s_spent)
                for t in range(GT):
                    mm = pe.transpose(p_xt[:, t * P:t * P + P], x[:, t, :], C("ident"))
                mm.then_inc(s_xt_p, 1)
                pause(pe, s_xt, i + 1, s_spent)
                for t in range(GT):
                    mm = pe.matmul(p_kv[:, t, :], xt[:, t * P:t * P + P], W("kv_w")[0:D], start=True, stop=True)
                mm.then_inc(s_kv_p, 1)
                for n in range(2):
                    mm = pe.matmul(p_q[:, n * 512:n * 512 + 512], W("q_w")[0:D], xt[:, n * 512:n * 512 + 512], start=True, stop=True)
                mm.then_inc(s_q_p, 1)
                pause(pe, s_kv, i + 1, s_spent)
                for b in range(GB):
                    for n in range(2):
                        mm = pe.matmul(p_kvm[:, b, :], flat(kv)[:, 2 * b + n, 0:D], flat(kv)[:, 2 * b + n, D:2 * D], start=(n == 0), stop=(n == 1))
                mm.then_inc(s_kvm_p, 1)
                pause(pe, s_kvm, i + 1, s_spent)
                pause(pe, s_q, i + 1, s_spent)
                for b in range(GB):
                    mm = pe.matmul(p_q[:, b * T:b * T + T], kvm[:, b, :], qt[:, b * T:b * T + T], start=True, stop=True)
                mm.then_inc(s_o, 1)
                pause(pe, s_rt, i + 1, s_spent)
                for t in range(GT):
                    mm = pe.matmul(p_p[:, t, :], rt[:, t * P:t * P + P], W("proj_w")[0:D], start=True, stop=True)
                mm.then_inc(s_p, 1)

        @block.scalar
        def _(act):
            a = nc.scalar
            with act.Fori(0, GROUPS) as i:
                pause(act, s_xt_p, i + 1, s_spent)
                a.activation(xt[:], p_xt[:], ACT.Copy).then_inc(s_xt, 1)
                pause(act, s_q_p, i + 1, s_spent)
                a.activation(qt[:], p_q[:], ACT.Identity, bias=W("q_b")[0:D]).then_inc(s_q, 1)
                pause(act, s_var, i + 1, s_spent)
                a.activation(sd[:], sd[:], ACT.Sqrt, scale=1.0 / (C1 - 1)).then_inc(s_std, 1)
                pause(act, s_pj, i + 1, s_spent)
                a.activation(gj[:], pj[:], ACT.Gelu).then_inc(s_gj, 1)


def route(nc, mem, route_dram):
    xc, rstd, C, W = mem["xc"], mem["rstd"], mem["C"], mem["W"]
    Q = TILES // 4
    with ExitStack() as ctx:
        sem = lambda name: ctx.enter_context(nc.semaphore("rt_" + name))
        prod = ctx.enter_context(nc.sbuf_tensor("rt_prod", [P, Q, D], F32))
        turned = ctx.enter_context(nc.sbuf_tensor("rt_turned", [P, P], F32))
        p_t = ctx.enter_context(nc.psum_tensor("rt_pt", [P, P], F32))
        s_dve, s_w, s_p, s_t, s_out = (sem(n) for n in ("dve", "w", "p", "t", "out"))
        block = ctx.enter_context(nc.Block())
        rw = mem["route"]

        @block.vector
        def _(dve):
            ch = Chain(dve, s_dve)
            v = nc.vector
            for q in range(4):
                t = slice(q * Q, q * Q + Q)
                ch.step(v.tensor_tensor(prod[:], xc[:, t], repeat(W("route_w"), Q), ALU.mult)); ch.settle()
                ch.step(v.tensor_reduce(rw[:, t], prod[:], AX.X, ALU.add)); ch.settle()
            ch.step(v.tensor_tensor(rw[:], rw[:], rstd[:], ALU.mult)); ch.settle()
            v.tensor_scalar(rw[:], rw[:], W("route_b"), None, ALU.add).then_inc(s_w, 1)
            dve.wait_ge(s_p, 1)
            v.tensor_copy(turned[:], p_t[:]).then_inc(s_t, 1)

        @block.tensor
        def _(pe):
            pe.wait_ge(s_w, 1)
            pe.transpose(p_t[:], rw[:], C("ident")).then_inc(s_p, 1)

        @block.sync
        def _(sp):
            sp.wait_ge(s_t, 1)
            sp.dma_start(route_dram.rearrange("(t p) -> t p", p=P), turned[:]).then_inc(s_out, 16)
            sp.wait_ge(s_out, 16)


def depth_mlp(nc, mem, route_dram):
    h, xc, rstd, C, W = mem["h"], mem["xc"], mem["rstd"], mem["C"], mem["W"]
    N = GT * P
    with ExitStack() as ctx:
        sb = lambda name, shape, dt=F32: ctx.enter_context(nc.sbuf_tensor("m_" + name, shape, dt))
        ps = lambda name, shape: ctx.enter_context(nc.psum_tensor("m_" + name, shape, F32))
        sem = lambda name: ctx.enter_context(nc.semaphore("m_" + name))
        mem["route"] = sb("route", [P, TILES])
        route(nc, mem, route_dram)
        x, xt, hid = sb("x", [P, GT, D]), sb("xt", [D, N]), sb("hid", [P, 2, N])
        y = sb("y", [P, GT, D])
        every = sb("every", [P, 2, GB, T])
        own = sb("own", [P, GT])
        cmp = sb("cmp", [P, 2, GT, T])
        rank = sb("rank", [P, 2, GT])
        p_xt, p_hid, p_y = ps("pxt", [D, N]), ps("phid", [P, 2, N]), ps("py", [P, GT, D])
        s_x, s_xt_p, s_xt, s_hid_p, s_hid, s_y_p, s_dve, s_ranked, s_spent = (sem(n) for n in ("x", "xtp", "xt", "hidp", "hid", "yp", "dve", "ranked", "spent"))
        s_every = [sem("every0"), sem("every1")]
        block = ctx.enter_context(nc.Block())

        @block.sync
        def _(sp):
            sp.sem_inc(s_ranked, 2)
            rows = route_dram.rearrange("(g n) -> g n", n=N)
            with sp.Fori(0, GROUPS // 2) as i:
                for r in range(2):
                    pause(sp, s_ranked, i * 2 + r + 1, s_spent)
                    sp.dma_start(every[:, r].rearrange("p b t -> p (b t)"), rows[bass.ds(i * 2 + r, 1), :].broadcast_to([P, N])).then_inc(s_every[r], 16)

        @block.vector
        def _(dve):
            ch = Chain(dve, s_dve)
            v = nc.vector

            def do(ins):
                ch.step(ins)
                ch.settle()

            with dve.Fori(0, GROUPS // 2) as i:
                ch.turn(i, 2 * (2 * GT + 8))
                for r in range(2):
                    g = bass.ds((i * 2 + r) * GT, GT)
                    v.tensor_tensor(x[:], xc[:, g], spread(rstd[:, g], D), ALU.mult).then_inc(s_x, 1)
                    do(v.tensor_copy(own[:], mem["route"][:, g]))
                    pause(dve, s_every[r], (i + 1) * 16, s_spent)
                    for t in range(GT):
                        them = every[:, r, t // 2, :]
                        ch.step(v.tensor_scalar(cmp[:, 0, t], them, own[:, t:t + 1], None, ALU.is_gt, op1=ALU.add, accum_out=rank[:, 0, t:t + 1]))
                        ch.step(v.scalar_tensor_tensor(out=cmp[:, 1, t], in0=them, scalar=own[:, t:t + 1], in1=C("ties")[:, (t % 2) * T:(t % 2) * T + T], op0=ALU.is_equal, op1=ALU.mult, accum_out=rank[:, 1, t:t + 1]))
                    ch.settle()
                    dve.sem_inc(s_ranked, 1)
                    do(v.tensor_tensor(rank[:, 0], rank[:, 0], rank[:, 1], ALU.add))
                    do(v.tensor_scalar(rank[:, 0], rank[:, 0], KEEP - 0.5, None, ALU.is_lt))
                    do(v.tensor_tensor(rank[:, 0], rank[:, 0], own[:], ALU.mult))
                    pause(dve, s_y_p, i * 2 + r + 1, s_spent)
                    do(v.tensor_tensor(y[:], p_y[:], repeat(W("m_b2"), GT), ALU.add))
                    do(v.tensor_tensor(y[:], y[:], spread(rank[:, 0], D), ALU.mult))
                    do(v.tensor_tensor(y[:], y[:], x[:], ALU.add))
                    do(v.tensor_tensor(h[:, g], h[:, g], y[:], ALU.add))
                ch.end(GROUPS // 2)

        @block.tensor
        def _(pe):
            with pe.Fori(0, GROUPS) as i:
                pause(pe, s_x, i + 1, s_spent)
                for t in range(GT):
                    mm = pe.transpose(p_xt[:, t * P:t * P + P], x[:, t, :], C("ident"))
                mm.then_inc(s_xt_p, 1)
                pause(pe, s_xt, i + 1, s_spent)
                for m in range(2):
                    for n in range(2):
                        mm = pe.matmul(p_hid[:, m, n * 512:n * 512 + 512], W("m_w1")[0:D, m * P:m * P + P], xt[:, n * 512:n * 512 + 512], start=True, stop=True)
                    mm.then_inc(s_hid_p, 1)
                pause(pe, s_hid, i * 2 + 2, s_spent)
                for t in range(GT):
                    for m in range(2):
                        mm = pe.matmul(p_y[:, t, :], hid[:, m, t * P:t * P + P], W("m_w2")[:, m * D:m * D + D], start=(m == 0), stop=(m == 1))
                mm.then_inc(s_y_p, 1)

        @block.scalar
        def _(act):
            with act.Fori(0, GROUPS) as i:
                pause(act, s_xt_p, i + 1, s_spent)
                nc.scalar.activation(xt[:], p_xt[:], ACT.Copy).then_inc(s_xt, 1)
                for m in range(2):
                    pause(act, s_hid_p, i * 2 + m + 1, s_spent)
                    nc.scalar.activation(hid[:, m], p_hid[:, m], ACT.Gelu_apprx_tanh, bias=W("m_b1")[:, m:m + 1]).then_inc(s_hid, 1)


def lm_tower_kernel(nc, ids, emb_2, emb_3, emb_4, edges, consts, weights, scratch, out):
    sorted_keys, table_dram, state_dram, top_dram, wt_dram, end_dram = scratch
    with ExitStack() as ctx:
        sb = lambda name, shape, dt: ctx.enter_context(nc.sbuf_tensor(name, shape, dt))
        mem = {"c": sb("consts", [P, CONST_N], F32), "w": sb("weights", [P, WEIGHT_N], F32),
               "h": sb("h", [P, TILES, D], F32), "mean": sb("mean", [P, TILES], F32), "rstd": sb("rstd", [P, TILES], F32),
               "top_dram": top_dram, "s_weights": ctx.enter_context(nc.semaphore("s_weights"))}
        mem["C"] = lambda name: mem["c"][:, CONST[name][0]:sum(CONST[name])]
        mem["W"] = lambda name: mem["w"][:, WEIGHT[name][0]:sum(WEIGHT[name])]
        h = mem["h"]
        with nc.sbuf_tensor("e34", [P, 2, TILES, D], F32) as e34:
            mem["e34"] = e34
            embed_and_sort(nc, mem, ids, (emb_2, emb_3, emb_4), edges, consts, weights, sorted_keys)
            with nc.semaphore("s_sum") as s_sum, nc.Block() as block:
                @block.vector
                def _(dve):
                    nc.vector.tensor_tensor(h[:], h[:], e34[:, 0], ALU.add).then_inc(s_sum, 1)
                    dve.wait_ge(s_sum, 1)
                    nc.vector.tensor_tensor(h[:], h[:], e34[:, 1], ALU.add)
        mem["xc"] = sb("xc", [P, TILES, D], F32)
        layernorm_stats(nc, mem, ctx, "0")
        phase_attention(nc, mem)
        layernorm_stats(nc, mem, ctx, "1")
        graph_experts(nc, mem, sorted_keys, table_dram, state_dram, end_dram)
        layernorm_stats(nc, mem, ctx, "2")
        head_attention(nc, mem)
        layernorm_stats(nc, mem, ctx, "3")
        depth_mlp(nc, mem, wt_dram)
        with nc.semaphore("s_out") as s_out, nc.Block() as block:
            @block.sync
            def _(sp):
                sp.dma_start(out.rearrange("b (two p) d -> p b two d", p=P), h[:].rearrange("p (b two) d -> p b two d", two=2)).then_inc(s_out, 16)
                sp.wait_ge(s_out, 16)


def shape_constants():
    import numpy as np
    p = np.arange(P)
    f = np.float32
    bits = [1.0 - 2.0 * ((p >> b) & 1) for b in range(7)]
    two_pi_half = np.pi
    c = {
        "ident": np.eye(P), "causal": np.concatenate([np.arange(T)[None] >= p[:, None], (p[None] >= p[:, None])], 1),
        "rnorm": 1.0 / np.sqrt(np.stack([p + 1, p + P + 1], 1) * float(K)),
        "emb_scale": np.stack([np.where((p < n + 1) & (half == 0), 0.0, 0.25) for n in range(3) for half in range(2)], 1),
        "fold": np.where(p % 64 < K, -1.0, 1.0)[:, None], "sin_scale": np.where(p % 64 < K, -two_pi_half, two_pi_half)[:, None],
        "sin_bias": np.where(p % 64 < K, two_pi_half / 2, 0.0)[:, None], "eps": np.full((P, 1), EPS),
        "iota": np.tile(p[None], (P, 1)), "bit_sign": np.stack(bits, 1),
        "flip": np.stack([-bits[0]] + [bits[b] * bits[b + 1] for b in range(6)], 1),
        "before": p[:, None] < p[None], "ties": np.concatenate([np.arange(T)[None] < p[:, None], np.arange(T)[None] < p[:, None] + P], 1),
        "own_head": np.where((p[:, None] // C1 == np.arange(D)[None] // C1) & (p[:, None] < D), 1.0 / T, 0.0),
        "zero": np.zeros((P, 1)), "ones": np.ones((P, 1)),
        "all_but_last": np.tile((p[None] < P - 1), (P, 1)), "slice_end": ((p + 1) * float(ALL_COLS))[:, None],
    }
    out = np.zeros((P, CONST_N), f)
    for name, (at, width) in CONST.items():
        out[:, at:at + width] = c[name]
    return out


def lay_out_weights(a):
    import numpy as np
    row = lambda v: np.broadcast_to(np.asarray(v).reshape(1, -1), (P, np.asarray(v).size))
    col = lambda *vs: np.concatenate([np.asarray(v).reshape(-1, 1) for v in vs], 0)
    qkv_w = np.asarray(a["L1_attn_W_qkv"]).reshape(H1, 3, C1, D)
    qkv_b = np.asarray(a["L1_attn_b_qkv"]).reshape(H1, 3, C1)
    side = lambda m: np.concatenate([np.asarray(m[e]) for e in range(m.shape[0])], 1)
    kv = lambda x: np.concatenate([x[:, 1].reshape(D, -1), x[:, 2].reshape(D, -1)], 0)
    w = {
        "kq_w1": np.concatenate([a["L0_attn_kw1"].T, a["L0_attn_qw1"].T], 1),
        "kq_w2": np.concatenate([np.concatenate([a["L0_attn_%sw2" % n].T] * 2, 1) for n in "kq"], 0),
        "v_w": a["L0_attn_vw"].T, "kq_b1": col(a["L0_attn_kb1"], a["L0_attn_qb1"]),
        "k_b2": col(a["L0_attn_kb2"], a["L0_attn_kb2"]), "q_b2": col(a["L0_attn_qb2"], a["L0_attn_qb2"]),
        "v_b": row(a["L0_attn_vb"]), "w_gat": a["L0_ffn_W_gat"], "att_src": row(a["L0_ffn_att_src"]),
        "att_dst": row(a["L0_ffn_att_dst"]), "b_gat": row(a["L0_ffn_b_gat"]), "gamma": row(a["L0_ffn_ln_gamma"]),
        "beta": row(a["L0_ffn_ln_beta"]), "e_w1": side(a["L0_ffn_W1"]), "e_b1": a["L0_ffn_b1"].T,
        "e_w2": side(a["L0_ffn_W2"]), "e_b2": row(a["L0_ffn_b2"]),
        "q_w": qkv_w[:, 0].reshape(D, D).T, "q_b": col(qkv_b[:, 0]), "kv_w": kv(qkv_w).T, "kv_b": row(kv(qkv_b[..., None])),
        "kv_ln_w": row(np.concatenate([a["L1_attn_kln_w"].reshape(-1), a["L1_attn_vln_w"].reshape(-1)])),
        "kv_ln_b": row(np.concatenate([a["L1_attn_kln_b"].reshape(-1), a["L1_attn_vln_b"].reshape(-1)])),
        "proj_w": a["L1_attn_W_proj"].T, "proj_b": row(a["L1_attn_b_proj"]),
        "route_w": row(a["L1_ffn_wr"]), "route_b": row(a["L1_ffn_br"]), "m_w1": a["L1_ffn_w1"],
        "m_b1": np.asarray(a["L1_ffn_b1"]).reshape(2, P).T, "m_w2": np.concatenate([a["L1_ffn_w2"][:P], a["L1_ffn_w2"][P:]], 1),
        "m_b2": row(a["L1_ffn_b2"]),
    }
    out = np.zeros((P, WEIGHT_N), np.float32)
    for name, (at, width) in WEIGHT.items():
        out[:w[name].shape[0], at:at + width] = w[name]
    return out


def kernel(**inputs):
    import numpy as _np
    import concourse.bacc as _bacc
    from concourse import mybir as _mybir
    from concourse.bass_utils import run_bass_kernel_spmd as _run

    nc = _bacc.Bacc("TRN2", target_bir_lowering=False, num_devices=1)
    a = {k: _np.asarray(v) for k, v in inputs.items()}
    arrays = {"ids": a["x"], "emb_2": a["L0_tok_emb_2"], "emb_3": a["L0_tok_emb_3"], "emb_4": a["L0_tok_emb_4"],
              "edges": a["L0_ffn_edge_index"], "consts": shape_constants(), "weights": lay_out_weights(a)}
    args = [nc.dram_tensor("in_" + n, v.shape, _mybir.dt.from_np(v.dtype), kind="ExternalInput").ap() for n, v in arrays.items()]
    scratch = [nc.dram_tensor(n, shape, F32, kind="Internal").ap() for n, shape in (
        ("sorted_keys", (EDGES + M,)), ("node_table", (M, ROW)), ("edge_states", (EDGES + M, ROW)), ("top_keys", (M,)), ("route", (B * T,)), ("node_ends", (M, 1)))]
    out = nc.dram_tensor("out_0_dram", (B, T, D), F32, kind="ExternalOutput").ap()
    lm_tower_kernel(nc, *args, scratch, out)
    r = _run(nc, [{"in_" + n: _np.ascontiguousarray(v) for n, v in arrays.items()}], core_ids=[0])
    return r.results[0]["out_0_dram"]
```

```python
from contextlib import ExitStack

import concourse.bass as bass
from concourse import mybir

ALU = mybir.AluOpType
ACT = mybir.ActivationFunctionType
AX = mybir.AxisListType
F32 = mybir.dt.float32
BF16 = mybir.dt.bfloat16
I32 = mybir.dt.int32
U32 = mybir.dt.uint32

P = 128
B, T, D = 64, 256, 64
M = B * T
TILES = M // P
GT = 8
GB = GT // 2
GROUPS = TILES // GT
ST = 4
SB = ST // 2
SLOTS = TILES // ST
TURNS = SLOTS // 2
SN = ST * P
VOCAB, PRIME = 125000, 31
EPS = 1e-5
K = 32
EDGES = 262144
COLS = EDGES // P
NODE_COLS = M // P
ALL_COLS = COLS + NODE_COLS
EXPERTS, HEADS = 4, 4
HID = 2 * D
KEY_BASE = 1 << 29
ROW = 24
BIG = 1e30
H1, C1 = 16, 4
F2 = 4 * D
KEEP = T // 2 - 1


def columns(spec):
    at, n = {}, 0
    for name, width in spec:
        at[name] = (n, width)
        n += width
    return at, n


CONST, CONST_N = columns([
    ("ident", 128), ("causal", 384), ("rnorm", 2), ("emb_scale", 6), ("fold", 1), ("sin_scale", 1),
    ("sin_bias", 1), ("eps", 1), ("iota", 128), ("bit_sign", 7), ("before", 128), ("ties", 512),
    ("own_head", 128), ("zero", 1), ("flip", 7), ("all_but_last", 128), ("slice_end", 1), ("ones", 1), ("ones_row", 128),
])
WEIGHT, WEIGHT_N = columns([
    ("k_w1", 128), ("q_w1", 128), ("k_w2", 128), ("q_w2", 128), ("v_w", 128), ("k_b1", 1), ("q_b1", 1), ("k_b2", 1), ("q_b2", 1), ("v_b", 64),
    ("w_gat", 16), ("att_src", 16), ("att_dst", 16), ("b_gat", 16), ("gamma", 16), ("beta", 16),
    ("e_w1", EXPERTS * HID), ("e_b1", EXPERTS), ("e_w2", EXPERTS * D), ("e_b2", EXPERTS * D),
    ("q_w", 128), ("q_b", 1), ("kv_w", 256), ("kv_b", 256), ("kv_ln_w", 256), ("kv_ln_b", 256),
    ("proj_w", 128), ("proj_b", 64), ("route_w", 64), ("route_b", 1),
    ("m_w1", F2), ("m_b1", 2), ("m_w2", 2 * D), ("m_b2", 64),
])


class Chain:

    def __init__(self, eng, sem):
        self.eng, self.sem, self.base, self.n = eng, sem, 0, 0

    def step(self, ins):
        ins.then_inc(self.sem, 1)
        self.n += 1

    def settle(self):
        self.eng.wait_ge(self.sem, self.base + self.n)

    def turn(self, i, per_turn):
        self.start, self.per_turn = self.n if isinstance(self.base, int) else None, per_turn
        self.base, self.n = i * per_turn + self.start, 0

    def resume(self, i):
        self.base, self.n = i * self.per_turn + self.start, 0

    def end(self, turns):
        assert self.n == self.per_turn, (self.n, self.per_turn)
        self.base, self.n = 0, self.start + turns * self.per_turn


def pause(eng, sem, value, spent):
    eng.wait_ge(sem, value)
    eng.sem_inc(spent, 1)


def spread(ap, n):
    return ap.unsqueeze(len(ap.shape)).broadcast_to(list(ap.shape) + [n])


def repeat(ap, n):
    s = list(ap.shape)
    return ap.unsqueeze(1).broadcast_to([s[0], n] + s[1:])


def clear(nc, sems):
    with nc.Block() as block:
        @block.gpsimd
        def _(pool):
            for s in sems:
                pool.sem_clear(s)


def ln_sums(do, apart, v, mem, g, sq):
    h, xc, mean, rstd = mem["h"], mem["xc"], mem["mean"], mem["rstd"]
    apart()
    do(v.tensor_reduce(mean[:, g], h[:, g], AX.X, ALU.add))
    do(v.scalar_tensor_tensor(out=xc[:, g], in0=spread(mean[:, g], D), scalar=-1.0 / D, in1=h[:, g], op0=ALU.mult, op1=ALU.add))
    do(v.tensor_tensor(sq, xc[:, g], xc[:, g], ALU.mult))
    apart()
    do(v.tensor_reduce(rstd[:, g], sq, AX.X, ALU.add))


LN_STEPS = 4


def ln_root(nc, mem, act, s_sums, s_root):
    act.wait_ge(s_sums, 1)
    nc.scalar.activation(mem["rstd"][:], mem["rstd"][:], ACT.Sqrt, scale=1.0 / D, bias=mem["C"]("eps")).then_inc(s_root, 1)


def ln_finish(nc, mem, dve, s_sums, s_root):
    dve.sem_inc(s_sums, 1)
    dve.wait_ge(s_root, 1)
    nc.vector.reciprocal(mem["rstd"][:], mem["rstd"][:])


def staggered(eng, step, stages, chain=None, per_turn=0):
    def edge(n):
        step([n - s if 0 <= n - s < SLOTS else None for s in range(stages)], n % 2)

    first = stages + (stages % 2)
    for n in range(first):
        edge(n)
    turns = (SLOTS - first) // 2
    with eng.Fori(0, turns) as i:
        if chain is not None:
            chain.turn(i, per_turn)
        for r in range(2):
            step([i * 2 + (first + r - s) for s in range(stages)], r)
        if chain is not None:
            chain.end(turns)
    for n in range(SLOTS, SLOTS + stages - 1):
        edge(n)


def embed_and_sort(nc, mem, ids, tables, edges, consts, weights, sorted_keys):
    c, w, h, e34 = mem["c"], mem["w"], mem["h"], mem["e34"]
    with ExitStack() as ctx:
        sb = lambda name, shape, dt: ctx.enter_context(nc.sbuf_tensor(name, shape, dt))
        sems = []

        def sem(name):
            sems.append(ctx.enter_context(nc.semaphore(name)))
            return sems[-1]

        idf = sb("idf", [B, T + 3], F32)
        idi = sb("idi", [B, T], I32)
        hashes = sb("hashes", [B, 3, T], F32)
        quot = sb("quot", [B, 3, T], I32)
        quotf = sb("quotf", [B, 3, T], F32)
        rows = sb("rows", [P, TILES, 3], I32)
        rows_now = sb("rows_now", [P, 2, GT * 3], I32)
        ring = sb("ring", [P, 2, 3, GT, D], F32)
        ends = sb("ends", [P, 2, COLS], I32)
        keys = [sb("keys0", [P, COLS], F32), sb("keys1", [P, COLS], F32)]
        nodes = sb("nodes", [P, COLS], I32)
        nodes2 = sb("nodes2", [P, COLS], I32)
        tops = [sb("tops0", [P, P], F32), sb("tops1", [P, P], F32)]
        turned = ctx.enter_context(nc.psum_tensor("turned", [P, COLS], F32))
        idx_t = ctx.enter_context(nc.psum_tensor("idx_t", [P, 6, B], F32))

        s_const, s_ids, s_edges = sem("s_const"), sem("s_ids"), sem("s_edges")
        s_dve = sem("s_dve1")
        s_pool = sem("s_pool1")
        s_hash = sem("s_hash")
        s_idx_t = sem("s_idx_t")
        s_rows = sem("s_rows")
        s_landed = [sem("s_landed0"), sem("s_landed1")]
        s_drained = [sem("s_drained0"), sem("s_drained1")]
        s_spent = sem("s_spent1")
        s_turn_go, s_turned = sem("s_turn_go"), sem("s_turned")
        s_iota = sem("s_iota")
        s_tops, s_tops_back, s_sorted = sem("s_tops"), sem("s_tops_back"), sem("s_sorted")
        s_tops_w, s_low_w = sem("s_tops_w"), sem("s_low_w")

        ident = mem["C"]("ident")
        kept = {"k": keys, "t": tops}
        PHASES = [("k", top) for top in range(1, 19)] + [("k", 18), ("t", 14)]
        top_dram = mem["top_dram"]

        final, final_top = (sum(range(1, 19)) + 1 + 18) % 2, 14 % 2

        stage = ExitStack()
        block = stage.enter_context(nc.Block())

        @block.sync
        def _(sp):
            sp.dma_start(idi[:], ids).then_inc(s_ids, 16)
            sp.dma_start(c[:], consts).then_inc(s_const, 16)
            sp.dma_start(ends[:], edges.rearrange("two (p c) -> p two c", p=P)).then_inc(s_edges, 16)
            sp.dma_start(w[:], weights).then_inc(mem["s_weights"], 16)
            sp.wait_ge(s_tops, 1)
            sp.dma_start(top_dram.rearrange("(p c) -> p c", p=8), nodes2[120:128, :].bitcast(F32)).then_inc(s_tops_w, 16)
            sp.wait_ge(s_tops_w, 16)
            sp.dma_start(tops[0][:], top_dram.rearrange("(p c) -> p c", p=P)).then_inc(s_tops_back, 16)
            sp.wait_ge(s_sorted, 2)
            sp.dma_start(sorted_keys[0:EDGES].rearrange("(p c) -> p c", p=P), keys[final][:]).then_inc(s_low_w, 16)
            sp.dma_start(sorted_keys[EDGES:].rearrange("(p c) -> p c", p=P), tops[final_top][:]).then_inc(s_low_w, 16)
            sp.wait_ge(s_low_w, 32)
            sp.wait_ge(mem["s_weights"], 16)

        @block.gpsimd
        def _(pool):
            nc.gpsimd.iota(nodes[:], pattern=[[-1, COLS]], base=EDGES - 1, channel_multiplier=-COLS).then_inc(s_iota, 1)
            pool.wait_ge(s_rows, 1)
            with pool.Fori(0, GROUPS // 2) as i:
                for r in range(2):
                    pause(pool, s_drained[r], i * 6 + 6, s_spent)
                    nc.gpsimd.tensor_copy(rows_now[:, r, :], rows[:].rearrange("p t n -> p (t n)")[:, bass.ds((i * 2 + r) * (GT * 3), GT * 3)]).then_inc(s_pool, 1)
                    pause(pool, s_pool, i * 2 + r + 1, s_spent)
                    for t in range(GT):
                        for n in range(3):
                            pool.indirect_dma_start(
                                out=ring[:, r, n, t, :], out_offset=None, in_=tables[n],
                                in_offset=bass.IndirectOffsetOnAxis(ap=rows_now[:, r, t * 3 + n:t * 3 + n + 1].bitcast(U32), axis=0),
                            ).then_inc(s_landed[r], 16)

        @block.scalar
        def _(act):
            act.wait_ge(s_const, 16)
            for r in range(2):
                act.sem_inc(s_drained[r], 6)
            with act.Fori(0, GROUPS // 2) as i:
                for r in range(2):
                    pause(act, s_landed[r], (i + 1) * (GT * 3 * 16), s_spent)
                    for n in range(3):
                        for half in range(2):
                            to = h[:] if n == 0 else e34[:, n - 1]
                            to = to.rearrange("p (g b two) d -> p g b two d", b=GB, two=2)[:, bass.ds(i * 2 + r, 1), :, half, :]
                            nc.scalar.activation(
                                to.rearrange("p g b d -> p (g b) d"),
                                ring[:, r, n].rearrange("p (b two) d -> p b two d", two=2)[:, :, half, :],
                                ACT.Copy, scale=mem["C"]("emb_scale")[:, n * 2 + half:n * 2 + half + 1],
                            ).then_inc(s_drained[r], 1)

        @block.vector
        def _(dve):
            ch = Chain(dve, s_dve)
            v = nc.vector
            ch.step(v.memset(idf[:, 0:3], 0.0))
            dve.wait_ge(s_ids, 16)
            ch.step(v.tensor_copy(idf[:, 3:], idi[:]))
            ch.settle()
            for n in range(3):
                power = float(PRIME ** (n + 1) % VOCAB)
                before = idf[:, 3:] if n == 0 else hashes[:, n - 1, :]
                ch.step(v.scalar_tensor_tensor(out=hashes[:, n, :], in0=idf[:, 2 - n:2 - n + T], scalar=power, in1=before, op0=ALU.mult, op1=ALU.add))
                ch.settle()
            ch.step(v.tensor_scalar(quot[:], hashes[:], 1.0 / VOCAB, None, ALU.mult)); ch.settle()
            ch.step(v.tensor_copy(quotf[:], quot[:])); ch.settle()
            ch.step(v.scalar_tensor_tensor(out=hashes[:], in0=quotf[:], scalar=-float(VOCAB), in1=hashes[:], op0=ALU.mult, op1=ALU.add)); ch.settle()
            ch.step(v.tensor_scalar(quotf[:], hashes[:], 0.0, float(VOCAB), ALU.is_lt, ALU.mult)); ch.settle()
            ch.step(v.tensor_tensor(hashes[:], hashes[:], quotf[:], ALU.add)); ch.settle()
            ch.step(v.tensor_scalar(quotf[:], hashes[:], float(VOCAB), -float(VOCAB), ALU.is_ge, ALU.mult)); ch.settle()
            v.tensor_tensor(hashes[:], hashes[:], quotf[:], ALU.add).then_inc(s_hash, 1)
            dve.wait_ge(s_idx_t, 1)
            v.tensor_copy(rows[:].rearrange("p (b two) n -> p n two b", two=2),
                          idx_t[:].rearrange("p (n two) b -> p n two b", two=2)).then_inc(s_rows, 1)

            dve.wait_ge(s_edges, 16)
            ki = keys[0][:].bitcast(I32)
            ch.step(v.tensor_scalar(ends[:, 1], ends[:, 1], 15, KEY_BASE | (1 << 14), ALU.logical_shift_left, ALU.bitwise_or)); ch.settle()
            ch.step(v.tensor_tensor(ki, ends[:, 1], ends[:, 0], ALU.bitwise_or))
            dve.wait_ge(s_iota, 1)
            ch.step(v.tensor_scalar(nodes[:], nodes[:], float(M), None, ALU.min)); ch.settle()
            ch.step(v.tensor_scalar(nodes2[:], nodes[:], float(M), None, ALU.add)); ch.settle()
            ch.step(v.tensor_scalar(nodes2[:], nodes2[:], 15, None, ALU.logical_shift_left)); ch.settle()
            ch.step(v.tensor_tensor(nodes2[:], nodes2[:], nodes[:], ALU.bitwise_or)); ch.settle()
            dve.wait_ge(s_const, 16)

            now = [0]
            turns = [0]

            def exchange(arr, step, lo_from=None):
                pairs = lambda t: t.rearrange("p (n two d) -> p n two d", two=2, d=step)
                a = pairs(kept[arr][now[0]][:])
                left, right = a[:, :, 0, :], a[:, :, 1, :]
                o = pairs(kept[arr][1 - now[0]][:])
                if lo_from is not None:
                    left = pairs(lo_from)[:, :, 0, :]
                    ch.step(v.tensor_copy(right, pairs(lo_from)[:, :, 1, :]))
                    ch.settle()
                ch.step(v.tensor_tensor(o[:, :, 0, :], left, right, ALU.min))
                ch.step(v.tensor_tensor(o[:, :, 1, :], left, right, ALU.max))
                ch.settle()
                now[0] = 1 - now[0]

            def turn(arr):
                turns[0] += 1
                dve.sem_inc(s_turn_go, 1)
                dve.wait_ge(s_turned, turns[0])
                return turned[:, 0:COLS if arr == "k" else P]

            def merge(top, arr="k"):
                low = 11 if arr == "k" else 7
                j = top - 1
                if top > low:
                    src = turn(arr)
                    while j >= low:
                        exchange(arr, 1 << (j - low), src)
                        src = None
                        j -= 1
                    while j >= 7:
                        exchange(arr, 1 << j)
                        j -= 1
                    src = turn(arr)
                    while j >= 0:
                        exchange(arr, 1 << j, src)
                        src = None
                        j -= 1
                else:
                    while j >= 0:
                        exchange(arr, 1 << j)
                        j -= 1

            def negate(ap, by):
                ch.step(v.tensor_scalar(ap, ap, by, None, ALU.mult))

            for k in range(1, 19):
                cur = kept["k"][now[0]]
                if k == 1:
                    negate(cur[:].rearrange("p (n a d) -> p n a d", a=2, d=2)[:, :, 1, :], -1.0)
                elif k <= 10:
                    q = cur[:].rearrange("p (n a b d) -> p n a b d", a=2, b=2, d=1 << (k - 1))
                    negate(q[:, :, 0, 1, :], -1.0)
                    negate(q[:, :, 1, 0, :], -1.0)
                elif k == 11:
                    negate(cur[:, 0:COLS // 2], mem["C"]("bit_sign")[:, 0:1])
                    negate(cur[:, COLS // 2:], mem["C"]("flip")[:, 0:1])
                elif k < 18:
                    negate(cur[:], mem["C"]("flip")[:, k - 11:k - 10])
                else:
                    negate(cur[:], mem["C"]("bit_sign")[:, 6:7])
                ch.settle()
                merge(k)
            cur, oth = kept["k"][now[0]], kept["k"][1 - now[0]]
            n2 = nodes2[:].bitcast(F32)
            ch.step(v.tensor_copy(oth[0:96, :], cur[0:96, :]))
            ch.step(v.tensor_tensor(oth[96:P, :], cur[96:P, :], n2[96:P, :], ALU.min))
            ch.settle()
            v.tensor_tensor(n2[96:P, :], cur[96:P, :], n2[96:P, :], ALU.max).then_inc(s_tops, 1)
            now[0] = 1 - now[0]
            merge(18)
            assert now[0] == final
            dve.sem_inc(s_sorted, 1)
            now[0] = 0
            dve.wait_ge(s_tops_back, 16)
            merge(14, "t")
            assert now[0] == final_top
            dve.sem_inc(s_sorted, 1)

        @block.tensor
        def _(pe):
            pe.wait_ge(s_const, 16)
            pe.wait_ge(s_hash, 1)
            for n in range(3):
                for half in range(2):
                    mm = pe.transpose(idx_t[:, n * 2 + half, :], hashes[:, n, half * P:half * P + P], ident[0:B, 0:B])
            mm.then_inc(s_idx_t, 1)
            turns, done = 0, 0
            for n, (arr, top) in enumerate(PHASES):
                if n == 18:
                    done += 1
                if arr == "t":
                    done = 0
                if arr == "k" and top <= 11:
                    done += top
                    continue
                for exchanges in (top - 7, 7):
                    turns += 1
                    pe.wait_ge(s_turn_go, turns)
                    for b in range((COLS if arr == "k" else P) // P):
                        mm = pe.transpose(turned[:, b * P:b * P + P], kept[arr][done % 2][:, b * P:b * P + P], ident)
                    mm.then_inc(s_turned, 1)
                    done += exchanges
        stage.close()
        clear(nc, sems)


def layernorm_stats(nc, mem, ctx, name, first=None):
    h, xc, rstd = mem["h"], mem["xc"], mem["rstd"]
    with ExitStack() as ctx:
        sem = lambda n: ctx.enter_context(nc.semaphore(n + name))
        sq = ctx.enter_context(nc.sbuf_tensor("sq" + name, [P, 2, TILES // 4, D], F32))
        s_dve, s_xc, s_sq, s_var, s_std = sem("ln_dve"), sem("ln_xc"), sem("ln_sq"), sem("ln_var"), sem("ln_std")
        s_read = sem("ln_read")
        block = ctx.enter_context(nc.Block())
        Q = TILES // 4

        @block.vector
        def _(dve):
            ch = Chain(dve, s_dve)
            v = nc.vector
            if first is not None:
                first(v, ch)
            mean = mem["mean"]
            for q in range(4):
                t = slice(q * Q, q * Q + Q)
                ch.step(v.tensor_reduce(mean[:, t], h[:, t], AX.X, ALU.add)); ch.settle()
                ch.step(v.tensor_scalar(mean[:, t], mean[:, t], 1.0 / D, None, ALU.mult)); ch.settle()
                v.tensor_tensor(xc[:, t], h[:, t], spread(mean[:, t], D), ALU.subtract).then_inc(s_xc, 1)
                if q:
                    dve.wait_ge(s_sq, q)
                    v.tensor_reduce(rstd[:, (q - 1) * Q:q * Q], sq[:, (q - 1) % 2], AX.X, ALU.add).then_inc(s_read, 1)
            dve.wait_ge(s_sq, 4)
            v.tensor_reduce(rstd[:, 3 * Q:], sq[:, 1], AX.X, ALU.add).then_inc(s_read, 1)
            dve.wait_ge(s_std, 1)
            v.reciprocal(rstd[:], rstd[:])

        @block.scalar
        def _(act):
            for q in range(4):
                act.wait_ge(s_xc, q + 1)
                if q >= 2:
                    act.wait_ge(s_read, q - 1)
                nc.scalar.activation(sq[:, q % 2], xc[:, q * Q:q * Q + Q], ACT.Square).then_inc(s_sq, 1)
            act.wait_ge(s_read, 4)
            nc.scalar.activation(rstd[:], rstd[:], ACT.Sqrt, scale=1.0 / D, bias=mem["C"]("eps")).then_inc(s_std, 1)


def phase_attention(nc, mem):
    h, xc, rstd, C, W = mem["h"], mem["xc"], mem["rstd"], mem["C"], mem["W"]
    with ExitStack() as ctx:
        sb = lambda name, shape: ctx.enter_context(nc.sbuf_tensor("a0_" + name, shape, F32))
        ps = lambda name, shape: ctx.enter_context(nc.psum_tensor("a0_" + name, shape, F32))
        sem = lambda name: ctx.enter_context(nc.semaphore("a0_" + name))
        x = sb("x", [P, 2, 2, SB, D])
        xt = sb("xt", [P, 2, T])
        hid = sb("hid", [P, 2, 2, T])
        u, phi = sb("u", [P, 2, 2, T]), sb("phi", [P, 2, 2, T])
        val = sb("val", [P, 2, 2, SB, D])
        sm = sb("sm", [P, 2, SB, 384])
        ret, sq = sb("ret", [P, 2, ST, D]), sb("sq", [P, 2, ST, D])
        p_xt, p_hid, p_ph, p_v = ps("pxt", [P, 512]), ps("phid", [P, 2, T]), ps("pph", [P, 2, T]), ps("pv", [P, 512])
        p_sc, p_o = [ps("psc%d" % b, [P, 512]) for b in range(SB)], [ps("po%d" % r, [P, 512]) for r in range(2)]
        out_p = lambda r: p_o[r][:, 0:ST * D].rearrange("p (t d) -> p t d", d=D)
        s_dve, s_x, s_xt_p, s_xt, s_hid_p, s_hid, s_v, s_val, s_ph, s_u, s_fold, s_phi, s_sc, s_sm, s_out, s_sums, s_root, s_spent = (
            sem(n) for n in ("dve", "x", "xtp", "xt", "hidp", "hid", "v", "val", "ph", "u", "fold", "phi", "sc", "sm", "out", "sums", "root", "spent"))
        block = ctx.enter_context(nc.Block())
        at = lambda n: bass.ds(n * ST, ST)
        by_half = lambda ap: ap.rearrange("p (b two) d -> p two b d", two=2)
        STAGES = 4

        @block.vector
        def _(dve):
            ch = Chain(dve, s_dve)
            v = nc.vector

            def do(ins):
                ch.step(ins)
                ch.settle()

            def step(slots, r):
                new, phases, scores, last = slots
                o = 1 - r
                if new is not None:
                    v.tensor_tensor(x[:, r], by_half(xc[:, at(new)]), by_half(spread(rstd[:, at(new)], D)), ALU.mult).then_inc(s_x, 1)
                if last is not None:
                    pause(dve, s_out, last + 1, s_spent)
                    do(v.tensor_tensor(ret[:, o].rearrange("p (b two) d -> p b two d", two=2), out_p(o).rearrange("p (b two) d -> p b two d", two=2),
                                       repeat(spread(C("rnorm"), D), SB), ALU.mult))
                    do(v.tensor_tensor(h[:, at(last)], h[:, at(last)], ret[:, o], ALU.add))
                    ln_sums(do, lambda: dve.sem_inc(s_spent, 1), v, mem, at(last), sq[:, o])
                if phases is not None:
                    pause(dve, s_v, phases + 1, s_spent)
                    v.tensor_tensor(val[:, o].rearrange("p two b d -> p (two b) d"), p_v[:, 0:ST * D].rearrange("p (t d) -> p t d", d=D),
                                    repeat(W("v_b"), ST), ALU.add).then_inc(s_val, 1)
                if scores is not None:
                    for b in range(SB):
                        pause(dve, s_sc, scores * SB + b + 1, s_spent)
                        v.tensor_tensor(sm[:, r, b], p_sc[b][:, 0:384], C("causal"), ALU.mult).then_inc(s_sm, 1)
                if phases is not None:
                    pause(dve, s_u, phases * 2 + 2, s_spent)
                    v.scalar_tensor_tensor(out=u[:, o], in0=u[:, o], scalar=C("fold"), in1=u[:, o], op0=ALU.mult, op1=ALU.max).then_inc(s_fold, 1)

            staggered(dve, step, STAGES, ch, 2 * (2 + LN_STEPS))
            ln_finish(nc, mem, dve, s_sums, s_root)

        @block.tensor
        def _(pe):
            def step(slots, r):
                new, phases, scores, _ = slots
                o = 1 - r
                if phases is not None:
                    pause(pe, s_xt, phases + 1, s_spent)
                    for kq in range(2):
                        pe.matmul(p_hid[:, kq], W("q_w1" if kq else "k_w1"), xt[:, o], start=True, stop=True).then_inc(s_hid_p, 1)
                    if scores is not None:
                        pause(pe, s_val, scores + 1, s_spent)
                    for half in range(2):
                        mm = pe.matmul(p_v[:, half * P:half * P + P], xt[:, o, half * P:half * P + P], W("v_w"), start=True, stop=True)
                    mm.then_inc(s_v, 1)
                if new is not None:
                    pause(pe, s_x, new + 1, s_spent)
                    for half in range(2):
                        mm = pe.transpose(p_xt[:, half * P:half * P + P], x[:, r, half].rearrange("p b d -> p (b d)"), C("ident"))
                    mm.then_inc(s_xt_p, 1)
                if phases is not None:
                    if scores is not None:
                        pause(pe, s_u, scores * 2 + 2, s_spent)
                    pause(pe, s_hid, phases * 2 + 2, s_spent)
                    for kq in range(2):
                        pe.matmul(p_ph[:, kq], W("q_w2" if kq else "k_w2"), hid[:, o, kq], start=True, stop=True).then_inc(s_ph, 1)
                if scores is not None:
                    if phases is None:
                        pause(pe, s_val, scores + 1, s_spent)
                    pause(pe, s_phi, scores + 1, s_spent)
                    for b in range(SB):
                        k, q = (phi[b * D:b * D + D, r, kq] for kq in range(2))
                        pe.matmul(p_sc[b][:, 0:256], k[:, 0:P], q, start=True, stop=True)
                        pe.matmul(p_sc[b][:, 256:384], k[:, P:T], q[:, P:T], start=True, stop=True).then_inc(s_sc, 1)
                    for b in range(SB):
                        pause(pe, s_sm, scores * SB + b + 1, s_spent)
                        pe.matmul(out_p(r)[:, 2 * b, :], sm[:, r, b, 0:P], val[:, r, 0, b, :], start=True, stop=True)
                        pe.matmul(out_p(r)[:, 2 * b + 1, :], sm[:, r, b, P:2 * P], val[:, r, 0, b, :], start=True, stop=False)
                        mm = pe.matmul(out_p(r)[:, 2 * b + 1, :], sm[:, r, b, 2 * P:3 * P], val[:, r, 1, b, :], start=False, stop=True)
                    mm.then_inc(s_out, 1)

            staggered(pe, step, STAGES)

        @block.scalar
        def _(act):
            a = nc.scalar

            def step(slots, r):
                new, phases, scores, _ = slots
                o = 1 - r
                if phases is not None:
                    pause(act, s_hid_p, phases * 2 + 2, s_spent)
                    for kq in range(2):
                        a.activation(hid[:, o, kq], p_hid[:, kq], ACT.Tanh, bias=W("q_b1" if kq else "k_b1")).then_inc(s_hid, 1)
                if new is not None:
                    pause(act, s_xt_p, new + 1, s_spent)
                    a.activation(xt[:, r], p_xt[:, 0:T], ACT.Copy).then_inc(s_xt, 1)
                if scores is not None:
                    pause(act, s_fold, scores + 1, s_spent)
                    a.activation(phi[:, r], u[:, r], ACT.Sin, scale=C("sin_scale"), bias=C("sin_bias")).then_inc(s_phi, 1)
                if phases is not None:
                    pause(act, s_ph, phases * 2 + 2, s_spent)
                    for kq in range(2):
                        a.activation(u[:, o, kq], p_ph[:, kq], ACT.Tanh, bias=W("q_b2" if kq else "k_b2")).then_inc(s_u, 1)

            staggered(act, step, STAGES)
            ln_root(nc, mem, act, s_sums, s_root)


CH = 32
CHUNKS = ALL_COLS // CH
OH = 16


def node_table(nc, mem, table_dram):
    xc, rstd, C, W = mem["xc"], mem["rstd"], mem["C"], mem["W"]
    with ExitStack() as ctx:
        sb = lambda name, shape, dt: ctx.enter_context(nc.sbuf_tensor(name, shape, dt))
        sem = lambda name: ctx.enter_context(nc.semaphore("nt_" + name))
        x = sb("nt_x", [P, 2, GT, D], F32)
        xt = sb("nt_xt", [D, 2, GT * P], F32)
        tab = sb("nt_tab", [P, TILES, ROW], F32)
        att = sb("nt_att", [P, 2, TILES, 16], F32)
        p_xt = ctx.enter_context(nc.psum_tensor("nt_pxt", [D, 2, GT * P], F32))
        p_h = ctx.enter_context(nc.psum_tensor("nt_ph", [P, 2, 512], F32))
        s_x, s_xt_p, s_xt, s_h_p, s_h, s_dve, s_tab, s_out, s_spent = (sem(n) for n in ("x", "xtp", "xt", "hp", "h", "dve", "tab", "out", "spent"))
        block = ctx.enter_context(nc.Block())

        @block.vector
        def _(dve):
            v = nc.vector
            with dve.Fori(0, GROUPS // 2) as i:
                for r in range(2):
                    pause(dve, s_xt_p, i * 2 + r + 1, s_spent)
                    v.tensor_tensor(x[:, r], xc[:, bass.ds((i * 2 + r) * GT, GT)], spread(rstd[:, bass.ds((i * 2 + r) * GT, GT)], D), ALU.mult).then_inc(s_x, 1)
            ch = Chain(dve, s_dve)
            dve.wait_ge(s_h, GROUPS + 2)
            for n, name in enumerate(("att_src", "att_dst")):
                ch.step(v.tensor_tensor(att[:, n], tab[:, :, 0:16], repeat(W(name), TILES), ALU.mult))
            ch.settle()
            for n in range(2):
                v.tensor_reduce(tab[:, :, 16 + 4 * n:20 + 4 * n], att[:, n].rearrange("p t (h e) -> p t h e", e=EXPERTS), AX.X, ALU.add).then_inc(s_tab, 1)

        @block.tensor
        def _(pe):
            pe.sem_inc(s_xt_p, 2)
            pe.sem_inc(s_h, 2)
            with pe.Fori(0, GROUPS // 2) as i:
                for r in range(2):
                    pause(pe, s_x, i * 2 + r + 1, s_spent)
                    pause(pe, s_h, i * 2 + r + 1, s_spent)
                    for t in range(GT):
                        mm = pe.transpose(p_xt[:, r, t * P:t * P + P], x[:, r, t, :], C("ident"))
                    mm.then_inc(s_xt_p, 1)
                    pause(pe, s_xt, i * 2 + r + 1, s_spent)
                    for t in range(GT):
                        mm = pe.matmul(p_h[:, r, t * 16:t * 16 + 16], xt[:, r, t * P:t * P + P], W("w_gat")[0:D], start=True, stop=True)
                    mm.then_inc(s_h_p, 1)

        @block.scalar
        def _(act):
            with act.Fori(0, GROUPS // 2) as i:
                for r in range(2):
                    pause(act, s_xt_p, i * 2 + r + 3, s_spent)
                    nc.scalar.activation(xt[:, r], p_xt[:, r], ACT.Copy).then_inc(s_xt, 1)
                    pause(act, s_h_p, i * 2 + r + 1, s_spent)
                    nc.scalar.activation(tab[:, bass.ds((i * 2 + r) * GT, GT), 0:16], p_h[:, r, 0:GT * 16].rearrange("p (t f) -> p t f", f=16), ACT.Copy).then_inc(s_h, 1)

        @block.sync
        def _(sp):
            sp.wait_ge(s_tab, 2)
            sp.dma_start(table_dram.rearrange("(t p) r -> p t r", p=P), tab[:]).then_inc(s_out, 16)
            sp.wait_ge(s_out, 16)


def edge_stream(nc, mem, sorted_keys, table_dram, state_dram, y_dram):
    C = mem["C"]
    with ExitStack() as ctx:
        sb = lambda name, shape, dt: ctx.enter_context(nc.sbuf_tensor(name, shape, dt))
        sem = lambda name: ctx.enter_context(nc.semaphore("es_" + name))
        key = sb("es_key", [P, ALL_COLS], I32)
        src = sb("es_src", [P, ALL_COLS], I32)
        tmp = sb("es_tmp", [P, ALL_COLS], I32)
        keep = sb("es_keep", [P, ALL_COLS], F32)
        starts = tmp[:].bitcast(F32)
        drop = key[:].bitcast(F32)
        hi = sb("es_hi", [P, ALL_COLS], BF16)
        lo = sb("es_lo", [P, ALL_COLS], BF16)
        iota = sb("es_iota", [P, P], BF16)
        hot = sb("es_hot", [P, 2, 2, OH, P], BF16)
        now = sb("es_now", [P, 2, CH], I32)
        row0 = sb("es_row0", [P, ROW], F32)
        got = sb("es_got", [P, 2, CH, ROW], F32)
        a_self = sb("es_aself", [P, 4, CH], F32)
        a_dst = sb("es_adst", [P, 2, 4, CH], F32)
        e = sb("es_e", [P, 4, CH], F32)
        diff = sb("es_diff", [P, 2, CH, 4], F32)
        ex = sb("es_ex", [P, 2, CH, 4], F32)
        msg = sb("es_msg", [P, CH, 16], F32)
        st = sb("es_st", [P, 2, CH + 1, ROW], F32)
        counts = ctx.enter_context(nc.psum_tensor("es_counts", [P, P], F32))
        x, xt = sb("ex_x", [P, ST, D], F32), sb("ex_xt", [D, SN], F32)
        hid, y = sb("ex_hid", [P, 2, SN], F32), sb("ex_y", [P, ST, EXPERTS * D], F32)
        ps = lambda name, shape: ctx.enter_context(nc.psum_tensor("ex_" + name, shape, F32))
        p_xt, p_y = ps("pxt", [D, SN]), ps("py", [P, ST, EXPERTS * D])
        p_hid = [ps("phid0", [P, SN]), ps("phid1", [P, SN])]
        s_x, s_xt_p, s_xt, s_hid_p, s_hid, s_y_p, s_y, s_y_out = (sem(n) for n in ("x", "xtp", "xt", "hidp", "hid", "yp", "y", "yout"))
        C, W, xc, rstd = mem["C"], mem["W"], mem["xc"], mem["rstd"]
        SLOTS = TILES // ST
        s_keys, s_dve, s_pool, s_src, s_row0, s_diff, s_ex, s_state, s_stored0, s_stored1, s_spent, s_hot, s_used = (
            sem(n) for n in ("keys", "dve", "pool", "src", "row0", "diff", "ex", "state", "stored0", "stored1", "spent", "hot", "used"))
        s_landed, s_free, s_stored = [sem("landed0"), sem("landed1")], [sem("free0"), sem("free1")], [s_stored0, s_stored1]
        block = ctx.enter_context(nc.Block())
        HOTS = CH // OH

        @block.sync
        def _(sp):
            sp.dma_start(key[:], sorted_keys.rearrange("(p c) -> p c", p=P).bitcast(I32)).then_inc(s_keys, 16)
            states = state_dram.rearrange("(p c) r -> p c r", p=P)
            for r in range(2):
                sp.sem_inc(s_stored[r], 16)
            sp.sem_inc(s_y_out, 16)

            def turn(i, with_experts):
                for r in range(2):
                    pause(sp, s_state, i * 2 + r + 1, s_spent)
                    sp.dma_start(states[:, bass.ds((i * 2 + r) * CH, CH), :], st[:, r, 1:, :]).then_inc(s_stored[r], 16)
                    if r == 0 and with_experts:
                        pause(sp, s_y, i + 2, s_spent)
                        sp.dma_start(y_dram.rearrange("(s t p) f -> s p t f", p=P, t=ST)[bass.ds(i, 1)].rearrange("s p t f -> (s p) t f"), y[:]).then_inc(s_y_out, 16)

            with sp.Fori(0, SLOTS) as i:
                turn(i, True)
            with sp.Fori(SLOTS, CHUNKS // 2) as i:
                turn(i, False)
            sp.wait_ge(s_y_out, 16 * (SLOTS + 1))
            for r in range(2):
                sp.wait_ge(s_stored[r], 16 * (CHUNKS // 2 + 1))

        @block.gpsimd
        def _(pool):
            pool.wait_ge(s_src, 1)
            pool.indirect_dma_start(out=row0[:], out_offset=None, in_=table_dram,
                                    in_offset=bass.IndirectOffsetOnAxis(ap=mem["first"][:, 0:1].bitcast(U32), axis=0)).then_inc(s_row0, 16)
            for r in range(2):
                pool.sem_inc(s_free[r], 1)
            with pool.Fori(0, CHUNKS // 2) as i:
                for r in range(2):
                    pause(pool, s_free[r], i + 1, s_spent)
                    nc.gpsimd.tensor_copy(now[:, r, :], src[:, bass.ds((i * 2 + r) * CH, CH)]).then_inc(s_pool, 1)
                    pause(pool, s_pool, i * 2 + r + 1, s_spent)
                    for k in range(CH):
                        pool.indirect_dma_start(out=got[:, r, k, :], out_offset=None, in_=table_dram,
                                                in_offset=bass.IndirectOffsetOnAxis(ap=now[:, r, k:k + 1].bitcast(U32), axis=0)).then_inc(s_landed[r], 16)

        @block.scalar
        def _(act):
            def turn(i, with_experts):
                for r in range(2):
                    pause(act, s_diff, i * 2 + r + 1, s_spent)
                    nc.scalar.activation(ex[:], diff[:], ACT.Exp).then_inc(s_ex, 1)
                    if r == 0 and with_experts:
                        pause(act, s_xt_p, i + 1, s_spent)
                        nc.scalar.activation(xt[:], p_xt[:], ACT.Copy).then_inc(s_xt, 1)
                        for e in range(EXPERTS):
                            pause(act, s_hid_p, i * EXPERTS + e + 1, s_spent)
                            if e >= 2:
                                pause(act, s_y_p, i * EXPERTS + e - 1, s_spent)
                            nc.scalar.activation(hid[:, e % 2], p_hid[e % 2][:], ACT.Gelu, bias=W("e_b1")[:, e:e + 1]).then_inc(s_hid, 1)
                        pause(act, s_y_p, i * EXPERTS + EXPERTS, s_spent)
                        pause(act, s_y_out, i * 16 + 16, s_spent)
                        nc.scalar.activation(y[:], p_y[:], ACT.Copy).then_inc(s_y, 1)

            with act.Fori(0, SLOTS) as i:
                turn(i, True)
            with act.Fori(SLOTS, CHUNKS // 2) as i:
                turn(i, False)

        @block.tensor
        def _(pe):
            pe.wait_ge(s_src, 1)
            pe.matmul(counts[:], hot[:, 0, 0, 0, :], hot[:, 0, 1, 0, :], start=True, stop=False, skip_group_check=True).then_inc(s_used, 2)

            def expert(i, e):
                pe.matmul(p_hid[e % 2][:], W("e_w1")[0:D, e * HID:e * HID + HID], xt[:], start=True, stop=True).then_inc(s_hid_p, 1)

            def turn(i, with_experts):
                for n in range(2 * HOTS):
                    pause(pe, s_hot, i * (2 * HOTS) + n + 1, s_spent)
                    for k in range(OH):
                        mm = pe.matmul(counts[:], hot[:, n % 2, 0, k, :], hot[:, n % 2, 1, k, :], start=False, stop=False, skip_group_check=True)
                    mm.then_inc(s_used, 1)
                    if n == 0 and with_experts:
                        pause(pe, s_x, i + 1, s_spent)
                        for t in range(ST):
                            mm = pe.transpose(p_xt[:, t * P:t * P + P], x[:, t, :], C("ident"))
                        mm.then_inc(s_xt_p, 1)
                        pause(pe, s_xt, i + 1, s_spent)
                        expert(i, 0)
                        expert(i, 1)
                        pause(pe, s_y, i + 1, s_spent)
                        for t in range(ST):
                            pe.matmul(p_y[:, t, :], C("ones_row")[0:1], W("e_b2")[0:1], start=(t % 2 == 0), stop=False, skip_group_check=True)
                        for e in range(EXPERTS):
                            pause(pe, s_hid, i * EXPERTS + e + 1, s_spent)
                            for t in range(ST):
                                mm = pe.matmul(p_y[:, t, e * D:e * D + D], hid[:, e % 2, t * P:t * P + P], W("e_w2")[:, e * D:e * D + D], start=False, stop=True, skip_group_check=True)
                            mm.then_inc(s_y_p, 1)
                            if e + 2 < EXPERTS:
                                expert(i, e + 2)

            pe.sem_inc(s_y, 1)
            with pe.Fori(0, SLOTS) as i:
                turn(i, True)
            with pe.Fori(SLOTS, CHUNKS // 2) as i:
                turn(i, False)
            pe.matmul(counts[:], hot[:, 0, 0, 0, :], mem["zeros"][:], start=False, stop=True, skip_group_check=True).then_inc(s_used, 1)

        @block.vector
        def _(dve):
            ch = Chain(dve, s_dve)
            v = nc.vector
            dve.wait_ge(s_keys, 16)
            ch.step(v.tensor_scalar(src[:], key[:], M - 1, None, ALU.bitwise_and))
            ch.step(v.tensor_scalar(mem["first"][:], key[:, 0:1], 15, M - 1, ALU.logical_shift_right, ALU.bitwise_and))
            ch.step(v.tensor_copy(iota[:], C("iota")))
            ch.step(v.memset(mem["zeros"][:], 0.0))
            ch.step(v.memset(hot[:, 0, :, 0, :], 0.0))
            ch.settle()
            dve.sem_inc(s_src, 1)
            for to, shift in ((hi, 22), (lo, 15)):
                ch.step(v.tensor_scalar(tmp[:], key[:], shift, P - 1, ALU.logical_shift_right, ALU.bitwise_and)); ch.settle()
                ch.step(v.tensor_copy(to[:], tmp[:])); ch.settle()
            ch.step(v.tensor_scalar(tmp[:], key[:], 14, 1, ALU.logical_shift_right, ALU.bitwise_and)); ch.settle()
            ch.step(v.tensor_copy(keep[:], tmp[:])); ch.settle()
            ch.step(v.tensor_scalar(starts, keep[:], -1.0, 1.0, ALU.mult, ALU.add)); ch.settle()
            ch.step(v.tensor_scalar(drop, starts, -BIG, None, ALU.mult))
            ch.step(v.tensor_reduce(mem["has_start"][:], starts, AX.X, ALU.max))
            ch.step(v.tensor_copy(mem["first_keep"][:], keep[:, 0:1]))
            ch.step(v.memset(st[:, 1, CH, 0:4], -BIG))
            ch.step(v.memset(st[:, 1, CH, 4:ROW], 0.0))
            dve.wait_ge(s_row0, 16)
            ch.step(v.tensor_copy(a_dst[:, 1, :, CH - 1], row0[:, 20:24]))
            ch.settle()
            def turn(i, with_experts):
                if with_experts:
                    g = bass.ds(i * ST, ST)
                    v.tensor_tensor(x[:], xc[:, g], spread(rstd[:, g], D), ALU.mult).then_inc(s_x, 1)
                for r in range(2):
                    cols = bass.ds((i * 2 + r) * CH, CH)
                    for n in range(HOTS):
                        at = bass.ds((i * 2 + r) * CH + n * OH, OH)
                        pause(dve, s_used, (i * 2 + r) * HOTS + n + 1, s_spent)
                        v.tensor_tensor(hot[:, n % 2, 0], repeat(iota[:], OH), spread(hi[:, at], P), ALU.is_equal)
                        v.tensor_tensor(hot[:, n % 2, 1], repeat(iota[:], OH), spread(lo[:, at], P), ALU.is_equal).then_inc(s_hot, 1)
                    pause(dve, s_landed[r], (i + 1) * (16 * CH), s_spent)
                    g = got[:, r]
                    ch.step(v.tensor_tensor(a_self[:], g[:, :, 20:24].rearrange("p c k -> p k c"), repeat(starts[:, cols], 4), ALU.mult)); ch.settle()
                    for k in range(4):
                        ch.step(v.tensor_tensor_scan(a_dst[:, r, k], keep[:, cols], a_self[:, k], a_dst[:, 1 - r, k, CH - 1:CH], ALU.mult, ALU.add))
                    ch.settle()
                    ch.step(v.tensor_tensor(e[:], g[:, :, 16:20].rearrange("p c k -> p k c"), a_dst[:, r], ALU.add)); ch.settle()
                    ch.step(v.scalar_tensor_tensor(out=e[:], in0=e[:], scalar=0.2, in1=e[:], op0=ALU.mult, op1=ALU.max)); ch.settle()
                    pause(dve, s_stored[r], (i + 1) * 16, s_spent)
                    ch.step(v.tensor_copy(st[:, r, 0, :], st[:, 1 - r, CH, :]))
                    ch.settle()
                    for k in range(4):
                        ch.step(v.tensor_tensor_scan(st[:, r, 1:, k], drop[:, cols], e[:, k], st[:, r, 0, k:k + 1], ALU.add, ALU.max))
                    ch.settle()
                    ch.step(v.tensor_tensor(diff[:, 0], st[:, r, 0:CH, 0:4], st[:, r, 1:, 0:4], ALU.subtract))
                    ch.step(v.tensor_tensor(diff[:, 1], e[:].rearrange("p k c -> p c k"), st[:, r, 1:, 0:4], ALU.subtract))
                    ch.settle()
                    v.tensor_tensor(diff[:, 0], diff[:, 0], spread(drop[:, cols], 4), ALU.add).then_inc(s_diff, 1)
                    pause(dve, s_ex, i * 2 + r + 1, s_spent)
                    for k in range(4):
                        ch.step(v.tensor_tensor_scan(st[:, r, 1:, 4 + k], ex[:, 0, :, k], ex[:, 1, :, k], st[:, r, 0, 4 + k:5 + k], ALU.mult, ALU.add))
                    for k in range(4):
                        ch.step(v.tensor_tensor(msg[:, :, 4 * k:4 * k + 4], g[:, :, 4 * k:4 * k + 4], spread(ex[:, 1, :, k], 4), ALU.mult))
                    ch.settle()
                    dve.sem_inc(s_free[r], 1)
                    for j in range(16):
                        ch.step(v.tensor_tensor_scan(st[:, r, 1:, 8 + j], ex[:, 0, :, j // 4], msg[:, :, j], st[:, r, 0, 8 + j:9 + j], ALU.mult, ALU.add))
                    ch.settle()
                    dve.sem_inc(s_state, 1)

            PER = 2 * 38
            with dve.Fori(0, SLOTS) as i:
                ch.turn(i, PER)
                turn(i, True)
            with dve.Fori(SLOTS, CHUNKS // 2) as i:
                ch.resume(i)
                turn(i, False)
            ch.end(CHUNKS // 2)
            ch.step(v.tensor_copy(mem["last"][:], st[:, 1, CH, :]))
            dve.wait_ge(s_used, 2 + CHUNKS * HOTS + 1)
            ch.step(v.tensor_copy(mem["counts"][:], counts[:]))
            ch.settle()


def join_runs(nc, mem, state_dram, end_dram):
    C = mem["C"]
    with ExitStack() as ctx:
        sb = lambda name, shape, dt: ctx.enter_context(nc.sbuf_tensor("jr_" + name, shape, dt))
        ps = lambda name, shape: ctx.enter_context(nc.psum_tensor("jr_" + name, shape, F32))
        sem = lambda name: ctx.enter_context(nc.semaphore("jr_" + name))
        total, prefix, end_f, end_i = sb("total", [P, 1], F32), sb("prefix", [P, 1], F32), sb("endf", [P, P], F32), sb("endi", [P, P], I32)
        pos, pos_f, bad, to, row = sb("pos", [P, 1], I32), sb("posf", [P, 1], F32), sb("bad", [P, 1], F32), sb("to", [P, 1], I32), sb("row", [P, ROW], F32)
        wide = sb("wide", [P, 4, 16], F32)
        tr = sb("tr", [16, 4, P], F32)
        car = sb("car", [16, 3, P + 1], F32)
        df = sb("df", [16, 2, P], F32)
        fx = sb("fx", [16, 2, P], F32)
        ws = sb("ws", [16, 2, P], F32)
        cin = sb("cin", [P, 3, 16], F32)
        mine = sb("mine", [P, 3, 16], F32)
        d2, x2, mix, mix2, new = sb("d2", [P, 2, 16], F32), sb("x2", [P, 2, 16], F32), sb("mix", [P, 2, 16], F32), sb("mix2", [P, 2, 16], F32), sb("new", [P, ROW], F32)
        m16 = sb("m16", [P, 16], F32)
        p_pre, p_tr, p_back, p_end = ps("ppre", [P, 1]), ps("ptr", [16, 4, P]), ps("pback", [P, 3, 16]), ps("pend", [P, P])
        s_dve, s_total, s_pre, s_end, s_end_t, s_endd, s_pos, s_posok, s_row, s_wide, s_tr, s_ex, s_exd, s_car, s_back, s_ex2, s_ex2d, s_new, s_scat = (
            sem(n) for n in ("dve", "total", "pre", "end", "endt", "endd", "pos", "posok", "row", "wide", "tr", "ex", "exd", "car", "back", "ex2", "ex2d", "new", "scat"))
        block = ctx.enter_context(nc.Block())

        @block.vector
        def _(dve):
            ch = Chain(dve, s_dve)
            v = nc.vector
            counts = mem["counts"]
            v.tensor_reduce(total[:], counts[:], AX.X, ALU.add).then_inc(s_total, 1)
            dve.wait_ge(s_pre, 1)
            ch.step(v.tensor_copy(prefix[:], p_pre[:])); ch.settle()
            ch.step(v.tensor_scalar(prefix[:], prefix[:], -1.0, None, ALU.add)); ch.settle()
            ch.step(v.memset(end_f[:], 1.0)); ch.settle()
            ch.step(v.tensor_tensor_scan(end_f[:], end_f[:], counts[:], prefix[:], ALU.mult, ALU.add)); ch.settle()
            v.tensor_copy(end_i[:], end_f[:]).then_inc(s_end, 1)
            dve.wait_ge(s_end_t, 1)
            ch.step(v.tensor_copy(mem["node_end"][:], p_end[:]))
            last = mem["last"]
            ch.step(v.tensor_copy(wide[:, 0].rearrange("p (h e) -> p h e", e=4), spread(last[:, 0:4], 4)))
            ch.step(v.tensor_copy(wide[:, 1].rearrange("p (h e) -> p h e", e=4), spread(last[:, 4:8], 4)))
            ch.step(v.tensor_copy(wide[:, 2], last[:, 8:24]))
            ch.step(v.tensor_copy(wide[:, 3], mem["has_start"][:, 0:1].broadcast_to([P, 16]))); ch.settle()
            dve.sem_inc(s_wide, 1)
            dve.wait_ge(s_tr, 1)
            ch.step(v.tensor_copy(tr[:], p_tr[:]))
            ch.step(v.memset(car[:, 0, 0:1], -BIG))
            ch.step(v.memset(car[:, 1:, 0:1], 0.0)); ch.settle()
            ch.step(v.tensor_scalar(tr[:, 3], tr[:, 3], -BIG, None, ALU.mult)); ch.settle()
            ch.step(v.tensor_tensor_scan(car[:, 0, 1:], tr[:, 3], tr[:, 0], car[:, 0, 0:1], ALU.add, ALU.max)); ch.settle()
            ch.step(v.tensor_tensor(df[:, 0], car[:, 0, 0:P], car[:, 0, 1:], ALU.subtract))
            ch.step(v.tensor_tensor(df[:, 1], tr[:, 0], car[:, 0, 1:], ALU.subtract)); ch.settle()
            v.tensor_tensor(df[:, 0], df[:, 0], tr[:, 3], ALU.add).then_inc(s_ex, 1)
            dve.wait_ge(s_exd, 1)
            for k in range(2):
                ch.step(v.tensor_tensor(ws[:, k], fx[:, 1], tr[:, 1 + k], ALU.mult))
            ch.settle()
            for k in range(2):
                ch.step(v.tensor_tensor_scan(car[:, 1 + k, 1:], fx[:, 0], ws[:, k], car[:, 1 + k, 0:1], ALU.mult, ALU.add))
            ch.settle()
            dve.sem_inc(s_car, 1)
            dve.wait_ge(s_pos, 16)
            ch.step(v.tensor_copy(pos_f[:], pos[:])); ch.settle()
            ch.step(v.tensor_tensor(bad[:], pos_f[:], C("slice_end"), ALU.is_ge)); ch.settle()
            ch.step(v.tensor_tensor(bad[:], bad[:], mem["first_keep"][:], ALU.is_ge)); ch.settle()
            ch.step(v.scalar_tensor_tensor(out=pos_f[:], in0=bad[:], scalar=float(1 << 20), in1=pos_f[:], op0=ALU.mult, op1=ALU.add)); ch.settle()
            ch.step(v.tensor_copy(to[:], pos_f[:]))
            dve.wait_ge(s_back, 1)
            ch.step(v.tensor_copy(cin[:], p_back[:]))
            dve.wait_ge(s_row, 16)
            for k in range(2):
                ch.step(v.tensor_copy(mine[:, k].rearrange("p (h e) -> p h e", e=4), spread(row[:, 4 * k:4 * k + 4], 4)))
            ch.step(v.tensor_copy(mine[:, 2], row[:, 8:24])); ch.settle()
            ch.step(v.tensor_tensor(m16[:], cin[:, 0], mine[:, 0], ALU.max)); ch.settle()
            ch.step(v.tensor_tensor(d2[:, 0], cin[:, 0], m16[:], ALU.subtract))
            ch.step(v.tensor_tensor(d2[:, 1], mine[:, 0], m16[:], ALU.subtract)); ch.settle()
            dve.sem_inc(s_ex2, 1)
            dve.wait_ge(s_ex2d, 1)
            ch.step(v.tensor_tensor(mix[:], cin[:, 1:], repeat(x2[:, 0], 2), ALU.mult))
            ch.step(v.tensor_tensor(mix2[:], mine[:, 1:], repeat(x2[:, 1], 2), ALU.mult)); ch.settle()
            ch.step(v.tensor_tensor(mix[:], mix[:], mix2[:], ALU.add)); ch.settle()
            ch.step(v.tensor_copy(new[:, 0:4], m16[:].rearrange("p (h e) -> p h e", e=4)[:, :, 0]))
            ch.step(v.tensor_copy(new[:, 4:8], mix[:, 0].rearrange("p (h e) -> p h e", e=4)[:, :, 0]))
            ch.step(v.tensor_copy(new[:, 8:24], mix[:, 1])); ch.settle()
            dve.sem_inc(s_new, 1)

        @block.tensor
        def _(pe):
            pe.wait_ge(s_total, 1)
            pe.matmul(p_pre[:], C("before"), total[:], start=True, stop=True).then_inc(s_pre, 1)
            pe.wait_ge(s_end, 1)
            pe.transpose(p_end[:], end_f[:], C("ident")).then_inc(s_end_t, 1)
            pe.wait_ge(s_wide, 1)
            for k in range(4):
                mm = pe.transpose(p_tr[:, k], wide[:, k], C("ident"))
            mm.then_inc(s_tr, 1)
            pe.wait_ge(s_car, 1)
            for k in range(3):
                mm = pe.transpose(p_back[:, k], car[:, k, 0:P], C("ident")[0:16, 0:16])
            mm.then_inc(s_back, 1)

        @block.scalar
        def _(act):
            act.wait_ge(s_ex, 1)
            nc.scalar.activation(fx[:], df[:], ACT.Exp).then_inc(s_exd, 1)
            act.wait_ge(s_ex2, 1)
            nc.scalar.activation(x2[:], d2[:], ACT.Exp).then_inc(s_ex2d, 1)

        @block.gpsimd
        def _(pool):
            pool.wait_ge(s_end, 1)
            pool.dma_start(end_dram.rearrange("(p c) one -> p (c one)", p=P), end_i[:].bitcast(F32)).then_inc(s_endd, 16)
            pool.wait_ge(s_endd, 16)
            at = lambda t: bass.IndirectOffsetOnAxis(ap=t[:, 0:1].bitcast(U32), axis=0)
            pool.indirect_dma_start(out=pos[:].bitcast(F32), out_offset=None, in_=end_dram, in_offset=at(mem["first"])).then_inc(s_pos, 16)
            pool.wait_ge(s_pos, 16)
            pool.indirect_dma_start(out=row[:], out_offset=None, in_=state_dram, in_offset=at(pos)).then_inc(s_row, 16)
            pool.wait_ge(s_new, 1)
            pool.indirect_dma_start(out=state_dram, out_offset=at(to), in_=new[:], in_offset=None,
                                    bounds_check=EDGES + M - 1, oob_is_err=False).then_inc(s_scat, 16)
            pool.wait_ge(s_scat, 16)


def gate(nc, mem, state_dram, gates):
    C, W = mem["C"], mem["W"]
    RG = 16
    with ExitStack() as ctx:
        sb = lambda name, shape, dt: ctx.enter_context(nc.sbuf_tensor("gt_" + name, shape, dt))
        sem = lambda name: ctx.enter_context(nc.semaphore("gt_" + name))
        now = sb("now", [P, 2, RG], I32)
        ring = sb("ring", [P, 2, RG, ROW], F32)
        ns = sb("ns", [P, TILES, ROW], F32)
        den = sb("den", [P, TILES, 4], F32)
        agg, sq = sb("agg", [P, TILES, 16], F32), sb("sq", [P, TILES, 16], F32)
        mu, sd = sb("mu", [P, TILES], F32), sb("sd", [P, TILES], F32)
        sc = sb("sc", [P, TILES, 4], F32)
        best = sb("best", [P, 2, TILES], F32)
        pick = sb("pick", [P, 2, 4, TILES], F32)
        found, t, w1 = sb("found", [P, TILES], F32), sb("t", [P, TILES], F32), sb("w1", [P, 2, TILES], F32)
        s_pool, s_spent, s_dve, s_ns, s_var, s_std, s_t, s_exp = (sem(n) for n in ("pool", "spent", "dve", "ns", "var", "std", "t", "exp"))
        s_landed, s_free = [sem("landed0"), sem("landed1")], [sem("free0"), sem("free1")]
        block = ctx.enter_context(nc.Block())

        @block.gpsimd
        def _(pool):
            for r in range(2):
                pool.sem_inc(s_free[r], 1)
            with pool.Fori(0, TILES // RG // 2) as i:
                for r in range(2):
                    pause(pool, s_free[r], i + 1, s_spent)
                    nc.gpsimd.tensor_copy(now[:, r], mem["node_end"][:, bass.ds((i * 2 + r) * RG, RG)]).then_inc(s_pool, 1)
                    pause(pool, s_pool, i * 2 + r + 1, s_spent)
                    for k in range(RG):
                        pool.indirect_dma_start(out=ring[:, r, k, :], out_offset=None, in_=state_dram,
                                                in_offset=bass.IndirectOffsetOnAxis(ap=now[:, r, k:k + 1].bitcast(U32), axis=0)).then_inc(s_landed[r], 16)

        @block.scalar
        def _(act):
            with act.Fori(0, TILES // RG // 2) as i:
                for r in range(2):
                    pause(act, s_landed[r], (i + 1) * (16 * RG), s_spent)
                    nc.scalar.activation(ns[:, bass.ds((i * 2 + r) * RG, RG), :], ring[:, r], ACT.Copy).then_inc(s_free[r], 1)
            act.wait_ge(s_var, 1)
            nc.scalar.activation(sd[:], sd[:], ACT.Sqrt, scale=1.0 / 16, bias=C("eps")).then_inc(s_std, 1)
            act.wait_ge(s_t, 1)
            nc.scalar.activation(t[:], t[:], ACT.Exp).then_inc(s_exp, 1)

        @block.vector
        def _(dve):
            ch = Chain(dve, s_dve)
            v = nc.vector

            def do(ins):
                ch.step(ins)
                ch.settle()

            for r in range(2):
                dve.wait_ge(s_free[r], 1 + TILES // RG // 2)
            four = lambda a: a.rearrange("p t (h e) -> p t h e", e=4)
            do(v.tensor_scalar(den[:], ns[:, :, 4:8], 1e-16, None, ALU.add))
            do(v.reciprocal(den[:], den[:]))
            do(v.tensor_tensor(four(agg[:]), four(ns[:, :, 8:24]), spread(den[:], 4), ALU.mult))
            do(v.tensor_tensor(agg[:], agg[:], repeat(W("b_gat"), TILES), ALU.add))
            do(v.tensor_reduce(mu[:], agg[:], AX.X, ALU.add))
            do(v.tensor_scalar(mu[:], mu[:], 1.0 / 16, None, ALU.mult))
            do(v.tensor_tensor(agg[:], agg[:], spread(mu[:], 16), ALU.subtract))
            do(v.tensor_tensor(sq[:], agg[:], agg[:], ALU.mult))
            v.tensor_reduce(sd[:], sq[:], AX.X, ALU.add).then_inc(s_var, 1)
            dve.wait_ge(s_std, 1)
            do(v.reciprocal(sd[:], sd[:]))
            do(v.tensor_tensor(agg[:], agg[:], spread(sd[:], 16), ALU.mult))
            do(v.tensor_tensor(agg[:], agg[:], repeat(W("gamma"), TILES), ALU.mult))
            do(v.tensor_tensor(agg[:], agg[:], repeat(W("beta"), TILES), ALU.add))
            do(v.tensor_reduce(sc[:], agg[:].rearrange("p t (h e) -> p t e h", e=4), AX.X, ALU.add))
            do(v.tensor_scalar(sc[:], sc[:], 0.25, None, ALU.mult))
            for n in range(2):
                do(v.tensor_reduce(best[:, n], sc[:], AX.X, ALU.max))
                for ex in range(4):
                    do(v.tensor_tensor(pick[:, n, ex], sc[:, :, ex], best[:, n], ALU.is_equal))
                do(v.tensor_copy(found[:], pick[:, n, 0]))
                for ex in range(1, 4):
                    do(v.tensor_tensor(w1[:, 0], pick[:, n, ex], found[:], ALU.is_gt))
                    do(v.tensor_tensor(found[:], found[:], pick[:, n, ex], ALU.max))
                    do(v.tensor_copy(pick[:, n, ex], w1[:, 0]))
                if n == 0:
                    do(v.scalar_tensor_tensor(out=sc[:], in0=pick[:, 0].rearrange("p e t -> p t e"), scalar=-BIG, in1=sc[:], op0=ALU.mult, op1=ALU.add))
            v.tensor_tensor(t[:], best[:, 1], best[:, 0], ALU.subtract).then_inc(s_t, 1)
            dve.wait_ge(s_exp, 1)
            do(v.tensor_scalar(w1[:, 0], t[:], 1.0, None, ALU.add))
            do(v.reciprocal(w1[:, 0], w1[:, 0]))
            do(v.tensor_tensor(w1[:, 1], t[:], w1[:, 0], ALU.mult))
            for n in range(2):
                do(v.tensor_tensor(pick[:, n], pick[:, n], repeat(w1[:, n], 4), ALU.mult))
            do(v.tensor_tensor(gates[:], pick[:, 0].rearrange("p e t -> p t e"), pick[:, 1].rearrange("p e t -> p t e"), ALU.add))


def gated_sum(nc, mem, gates, y_dram):
    h = mem["h"]
    with ExitStack() as ctx:
        sb = lambda name, shape, dt: ctx.enter_context(nc.sbuf_tensor("gs_" + name, shape, dt))
        sem = lambda name: ctx.enter_context(nc.semaphore("gs_" + name))
        y = [sb("y%d" % r, [P, GT, EXPERTS, D], F32) for r in range(2)]
        total, sq = sb("total", [P, GT, D], F32), sb("sq", [P, GT, D], F32)
        s_dve, s_used, s_spent, s_sums, s_root = (sem(n) for n in ("dve", "used", "spent", "sums", "root"))
        s_y = [sem("y0"), sem("y1")]
        block = ctx.enter_context(nc.Block())

        @block.sync
        def _(sp):
            sp.sem_inc(s_used, 2)
            with sp.Fori(0, GROUPS // 2) as i:
                for r in range(2):
                    pause(sp, s_used, i * 2 + r + 1, s_spent)
                    sp.dma_start(y[r][:].rearrange("p t e d -> p t (e d)"),
                                 y_dram.rearrange("(s t p) f -> s p t f", p=P, t=GT)[bass.ds(i * 2 + r, 1)].rearrange("s p t f -> (s p) t f")).then_inc(s_y[r], 16)

        @block.vector
        def _(dve):
            ch = Chain(dve, s_dve)
            v = nc.vector

            def do(ins):
                ch.step(ins)
                ch.settle()

            with dve.Fori(0, GROUPS // 2) as i:
                ch.turn(i, 2 * (2 + LN_STEPS))
                for r in range(2):
                    g = bass.ds((i * 2 + r) * GT, GT)
                    pause(dve, s_y[r], (i + 1) * 16, s_spent)
                    do(v.tensor_tensor(y[r][:], y[r][:], spread(gates[:, g, :], D), ALU.mult))
                    v.tensor_reduce(total[:], y[r][:].rearrange("p t e d -> p t d e"), AX.X, ALU.add).then_inc(s_used, 1)
                    pause(dve, s_used, i * 2 + r + 3, s_spent)
                    do(v.tensor_tensor(h[:, g], h[:, g], total[:], ALU.add))
                    ln_sums(do, lambda: dve.sem_inc(s_spent, 1), v, mem, g, sq[:])
                ch.end(GROUPS // 2)
            ln_finish(nc, mem, dve, s_sums, s_root)

        @block.scalar
        def _(act):
            ln_root(nc, mem, act, s_sums, s_root)


def graph_experts(nc, mem, sorted_keys, table_dram, state_dram, end_dram, y_dram):
    with ExitStack() as ctx:
        sb = lambda name, shape, dt: ctx.enter_context(nc.sbuf_tensor(name, shape, dt))
        mem.update(zeros=sb("zeros", [P, P], BF16), first=sb("first", [P, 1], I32), has_start=sb("has_start", [P, 1], F32),
                   first_keep=sb("first_keep", [P, 1], F32), last=sb("last", [P, ROW], F32), counts=sb("counts", [P, P], F32),
                   node_end=sb("node_end", [P, TILES], I32))
        gates = sb("gates", [P, TILES, EXPERTS], F32)
        node_table(nc, mem, table_dram)
        edge_stream(nc, mem, sorted_keys, table_dram, state_dram, y_dram)
        join_runs(nc, mem, state_dram, end_dram)
        gate(nc, mem, state_dram, gates)
        gated_sum(nc, mem, gates, y_dram)


def head_attention(nc, mem):
    h, xc, rstd, C, W = mem["h"], mem["xc"], mem["rstd"], mem["C"], mem["W"]
    NG = SB * 2 * H1
    with ExitStack() as ctx:
        sb = lambda name, shape: ctx.enter_context(nc.sbuf_tensor("a1_" + name, shape, F32))
        ps = lambda name, shape: ctx.enter_context(nc.psum_tensor("a1_" + name, shape, F32))
        sem = lambda name: ctx.enter_context(nc.semaphore("a1_" + name))
        x, xt, qt, rt = sb("x", [P, 2, 2, SB, D]), sb("xt", [P, 2, T]), sb("qt", [P, 2, T]), sb("rt", [P, 2, T])
        kv, sq = sb("kv", [P, 2, 2 * NG, C1]), sb("sq", [P, 2 * NG, C1])
        mu, sd = sb("mu", [P, 2 * NG]), sb("sd", [P, 2 * NG])
        kvm = sb("kvm", [P, P])
        gj, sq_h = sb("gj", [P, 2, 2, SB, D]), sb("sqh", [P, ST, D])
        p_xt, p_q, p_kv, p_kvm, p_o, p_prj = (ps("p" + n, [P, 512]) for n in ("xt", "q", "kv", "kvm", "o", "prj"))
        s_x, s_hx, s_xt_p, s_xt, s_q_p, s_q, s_kv_p, s_cent, s_sq, s_var, s_std, s_norm, s_kv, s_kvm_p, s_kvm, s_o, s_rt, s_p, s_gj, s_dve, s_pool, s_sums, s_root, s_spent = (
            sem(n) for n in ("x", "hx", "xtp", "xt", "qp", "q", "kvp", "cent", "sq", "var", "std", "norm", "kv", "kvmp", "kvm", "o", "rt", "p", "gj", "dve", "pool", "sums", "root", "spent"))
        block = ctx.enter_context(nc.Block())
        at = lambda n: bass.ds(n * ST, ST)
        by_half = lambda ap: ap.rearrange("p (b two) d -> p two b d", two=2)
        groups = p_kv[:].rearrange("p (g c) -> p g c", c=C1)
        halves = lambda r: kv[:, r].rearrange("p (two g) c -> p two (g c)", two=2)
        STAGES = 4

        @block.vector
        def _(dve):
            ch = Chain(dve, s_dve)
            v = nc.vector

            def do(ins):
                ch.step(ins)
                ch.settle()

            def step(slots, r):
                new, qkv, products, last = slots
                o = 1 - r
                if products is not None:
                    pause(dve, s_hx, products + 1, s_spent)
                if new is not None:
                    v.tensor_tensor(x[:, r], by_half(xc[:, at(new)]), by_half(spread(rstd[:, at(new)], D)), ALU.mult).then_inc(s_x, 1)
                if last is not None:
                    pause(dve, s_gj, last + 1, s_spent)
                    do(v.tensor_tensor(by_half(h[:, at(last)]), by_half(h[:, at(last)]), gj[:, o], ALU.add))
                if qkv is not None:
                    pause(dve, s_kv_p, qkv + 1, s_spent)
                    do(v.tensor_reduce(mu[:], groups, AX.X, ALU.add))
                    v.scalar_tensor_tensor(out=kv[:, o], in0=spread(mu[:], C1), scalar=-1.0 / C1, in1=groups, op0=ALU.mult, op1=ALU.add).then_inc(s_cent, 1)
                if products is not None:
                    pause(dve, s_kvm_p, products + 1, s_spent)
                    v.tensor_tensor(kvm[:], p_kvm[:, 0:P], C("own_head"), ALU.mult).then_inc(s_kvm, 1)
                if qkv is not None:
                    pause(dve, s_sq, qkv + 1, s_spent)
                    v.tensor_reduce(sd[:], sq[:], AX.X, ALU.add).then_inc(s_var, 1)
                if products is not None:
                    pause(dve, s_o, products + 1, s_spent)
                    v.tensor_tensor(rt[:, r], p_o[:, 0:T], xt[:, r], ALU.add).then_inc(s_rt, 1)
                if last is not None:
                    ln_sums(do, lambda: dve.sem_inc(s_spent, 1), v, mem, at(last), sq_h[:])
                if qkv is not None:
                    pause(dve, s_std, qkv + 1, s_spent)
                    do(v.tensor_scalar(sd[:], sd[:], EPS, None, ALU.add))
                    do(v.reciprocal(sd[:], sd[:]))
                    v.tensor_tensor(kv[:, o], kv[:, o], spread(sd[:], C1), ALU.mult).then_inc(s_norm, 1)

            staggered(dve, step, STAGES, ch, 2 * (4 + LN_STEPS))
            ln_finish(nc, mem, dve, s_sums, s_root)

        @block.gpsimd
        def _(pool):
            def step(slots, r):
                new, qkv, _, _ = slots
                o = 1 - r
                if new is not None:
                    pause(pool, s_x, new + 1, s_spent)
                    nc.gpsimd.tensor_tensor(by_half(h[:, at(new)]), by_half(h[:, at(new)]), x[:, r], ALU.add).then_inc(s_hx, 1)
                if qkv is not None:
                    pause(pool, s_norm, qkv + 1, s_spent)
                    nc.gpsimd.tensor_tensor(halves(o), halves(o), repeat(W("kv_ln_w"), 2), ALU.mult).then_inc(s_pool, 1)
                    pause(pool, s_pool, qkv + 1, s_spent)
                    nc.gpsimd.tensor_tensor(halves(o), halves(o), repeat(W("kv_ln_b"), 2), ALU.add).then_inc(s_kv, 1)

            staggered(pool, step, STAGES)

        @block.tensor
        def _(pe):
            def step(slots, r):
                new, qkv, products, last = slots
                o = 1 - r
                if qkv is not None:
                    pause(pe, s_xt, qkv + 1, s_spent)
                    for half in range(2):
                        mm = pe.matmul(p_kv[:, half * T:half * T + T], xt[:, o, half * P:half * P + P], W("kv_w"), start=False, stop=(half == 1))
                    mm.then_inc(s_kv_p, 1)
                if products is not None:
                    pause(pe, s_q, products + 1, s_spent)
                if qkv is not None:
                    pe.matmul(p_q[:, 0:T], W("q_w"), xt[:, o], start=True, stop=True).then_inc(s_q_p, 1)
                if products is not None:
                    pause(pe, s_kv, products + 1, s_spent)
                    for half in range(2):
                        mm = pe.matmul(p_kvm[:, 0:P], halves(r)[:, half, 0:P], halves(r)[:, half, P:2 * P], start=(half == 0), stop=(half == 1))
                    mm.then_inc(s_kvm_p, 1)
                    pause(pe, s_kvm, products + 1, s_spent)
                    pe.matmul(p_o[:, 0:T], kvm[:], qt[:, r], start=True, stop=True).then_inc(s_o, 1)
                if new is not None:
                    pause(pe, s_x, new + 1, s_spent)
                    for half in range(2):
                        mm = pe.transpose(p_xt[:, half * P:half * P + P], x[:, r, half].rearrange("p b d -> p (b d)"), C("ident"))
                    mm.then_inc(s_xt_p, 1)
                if products is not None:
                    if last is not None:
                        pause(pe, s_gj, last + 1, s_spent)
                    pe.matmul(p_prj[:, 0:ST * D], C("ones_row")[0:1], repeat(W("proj_b")[0:1], ST), start=True, stop=False)
                    pause(pe, s_rt, products + 1, s_spent)
                    for half in range(2):
                        mm = pe.matmul(p_prj[:, half * P:half * P + P], rt[:, r, half * P:half * P + P], W("proj_w"), start=False, stop=(half == 1))
                    mm.then_inc(s_p, 1)
                if new is not None:
                    if qkv is not None:
                        pause(pe, s_cent, qkv + 1, s_spent)
                    pe.matmul(p_kv[:], C("ones_row")[0:1], repeat(W("kv_b")[0:1], 2), start=True, stop=False)

            staggered(pe, step, STAGES)

        @block.scalar
        def _(act):
            a = nc.scalar

            def step(slots, r):
                new, qkv, products, _ = slots
                o = 1 - r
                if qkv is not None:
                    pause(act, s_cent, qkv + 1, s_spent)
                    a.activation(sq[:], kv[:, o], ACT.Square).then_inc(s_sq, 1)
                    pause(act, s_q_p, qkv + 1, s_spent)
                    a.activation(qt[:, o], p_q[:, 0:T], ACT.Identity, bias=W("q_b")).then_inc(s_q, 1)
                    pause(act, s_var, qkv + 1, s_spent)
                    a.activation(sd[:], sd[:], ACT.Sqrt, scale=1.0 / (C1 - 1)).then_inc(s_std, 1)
                if products is not None:
                    pause(act, s_p, products + 1, s_spent)
                    a.activation(gj[:, r].rearrange("p two b d -> p (two b d)"), p_prj[:, 0:ST * D], ACT.Gelu).then_inc(s_gj, 1)
                if new is not None:
                    pause(act, s_xt_p, new + 1, s_spent)
                    a.activation(xt[:, r], p_xt[:, 0:T], ACT.Copy).then_inc(s_xt, 1)

            staggered(act, step, STAGES)
            ln_root(nc, mem, act, s_sums, s_root)


def route(nc, mem, route_dram):
    xc, rstd, C, W = mem["xc"], mem["rstd"], mem["C"], mem["W"]
    Q = TILES // 4
    with ExitStack() as ctx:
        sem = lambda name: ctx.enter_context(nc.semaphore("rt_" + name))
        prod = ctx.enter_context(nc.sbuf_tensor("rt_prod", [P, Q, D], F32))
        turned = ctx.enter_context(nc.sbuf_tensor("rt_turned", [P, P], F32))
        p_t = ctx.enter_context(nc.psum_tensor("rt_pt", [P, P], F32))
        s_dve, s_w, s_p, s_t, s_out = (sem(n) for n in ("dve", "w", "p", "t", "out"))
        block = ctx.enter_context(nc.Block())
        rw = mem["route"]

        @block.vector
        def _(dve):
            ch = Chain(dve, s_dve)
            v = nc.vector
            for q in range(4):
                t = slice(q * Q, q * Q + Q)
                ch.step(v.tensor_tensor(prod[:], xc[:, t], repeat(W("route_w"), Q), ALU.mult)); ch.settle()
                ch.step(v.tensor_reduce(rw[:, t], prod[:], AX.X, ALU.add)); ch.settle()
            ch.step(v.tensor_tensor(rw[:], rw[:], rstd[:], ALU.mult)); ch.settle()
            v.tensor_scalar(rw[:], rw[:], W("route_b"), None, ALU.add).then_inc(s_w, 1)
            dve.wait_ge(s_p, 1)
            v.tensor_copy(turned[:], p_t[:]).then_inc(s_t, 1)

        @block.tensor
        def _(pe):
            pe.wait_ge(s_w, 1)
            pe.transpose(p_t[:], rw[:], C("ident")).then_inc(s_p, 1)

        @block.sync
        def _(sp):
            sp.wait_ge(s_t, 1)
            sp.dma_start(route_dram.rearrange("(t p) -> t p", p=P), turned[:]).then_inc(s_out, 16)
            sp.wait_ge(s_out, 16)


def depth_mlp(nc, mem, route_dram):
    h, xc, rstd, C, W = mem["h"], mem["xc"], mem["rstd"], mem["C"], mem["W"]
    with ExitStack() as ctx:
        sb = lambda name, shape: ctx.enter_context(nc.sbuf_tensor("m_" + name, shape, F32))
        ps = lambda name, shape: ctx.enter_context(nc.psum_tensor("m_" + name, shape, F32))
        sem = lambda name: ctx.enter_context(nc.semaphore("m_" + name))
        mem["route"] = sb("route", [P, TILES])
        route(nc, mem, route_dram)
        x, xt, hid = sb("x", [P, 2, 2, SB, D]), sb("xt", [P, 2, T]), sb("hid", [P, 2, 2, SN])
        y = sb("y", [P, ST, D])
        every = sb("every", [P, 2, SB, T])
        own, cmp = sb("own", [P, ST]), sb("cmp", [P, 2, ST, T])
        rank, kept = sb("rank", [P, 2, ST]), sb("kept", [P, 2, ST])
        p_xt, p_hid, p_y = ps("pxt", [P, 512]), [ps("phid%d" % m, [P, SB, 512]) for m in range(2)], [ps("py%d" % r, [P, 512]) for r in range(2)]
        y_p = lambda r: p_y[r][:, 0:ST * D].rearrange("p (t d) -> p t d", d=D)
        s_x, s_hx, s_xt_p, s_xt, s_hid_p, s_hid, s_y_p, s_dve, s_every, s_ranked, s_taken, s_spent = (
            sem(n) for n in ("x", "hx", "xtp", "xt", "hidp", "hid", "yp", "dve", "every", "ranked", "taken", "spent"))
        block = ctx.enter_context(nc.Block())
        at = lambda n: bass.ds(n * ST, ST)
        by_half = lambda ap: ap.rearrange("p (b two) d -> p two b d", two=2)
        STAGES = 4

        @block.sync
        def _(sp):
            sp.sem_inc(s_ranked, 2)
            rows = route_dram.rearrange("(g n) -> g n", n=SN)
            with sp.Fori(0, TURNS) as i:
                for r in range(2):
                    pause(sp, s_ranked, i * 2 + r + 1, s_spent)
                    sp.dma_start(every[:, r].rearrange("p b t -> p (b t)"), rows[bass.ds(i * 2 + r, 1), :].broadcast_to([P, SN])).then_inc(s_every, 16)
                    pause(sp, s_every, (i * 2 + r + 1) * 16, s_spent)

        @block.vector
        def _(dve):
            ch = Chain(dve, s_dve)
            v = nc.vector

            def do(ins):
                ch.step(ins)
                ch.settle()

            def step(slots, r):
                new, _, ranks, last = slots
                o = 1 - r
                if ranks is not None:
                    pause(dve, s_hx, ranks + 1, s_spent)
                    pause(dve, s_xt_p, ranks + 1, s_spent)
                if new is not None:
                    v.tensor_tensor(x[:, r], by_half(xc[:, at(new)]), by_half(spread(rstd[:, at(new)], D)), ALU.mult).then_inc(s_x, 1)
                if ranks is not None:
                    do(v.tensor_copy(own[:], mem["route"][:, at(ranks)]))
                    pause(dve, s_every, (ranks + 1) * 16, s_spent)
                    for t in range(ST):
                        them = every[:, r, t // 2, :]
                        ch.step(v.tensor_scalar(cmp[:, 0, t], them, own[:, t:t + 1], None, ALU.is_gt, op1=ALU.add, accum_out=rank[:, 0, t:t + 1]))
                        ch.step(v.scalar_tensor_tensor(out=cmp[:, 1, t], in0=them, scalar=own[:, t:t + 1], in1=C("ties")[:, (t % 2) * T:(t % 2) * T + T], op0=ALU.is_equal, op1=ALU.mult, accum_out=rank[:, 1, t:t + 1]))
                    ch.settle()
                    dve.sem_inc(s_ranked, 1)
                    do(v.tensor_tensor(rank[:, 0], rank[:, 0], rank[:, 1], ALU.add))
                    do(v.tensor_scalar(rank[:, 0], rank[:, 0], KEEP - 0.5, None, ALU.is_lt))
                    do(v.tensor_tensor(kept[:, r], rank[:, 0], own[:], ALU.mult))
                if last is not None:
                    pause(dve, s_y_p, last + 1, s_spent)
                    do(v.tensor_tensor(y[:], y_p(o), repeat(W("m_b2"), ST), ALU.add))
                    dve.sem_inc(s_taken, 1)
                    do(v.tensor_tensor(y[:], y[:], spread(kept[:, o], D), ALU.mult))
                    do(v.tensor_tensor(h[:, at(last)], h[:, at(last)], y[:], ALU.add))

            staggered(dve, step, STAGES, ch, 2 * (2 * ST + 7))

        @block.gpsimd
        def _(pool):
            def step(slots, r):
                new = slots[0]
                if new is not None:
                    pause(pool, s_x, new + 1, s_spent)
                    nc.gpsimd.tensor_tensor(by_half(h[:, at(new)]), by_half(h[:, at(new)]), x[:, r], ALU.add).then_inc(s_hx, 1)

            staggered(pool, step, STAGES)

        @block.tensor
        def _(pe):
            def step(slots, r):
                new, hidden, output, last = slots
                o = 1 - r
                if hidden is not None:
                    pause(pe, s_xt, hidden + 1, s_spent)
                if output is not None:
                    pause(pe, s_hid, output * 2 + 2, s_spent)
                if hidden is not None:
                    for m in range(2):
                        for b in range(SB):
                            mm = pe.matmul(p_hid[m][:, b, 0:T], W("m_w1")[b * D:b * D + D, m * P:m * P + P], xt[b * D:b * D + D, o], start=True, stop=True)
                        mm.then_inc(s_hid_p, 1)
                if output is not None:
                    if not isinstance(output, int) or output >= 2:
                        pause(pe, s_taken, output - 1, s_spent)
                    for t in range(ST):
                        for m in range(2):
                            mm = pe.matmul(y_p(r)[:, t, :], hid[:, r, m, t * P:t * P + P], W("m_w2")[:, m * D:m * D + D], start=(m == 0), stop=(m == 1))
                    mm.then_inc(s_y_p, 1)
                if new is not None:
                    pause(pe, s_x, new + 1, s_spent)
                    for half in range(2):
                        mm = pe.transpose(p_xt[:, half * P:half * P + P], x[:, r, half].rearrange("p b d -> p (b d)"), C("ident"))
                    mm.then_inc(s_xt_p, 1)

            staggered(pe, step, STAGES)

        @block.scalar
        def _(act):
            def step(slots, r):
                new, hidden = slots[:2]
                o = 1 - r
                if hidden is not None:
                    for m in range(2):
                        pause(act, s_hid_p, hidden * 2 + m + 1, s_spent)
                        nc.scalar.activation(hid[:, o, m].rearrange("p (b t) -> p b t", b=SB), p_hid[m][:, :, 0:T], ACT.Gelu_apprx_tanh, bias=W("m_b1")[:, m:m + 1]).then_inc(s_hid, 1)
                if new is not None:
                    pause(act, s_xt_p, new + 1, s_spent)
                    nc.scalar.activation(xt[:, r], p_xt[:, 0:T], ACT.Copy).then_inc(s_xt, 1)

            staggered(act, step, STAGES)


def lm_tower_kernel(nc, ids, emb_2, emb_3, emb_4, edges, consts, weights, scratch, out):
    sorted_keys, table_dram, state_dram, top_dram, wt_dram, end_dram, y_dram = scratch
    with ExitStack() as ctx:
        sb = lambda name, shape, dt: ctx.enter_context(nc.sbuf_tensor(name, shape, dt))
        mem = {"c": sb("consts", [P, CONST_N], F32), "w": sb("weights", [P, WEIGHT_N], F32),
               "h": sb("h", [P, TILES, D], F32), "mean": sb("mean", [P, TILES], F32), "rstd": sb("rstd", [P, TILES], F32),
               "top_dram": top_dram, "s_weights": ctx.enter_context(nc.semaphore("s_weights"))}
        mem["C"] = lambda name: mem["c"][:, CONST[name][0]:sum(CONST[name])]
        mem["W"] = lambda name: mem["w"][:, WEIGHT[name][0]:sum(WEIGHT[name])]
        h = mem["h"]
        with nc.sbuf_tensor("e34", [P, 2, TILES, D], F32) as e34:
            mem["e34"] = e34
            embed_and_sort(nc, mem, ids, (emb_2, emb_3, emb_4), edges, consts, weights, sorted_keys)
            with nc.semaphore("s_sum") as s_sum, nc.Block() as block:
                @block.vector
                def _(dve):
                    nc.vector.tensor_tensor(h[:], h[:], e34[:, 0], ALU.add).then_inc(s_sum, 1)
                    dve.wait_ge(s_sum, 1)
                    nc.vector.tensor_tensor(h[:], h[:], e34[:, 1], ALU.add)
        mem["xc"] = sb("xc", [P, TILES, D], F32)
        layernorm_stats(nc, mem, ctx, "0")
        phase_attention(nc, mem)
        graph_experts(nc, mem, sorted_keys, table_dram, state_dram, end_dram, y_dram)
        head_attention(nc, mem)
        depth_mlp(nc, mem, wt_dram)
        with nc.semaphore("s_out") as s_out, nc.Block() as block:
            @block.sync
            def _(sp):
                sp.dma_start(out.rearrange("b (two p) d -> p b two d", p=P), h[:].rearrange("p (b two) d -> p b two d", two=2)).then_inc(s_out, 16)
                sp.wait_ge(s_out, 16)


def shape_constants():
    import numpy as np
    p = np.arange(P)
    f = np.float32
    bits = [1.0 - 2.0 * ((p >> b) & 1) for b in range(7)]
    two_pi_half = np.pi
    c = {
        "ident": np.eye(P), "causal": np.concatenate([np.arange(T)[None] >= p[:, None], (p[None] >= p[:, None])], 1),
        "rnorm": 1.0 / np.sqrt(np.stack([p + 1, p + P + 1], 1) * float(K)),
        "emb_scale": np.stack([np.where((p < n + 1) & (half == 0), 0.0, 0.25) for n in range(3) for half in range(2)], 1),
        "fold": np.where(p % 64 < K, -1.0, 1.0)[:, None], "sin_scale": np.where(p % 64 < K, -two_pi_half, two_pi_half)[:, None],
        "sin_bias": np.where(p % 64 < K, two_pi_half / 2, 0.0)[:, None], "eps": np.full((P, 1), EPS),
        "iota": np.tile(p[None], (P, 1)), "bit_sign": np.stack(bits, 1),
        "flip": np.stack([-bits[0]] + [bits[b] * bits[b + 1] for b in range(6)], 1),
        "before": p[:, None] < p[None], "ties": np.concatenate([np.arange(T)[None] < p[:, None], np.arange(T)[None] < p[:, None] + P], 1),
        "own_head": np.where(p[:, None] // C1 == p[None] // C1, 1.0 / T, 0.0),
        "zero": np.zeros((P, 1)), "ones": np.ones((P, 1)), "ones_row": np.ones((P, P)),
        "all_but_last": np.tile((p[None] < P - 1), (P, 1)), "slice_end": ((p + 1) * float(ALL_COLS))[:, None],
    }
    out = np.zeros((P, CONST_N), f)
    for name, (at, width) in CONST.items():
        out[:, at:at + width] = c[name]
    return out


def lay_out_weights(a):
    import numpy as np
    row = lambda v: np.broadcast_to(np.asarray(v).reshape(1, -1), (P, np.asarray(v).size))
    col = lambda *vs: np.concatenate([np.asarray(v).reshape(-1, 1) for v in vs], 0)
    qkv_w = np.asarray(a["L1_attn_W_qkv"]).reshape(H1, 3, C1, D)
    qkv_b = np.asarray(a["L1_attn_b_qkv"]).reshape(H1, 3, C1)
    under = lambda m, bias: np.concatenate([np.asarray(m), np.asarray(bias).reshape(1, -1)], 0)
    side = lambda m: np.concatenate([np.asarray(m[e]) for e in range(m.shape[0])], 1)
    kkvv = lambda k, v: np.concatenate([np.asarray(m).reshape(-1) for m in (k, k, v, v)])

    def twice(m):
        m = np.asarray(m)
        both = np.zeros((2 * m.shape[0], 2 * m.shape[1]), m.dtype)
        both[:m.shape[0], :m.shape[1]] = m
        both[m.shape[0]:, m.shape[1]:] = m
        return both

    beside = lambda m: np.concatenate([np.asarray(m)] * 2, 1)
    w = {
        "k_w1": twice(a["L0_attn_kw1"].T), "q_w1": twice(a["L0_attn_qw1"].T),
        "k_w2": twice(beside(a["L0_attn_kw2"].T)), "q_w2": twice(beside(a["L0_attn_qw2"].T)), "v_w": twice(a["L0_attn_vw"].T),
        "k_b1": col(*[a["L0_attn_kb1"]] * 2), "q_b1": col(*[a["L0_attn_qb1"]] * 2),
        "k_b2": col(*[a["L0_attn_kb2"]] * 4), "q_b2": col(*[a["L0_attn_qb2"]] * 4),
        "v_b": row(a["L0_attn_vb"]), "w_gat": a["L0_ffn_W_gat"], "att_src": row(a["L0_ffn_att_src"]),
        "att_dst": row(a["L0_ffn_att_dst"]), "b_gat": row(a["L0_ffn_b_gat"]), "gamma": row(a["L0_ffn_ln_gamma"]),
        "beta": row(a["L0_ffn_ln_beta"]), "e_w1": side(a["L0_ffn_W1"]), "e_b1": a["L0_ffn_b1"].T,
        "e_w2": side(a["L0_ffn_W2"]), "e_b2": row(a["L0_ffn_b2"]),
        "q_w": twice(qkv_w[:, 0].reshape(D, D).T), "q_b": col(*[qkv_b[:, 0]] * 2),
        "kv_w": np.concatenate([twice(qkv_w[:, n].reshape(D, D).T) for n in (1, 2)], 1), "kv_b": row(kkvv(qkv_b[:, 1], qkv_b[:, 2])),
        "kv_ln_w": row(kkvv(a["L1_attn_kln_w"], a["L1_attn_vln_w"])), "kv_ln_b": row(kkvv(a["L1_attn_kln_b"], a["L1_attn_vln_b"])),
        "proj_w": twice(a["L1_attn_W_proj"].T), "proj_b": row(a["L1_attn_b_proj"]),
        "route_w": row(a["L1_ffn_wr"]), "route_b": row(a["L1_ffn_br"]), "m_w1": np.concatenate([a["L1_ffn_w1"]] * 2, 0),
        "m_b1": np.asarray(a["L1_ffn_b1"]).reshape(2, P).T, "m_w2": np.concatenate([a["L1_ffn_w2"][:P], a["L1_ffn_w2"][P:]], 1),
        "m_b2": row(a["L1_ffn_b2"]),
    }
    out = np.zeros((P, WEIGHT_N), np.float32)
    for name, (at, width) in WEIGHT.items():
        out[:w[name].shape[0], at:at + width] = w[name]
    return out


def kernel(**inputs):
    import numpy as _np
    import concourse.bacc as _bacc
    from concourse import mybir as _mybir
    from concourse.bass_utils import run_bass_kernel_spmd as _run

    nc = _bacc.Bacc("TRN2", target_bir_lowering=False, num_devices=1)
    a = {k: _np.asarray(v) for k, v in inputs.items()}
    arrays = {"ids": a["x"], "emb_2": a["L0_tok_emb_2"], "emb_3": a["L0_tok_emb_3"], "emb_4": a["L0_tok_emb_4"],
              "edges": a["L0_ffn_edge_index"], "consts": shape_constants(), "weights": lay_out_weights(a)}
    args = [nc.dram_tensor("in_" + n, v.shape, _mybir.dt.from_np(v.dtype), kind="ExternalInput").ap() for n, v in arrays.items()]
    scratch = [nc.dram_tensor(n, shape, F32, kind="Internal").ap() for n, shape in (
        ("sorted_keys", (EDGES + M,)), ("node_table", (M, ROW)), ("edge_states", (EDGES + M, ROW)), ("top_keys", (M,)), ("route", (B * T,)), ("node_ends", (M, 1)), ("expert_outputs", (M, EXPERTS * D)))]
    out = nc.dram_tensor("out_0_dram", (B, T, D), F32, kind="ExternalOutput").ap()
    lm_tower_kernel(nc, *args, scratch, out)
    r = _run(nc, [{"in_" + n: _np.ascontiguousarray(v) for n, v in arrays.items()}], core_ids=[0])
    return r.results[0]["out_0_dram"]
```

```python
from contextlib import ExitStack

import concourse.bass as bass
from concourse import mybir

ALU = mybir.AluOpType
ACT = mybir.ActivationFunctionType
AX = mybir.AxisListType
F32 = mybir.dt.float32
BF16 = mybir.dt.bfloat16
I32 = mybir.dt.int32
U32 = mybir.dt.uint32

P = 128
B, T, D = 64, 256, 64
M = B * T
TILES = M // P
GT = 8
GB = GT // 2
GROUPS = TILES // GT
ST = 4
SB = ST // 2
SLOTS = TILES // ST
TURNS = SLOTS // 2
SN = ST * P
VOCAB, PRIME = 125000, 31
EPS = 1e-5
K = 32
EDGES = 262144
COLS = EDGES // P
NODE_COLS = M // P
ALL_COLS = COLS + NODE_COLS
EXPERTS, HEADS = 4, 4
HID = 2 * D
KEY_BASE = 1 << 29
ROW = 24
BIG = 1e30
H1, C1 = 16, 4
F2 = 4 * D
KEEP = T // 2 - 1


def columns(spec):
    at, n = {}, 0
    for name, width in spec:
        at[name] = (n, width)
        n += width
    return at, n


CONST, CONST_N = columns([
    ("ident", 128), ("causal", 384), ("rnorm", 2), ("emb_scale", 6), ("fold", 1), ("sin_scale", 1),
    ("sin_bias", 1), ("eps", 1), ("iota", 128), ("bit_sign", 7), ("before", 128), ("ties", 512),
    ("own_head", 128), ("zero", 1), ("flip", 7), ("all_but_last", 128), ("slice_end", 1), ("ones", 1), ("ones_row", 128),
])
WEIGHT, WEIGHT_N = columns([
    ("k_w1", 128), ("q_w1", 128), ("k_w2", 128), ("q_w2", 128), ("v_w", 128), ("k_b1", 1), ("q_b1", 1), ("k_b2", 1), ("q_b2", 1), ("v_b", 64),
    ("w_gat", 32), ("att_src", 16), ("att_dst", 16), ("b_gat", 16), ("gamma", 16), ("beta", 16),
    ("e_w1", EXPERTS * HID), ("e_b1", EXPERTS), ("e_w2", EXPERTS * D), ("e_b2", EXPERTS * D),
    ("q_w", 128), ("q_b", 1), ("kv_w", 256), ("kv_b", 256), ("proj_b", 64), ("kv_ln_w", 256), ("kv_ln_b", 256),
    ("proj_w", 128), ("route_w", 64), ("route_b", 1),
    ("m_w1", F2), ("m_b1", 2), ("m_w2", 2 * D), ("m_b2", 64),
])


class Chain:

    def __init__(self, eng, sem):
        self.eng, self.sem, self.base, self.n = eng, sem, 0, 0

    def step(self, ins):
        ins.then_inc(self.sem, 1)
        self.n += 1

    def settle(self):
        self.eng.wait_ge(self.sem, self.base + self.n)

    def turn(self, i, per_turn):
        self.start, self.per_turn = self.n if isinstance(self.base, int) else None, per_turn
        self.base, self.n = i * per_turn + self.start, 0

    def resume(self, i):
        self.base, self.n = i * self.per_turn + self.start, 0

    def end(self, turns):
        assert self.n == self.per_turn, (self.n, self.per_turn)
        self.base, self.n = 0, self.start + turns * self.per_turn


def pause(eng, sem, value, spent):
    eng.wait_ge(sem, value)
    eng.sem_inc(spent, 1)


def spread(ap, n):
    return ap.unsqueeze(len(ap.shape)).broadcast_to(list(ap.shape) + [n])


def repeat(ap, n):
    s = list(ap.shape)
    return ap.unsqueeze(1).broadcast_to([s[0], n] + s[1:])


def clear(nc, sems):
    with nc.Block() as block:
        @block.gpsimd
        def _(pool):
            for s in sems:
                pool.sem_clear(s)


def exact_rows(do, v, to, row, part, rest, kept, C):
    for n in range(3):
        do(v.tensor_copy(to, row if n == 0 else rest))
        do(v.tensor_copy(part, to))
        do(v.tensor_tensor(rest, row if n == 0 else rest, part, ALU.subtract))
        if n == 0:
            do(v.tensor_scalar(kept, part, C("ident")[:, 0:1], None, ALU.mult))
        else:
            do(v.scalar_tensor_tensor(out=kept, in0=part, scalar=C("ident")[:, n:n + 1], in1=kept, op0=ALU.mult, op1=ALU.add))
    do(v.tensor_copy(to, kept))


def ln_centre(do, apart, v, mem, g):
    h, xc, mean = mem["h"], mem["xc"], mem["mean"]
    apart()
    do(v.tensor_reduce(mean[:, g], h[:, g], AX.X, ALU.add))
    do(v.scalar_tensor_tensor(out=xc[:, g], in0=spread(mean[:, g], D), scalar=-1.0 / D, in1=h[:, g], op0=ALU.mult, op1=ALU.add))


def ln_squares(do, apart, v, mem, g, sq):
    xc, rstd = mem["xc"], mem["rstd"]
    do(v.tensor_tensor(sq, xc[:, g], xc[:, g], ALU.mult))
    apart()
    do(v.tensor_reduce(rstd[:, g], sq, AX.X, ALU.add))


def ln_sums(do, apart, v, mem, g, sq):
    ln_centre(do, apart, v, mem, g)
    ln_squares(do, apart, v, mem, g, sq)


LN_STEPS = 4


def ln_root(nc, mem, act, s_sums, s_root):
    act.wait_ge(s_sums, 1)
    nc.scalar.activation(mem["rstd"][:], mem["rstd"][:], ACT.Sqrt, scale=1.0 / D, bias=mem["C"]("eps")).then_inc(s_root, 1)


def ln_finish(nc, mem, dve, s_sums, s_root):
    dve.sem_inc(s_sums, 1)
    dve.wait_ge(s_root, 1)
    nc.vector.reciprocal(mem["rstd"][:], mem["rstd"][:])


def staggered(eng, step, stages, chain=None, per_turn=0):
    def edge(n):
        step([n - s if 0 <= n - s < SLOTS else None for s in range(stages)], n % 2)

    first = stages + (stages % 2)
    for n in range(first):
        edge(n)
    turns = (SLOTS - first) // 2
    with eng.Fori(0, turns) as i:
        if chain is not None:
            chain.turn(i, per_turn)
        for r in range(2):
            step([i * 2 + (first + r - s) for s in range(stages)], r)
        if chain is not None:
            chain.end(turns)
    for n in range(SLOTS, SLOTS + stages - 1):
        edge(n)


def embed_and_sort(nc, mem, ids, tables, edges, consts, weights, sorted_keys):
    c, w, h, e3, xc, mean, rstd = (mem[n] for n in ("c", "w", "h", "e3", "xc", "mean", "rstd"))
    with ExitStack() as ctx:
        sb = lambda name, shape, dt: ctx.enter_context(nc.sbuf_tensor(name, shape, dt))
        sems = []

        def sem(name):
            sems.append(ctx.enter_context(nc.semaphore(name)))
            return sems[-1]

        idf = sb("idf", [B, T + 3], F32)
        idi = sb("idi", [B, T], I32)
        hashes = sb("hashes", [B, 3, T], F32)
        quot = sb("quot", [B, 3, T], I32)
        quotf = sb("quotf", [B, 3, T], F32)
        rows = sb("rows", [P, TILES, 3], I32)
        rows_now = sb("rows_now", [P, 2, GT * 3], I32)
        ring = sb("ring", [P, 2, 3, GT, D], F32)
        ends = sb("ends", [P, 2, COLS], I32)
        keys = [sb("keys0", [P, COLS], F32), sb("keys1", [P, COLS], F32)]
        nodes = sb("nodes", [P, COLS], I32)
        nodes2 = sb("nodes2", [P, COLS], I32)
        tops = [sb("tops0", [P, P], F32), sb("tops1", [P, P], F32)]
        turned = ctx.enter_context(nc.psum_tensor("turned", [P, COLS], F32))
        idx_t = ctx.enter_context(nc.psum_tensor("idx_t", [P, 6, B], F32))

        s_const, s_ids, s_edges = sem("s_const"), sem("s_ids"), sem("s_edges")
        s_dve = sem("s_dve1")
        s_pool = sem("s_pool1")
        s_hash = sem("s_hash")
        s_idx_t = sem("s_idx_t")
        s_rows = sem("s_rows")
        s_landed = [sem("s_landed0"), sem("s_landed1")]
        s_drained = [sem("s_drained0"), sem("s_drained1")]
        s_spent = sem("s_spent1")
        s_turn_go, s_turned = sem("s_turn_go"), sem("s_turned")
        s_iota = sem("s_iota")
        s_xc, s_sq, s_var, s_std = sem("s_xc0"), sem("s_sq0"), sem("s_var0"), sem("s_std0")
        s_tops, s_tops_back, s_sorted = sem("s_tops"), sem("s_tops_back"), sem("s_sorted")
        s_tops_w, s_low_w = sem("s_tops_w"), sem("s_low_w")

        ident = mem["C"]("ident")
        kept = {"k": keys, "t": tops}
        PHASES = [("k", top) for top in range(1, 19)] + [("k", 18), ("t", 14)]
        top_dram = mem["top_dram"]

        final, final_top = (sum(range(1, 19)) + 1 + 18) % 2, 14 % 2

        stage = ExitStack()
        block = stage.enter_context(nc.Block())

        @block.sync
        def _(sp):
            sp.dma_start(idi[:], ids).then_inc(s_ids, 16)
            sp.dma_start(c[:], consts).then_inc(s_const, 16)
            sp.dma_start(ends[:], edges.rearrange("two (p c) -> p two c", p=P)).then_inc(s_edges, 16)
            sp.dma_start(w[:], weights).then_inc(mem["s_weights"], 16)
            sp.wait_ge(s_tops, 1)
            sp.dma_start(top_dram.rearrange("(p c) -> p c", p=8), nodes2[120:128, :].bitcast(F32)).then_inc(s_tops_w, 16)
            sp.wait_ge(s_tops_w, 16)
            sp.dma_start(tops[0][:], top_dram.rearrange("(p c) -> p c", p=P)).then_inc(s_tops_back, 16)
            sp.wait_ge(s_sorted, 2)
            sp.dma_start(sorted_keys[0:EDGES].rearrange("(p c) -> p c", p=P), keys[final][:]).then_inc(s_low_w, 16)
            sp.dma_start(sorted_keys[EDGES:].rearrange("(p c) -> p c", p=P), tops[final_top][:]).then_inc(s_low_w, 16)
            sp.wait_ge(s_low_w, 32)
            sp.wait_ge(mem["s_weights"], 16)

        @block.gpsimd
        def _(pool):
            nc.gpsimd.iota(nodes[:], pattern=[[-1, COLS]], base=EDGES - 1, channel_multiplier=-COLS).then_inc(s_iota, 1)
            pool.wait_ge(s_rows, 1)
            with pool.Fori(0, GROUPS // 2) as i:
                for r in range(2):
                    pause(pool, s_drained[r], i * 6 + 6, s_spent)
                    nc.gpsimd.tensor_copy(rows_now[:, r, :], rows[:].rearrange("p t n -> p (t n)")[:, bass.ds((i * 2 + r) * (GT * 3), GT * 3)]).then_inc(s_pool, 1)
                    pause(pool, s_pool, i * 2 + r + 1, s_spent)
                    for t in range(GT):
                        for n in range(3):
                            pool.indirect_dma_start(
                                out=ring[:, r, n, t, :], out_offset=None, in_=tables[n],
                                in_offset=bass.IndirectOffsetOnAxis(ap=rows_now[:, r, t * 3 + n:t * 3 + n + 1].bitcast(U32), axis=0),
                            ).then_inc(s_landed[r], 16)
            for r in range(2):
                pool.wait_ge(s_drained[r], 6 + GROUPS // 2 * 6)
            ch = Chain(pool, s_pool)
            ch.n = GROUPS
            g = nc.gpsimd
            ch.step(g.tensor_tensor(h[:], h[:], e3[:], ALU.add)); ch.settle()
            ch.step(g.tensor_tensor(h[:], h[:], xc[:], ALU.add)); ch.settle()
            width = D // 2
            ch.step(g.tensor_tensor(e3[:, :, 0:width], h[:, :, 0:width], h[:, :, width:], ALU.add)); ch.settle()
            while width > 1:
                width //= 2
                ch.step(g.tensor_tensor(e3[:, :, 0:width], e3[:, :, 0:width], e3[:, :, width:2 * width], ALU.add)); ch.settle()
            ch.step(g.tensor_scalar(mean[:], e3[:, :, 0], 1.0 / D, None, ALU.mult)); ch.settle()
            g.tensor_tensor(xc[:], h[:], spread(mean[:], D), ALU.subtract).then_inc(s_xc, 1)
            pool.wait_ge(s_sq, 1)
            width = D
            while width > 2:
                width //= 2
                ch.step(g.tensor_tensor(e3[:, :, 0:width], e3[:, :, 0:width], e3[:, :, width:2 * width], ALU.add)); ch.settle()
            g.tensor_tensor(rstd[:], e3[:, :, 0], e3[:, :, 1], ALU.add).then_inc(s_var, 1)

        @block.scalar
        def _(act):
            act.wait_ge(s_const, 16)
            for r in range(2):
                act.sem_inc(s_drained[r], 6)
            with act.Fori(0, GROUPS // 2) as i:
                for r in range(2):
                    pause(act, s_landed[r], (i + 1) * (GT * 3 * 16), s_spent)
                    for n in range(3):
                        for half in range(2):
                            to = (h, e3, xc)[n][:]
                            to = to.rearrange("p (g b two) d -> p g b two d", b=GB, two=2)[:, bass.ds(i * 2 + r, 1), :, half, :]
                            nc.scalar.activation(
                                to.rearrange("p g b d -> p (g b) d"),
                                ring[:, r, n].rearrange("p (b two) d -> p b two d", two=2)[:, :, half, :],
                                ACT.Copy, scale=mem["C"]("emb_scale")[:, n * 2 + half:n * 2 + half + 1],
                            ).then_inc(s_drained[r], 1)
            act.wait_ge(s_xc, 1)
            nc.scalar.activation(e3[:], xc[:], ACT.Square).then_inc(s_sq, 1)
            act.wait_ge(s_var, 1)
            nc.scalar.activation(rstd[:], rstd[:], ACT.Sqrt, scale=1.0 / D, bias=mem["C"]("eps")).then_inc(s_std, 1)

        @block.vector
        def _(dve):
            ch = Chain(dve, s_dve)
            v = nc.vector
            ch.step(v.memset(idf[:, 0:3], 0.0))
            dve.wait_ge(s_ids, 16)
            ch.step(v.tensor_copy(idf[:, 3:], idi[:]))
            ch.settle()
            for n in range(3):
                power = float(PRIME ** (n + 1) % VOCAB)
                before = idf[:, 3:] if n == 0 else hashes[:, n - 1, :]
                ch.step(v.scalar_tensor_tensor(out=hashes[:, n, :], in0=idf[:, 2 - n:2 - n + T], scalar=power, in1=before, op0=ALU.mult, op1=ALU.add))
                ch.settle()
            ch.step(v.tensor_scalar(quot[:], hashes[:], 1.0 / VOCAB, None, ALU.mult)); ch.settle()
            ch.step(v.tensor_copy(quotf[:], quot[:])); ch.settle()
            ch.step(v.scalar_tensor_tensor(out=hashes[:], in0=quotf[:], scalar=-float(VOCAB), in1=hashes[:], op0=ALU.mult, op1=ALU.add)); ch.settle()
            ch.step(v.tensor_scalar(quotf[:], hashes[:], 0.0, float(VOCAB), ALU.is_lt, ALU.mult)); ch.settle()
            ch.step(v.tensor_tensor(hashes[:], hashes[:], quotf[:], ALU.add)); ch.settle()
            ch.step(v.tensor_scalar(quotf[:], hashes[:], float(VOCAB), -float(VOCAB), ALU.is_ge, ALU.mult)); ch.settle()
            v.tensor_tensor(hashes[:], hashes[:], quotf[:], ALU.add).then_inc(s_hash, 1)
            dve.wait_ge(s_idx_t, 1)
            v.tensor_copy(rows[:].rearrange("p (b two) n -> p n two b", two=2),
                          idx_t[:].rearrange("p (n two) b -> p n two b", two=2)).then_inc(s_rows, 1)

            dve.wait_ge(s_edges, 16)
            ki = keys[0][:].bitcast(I32)
            ch.step(v.tensor_scalar(ends[:, 1], ends[:, 1], 15, KEY_BASE | (1 << 14), ALU.logical_shift_left, ALU.bitwise_or)); ch.settle()
            ch.step(v.tensor_tensor(ki, ends[:, 1], ends[:, 0], ALU.bitwise_or))
            dve.wait_ge(s_iota, 1)
            ch.step(v.tensor_scalar(nodes[:], nodes[:], float(M), None, ALU.min)); ch.settle()
            ch.step(v.tensor_scalar(nodes2[:], nodes[:], float(M), None, ALU.add)); ch.settle()
            ch.step(v.tensor_scalar(nodes2[:], nodes2[:], 15, None, ALU.logical_shift_left)); ch.settle()
            ch.step(v.tensor_tensor(nodes2[:], nodes2[:], nodes[:], ALU.bitwise_or)); ch.settle()
            dve.wait_ge(s_const, 16)

            now = [0]
            turns = [0]

            def exchange(arr, step, lo_from=None):
                pairs = lambda t: t.rearrange("p (n two d) -> p n two d", two=2, d=step)
                a = pairs(kept[arr][now[0]][:])
                left, right = a[:, :, 0, :], a[:, :, 1, :]
                o = pairs(kept[arr][1 - now[0]][:])
                if lo_from is not None:
                    left = pairs(lo_from)[:, :, 0, :]
                    ch.step(v.tensor_copy(right, pairs(lo_from)[:, :, 1, :]))
                    ch.settle()
                ch.step(v.tensor_tensor(o[:, :, 0, :], left, right, ALU.min))
                ch.step(v.tensor_tensor(o[:, :, 1, :], left, right, ALU.max))
                ch.settle()
                now[0] = 1 - now[0]

            def turn(arr):
                turns[0] += 1
                dve.sem_inc(s_turn_go, 1)
                dve.wait_ge(s_turned, turns[0])
                return turned[:, 0:COLS if arr == "k" else P]

            def merge(top, arr="k"):
                low = 11 if arr == "k" else 7
                j = top - 1
                if top > low:
                    src = turn(arr)
                    while j >= low:
                        exchange(arr, 1 << (j - low), src)
                        src = None
                        j -= 1
                    while j >= 7:
                        exchange(arr, 1 << j)
                        j -= 1
                    src = turn(arr)
                    while j >= 0:
                        exchange(arr, 1 << j, src)
                        src = None
                        j -= 1
                else:
                    while j >= 0:
                        exchange(arr, 1 << j)
                        j -= 1

            def negate(ap, by):
                ch.step(v.tensor_scalar(ap, ap, by, None, ALU.mult))

            for k in range(1, 19):
                cur = kept["k"][now[0]]
                if k == 1:
                    negate(cur[:].rearrange("p (n a d) -> p n a d", a=2, d=2)[:, :, 1, :], -1.0)
                elif k <= 10:
                    q = cur[:].rearrange("p (n a b d) -> p n a b d", a=2, b=2, d=1 << (k - 1))
                    negate(q[:, :, 0, 1, :], -1.0)
                    negate(q[:, :, 1, 0, :], -1.0)
                elif k == 11:
                    negate(cur[:, 0:COLS // 2], mem["C"]("bit_sign")[:, 0:1])
                    negate(cur[:, COLS // 2:], mem["C"]("flip")[:, 0:1])
                elif k < 18:
                    negate(cur[:], mem["C"]("flip")[:, k - 11:k - 10])
                else:
                    negate(cur[:], mem["C"]("bit_sign")[:, 6:7])
                ch.settle()
                merge(k)
            cur, oth = kept["k"][now[0]], kept["k"][1 - now[0]]
            n2 = nodes2[:].bitcast(F32)
            ch.step(v.tensor_copy(oth[0:96, :], cur[0:96, :]))
            ch.step(v.tensor_tensor(oth[96:P, :], cur[96:P, :], n2[96:P, :], ALU.min))
            ch.settle()
            v.tensor_tensor(n2[96:P, :], cur[96:P, :], n2[96:P, :], ALU.max).then_inc(s_tops, 1)
            now[0] = 1 - now[0]
            merge(18)
            assert now[0] == final
            dve.sem_inc(s_sorted, 1)
            now[0] = 0
            dve.wait_ge(s_tops_back, 16)
            merge(14, "t")
            assert now[0] == final_top
            dve.sem_inc(s_sorted, 1)
            dve.wait_ge(s_std, 1)
            v.reciprocal(rstd[:], rstd[:])

        @block.tensor
        def _(pe):
            pe.wait_ge(s_const, 16)
            pe.wait_ge(s_hash, 1)
            for n in range(3):
                for half in range(2):
                    mm = pe.transpose(idx_t[:, n * 2 + half, :], hashes[:, n, half * P:half * P + P], ident[0:B, 0:B])
            mm.then_inc(s_idx_t, 1)
            turns, done = 0, 0
            for n, (arr, top) in enumerate(PHASES):
                if n == 18:
                    done += 1
                if arr == "t":
                    done = 0
                if arr == "k" and top <= 11:
                    done += top
                    continue
                for exchanges in (top - 7, 7):
                    turns += 1
                    pe.wait_ge(s_turn_go, turns)
                    for b in range((COLS if arr == "k" else P) // P):
                        mm = pe.transpose(turned[:, b * P:b * P + P], kept[arr][done % 2][:, b * P:b * P + P], ident)
                    mm.then_inc(s_turned, 1)
                    done += exchanges
        stage.close()
        clear(nc, sems)


def phase_attention(nc, mem):
    h, xc, rstd, C, W = mem["h"], mem["xc"], mem["rstd"], mem["C"], mem["W"]
    with ExitStack() as ctx:
        sb = lambda name, shape: ctx.enter_context(nc.sbuf_tensor("a0_" + name, shape, F32))
        ps = lambda name, shape: ctx.enter_context(nc.psum_tensor("a0_" + name, shape, F32))
        sem = lambda name: ctx.enter_context(nc.semaphore("a0_" + name))
        x = sb("x", [P, 2, 2, SB, D])
        xt = sb("xt", [P, 2, T])
        hid = sb("hid", [P, 2, 2, T])
        u, phi = sb("u", [P, 2, 2, T]), sb("phi", [P, 2, 2, T])
        val = sb("val", [P, 2, 2, SB, D])
        sm = sb("sm", [P, 2, SB, 384])
        ret, sq = sb("ret", [P, 2, ST, D]), sb("sq", [P, 2, ST, D])
        p_xt, p_hid, p_ph, p_v = ps("pxt", [P, 512]), ps("phid", [P, 2, T]), ps("pph", [P, 2, T]), ps("pv", [P, 512])
        p_sc, p_o = [ps("psc%d" % b, [P, 512]) for b in range(SB)], [ps("po%d" % r, [P, 512]) for r in range(2)]
        out_p = lambda r: p_o[r][:, 0:ST * D].rearrange("p (t d) -> p t d", d=D)
        s_dve, s_x, s_xt_p, s_xt, s_hid_p, s_hid, s_v, s_val, s_ph, s_u, s_fold, s_phi, s_sc, s_sm, s_out, s_sums, s_root, s_spent = (
            sem(n) for n in ("dve", "x", "xtp", "xt", "hidp", "hid", "v", "val", "ph", "u", "fold", "phi", "sc", "sm", "out", "sums", "root", "spent"))
        block = ctx.enter_context(nc.Block())
        at = lambda n: bass.ds(n * ST, ST)
        by_half = lambda ap: ap.rearrange("p (b two) d -> p two b d", two=2)
        STAGES = 4

        @block.vector
        def _(dve):
            ch = Chain(dve, s_dve)
            v = nc.vector

            def do(ins):
                ch.step(ins)
                ch.settle()

            def step(slots, r):
                new, phases, scores, last = slots
                o = 1 - r
                if new is not None:
                    v.tensor_tensor(x[:, r], by_half(xc[:, at(new)]), by_half(spread(rstd[:, at(new)], D)), ALU.mult).then_inc(s_x, 1)
                if last is not None:
                    pause(dve, s_out, last + 1, s_spent)
                    do(v.tensor_tensor(ret[:, o].rearrange("p (b two) d -> p b two d", two=2), out_p(o).rearrange("p (b two) d -> p b two d", two=2),
                                       repeat(spread(C("rnorm"), D), SB), ALU.mult))
                    do(v.tensor_tensor(h[:, at(last)], h[:, at(last)], ret[:, o], ALU.add))
                    ln_sums(do, lambda: dve.sem_inc(s_spent, 1), v, mem, at(last), sq[:, o])
                if phases is not None:
                    pause(dve, s_v, phases + 1, s_spent)
                    v.tensor_tensor(val[:, o].rearrange("p two b d -> p (two b) d"), p_v[:, 0:ST * D].rearrange("p (t d) -> p t d", d=D),
                                    repeat(W("v_b"), ST), ALU.add).then_inc(s_val, 1)
                if scores is not None:
                    for b in range(SB):
                        pause(dve, s_sc, scores * SB + b + 1, s_spent)
                        v.tensor_tensor(sm[:, r, b], p_sc[b][:, 0:384], C("causal"), ALU.mult).then_inc(s_sm, 1)
                if phases is not None:
                    pause(dve, s_u, phases * 2 + 2, s_spent)
                    v.scalar_tensor_tensor(out=u[:, o], in0=u[:, o], scalar=C("fold"), in1=u[:, o], op0=ALU.mult, op1=ALU.max).then_inc(s_fold, 1)

            staggered(dve, step, STAGES, ch, 2 * (2 + LN_STEPS))
            ln_finish(nc, mem, dve, s_sums, s_root)

        @block.tensor
        def _(pe):
            def step(slots, r):
                new, phases, scores, _ = slots
                o = 1 - r
                if phases is not None:
                    pause(pe, s_xt, phases + 1, s_spent)
                    for kq in range(2):
                        pe.matmul(p_hid[:, kq], W("q_w1" if kq else "k_w1"), xt[:, o], start=True, stop=True).then_inc(s_hid_p, 1)
                    if scores is not None:
                        pause(pe, s_val, scores + 1, s_spent)
                    for half in range(2):
                        mm = pe.matmul(p_v[:, half * P:half * P + P], xt[:, o, half * P:half * P + P], W("v_w"), start=True, stop=True)
                    mm.then_inc(s_v, 1)
                if new is not None:
                    pause(pe, s_x, new + 1, s_spent)
                    for half in range(2):
                        mm = pe.transpose(p_xt[:, half * P:half * P + P], x[:, r, half].rearrange("p b d -> p (b d)"), C("ident"))
                    mm.then_inc(s_xt_p, 1)
                if phases is not None:
                    if scores is not None:
                        pause(pe, s_u, scores * 2 + 2, s_spent)
                    pause(pe, s_hid, phases * 2 + 2, s_spent)
                    for kq in range(2):
                        pe.matmul(p_ph[:, kq], W("q_w2" if kq else "k_w2"), hid[:, o, kq], start=True, stop=True).then_inc(s_ph, 1)
                if scores is not None:
                    if phases is None:
                        pause(pe, s_val, scores + 1, s_spent)
                    pause(pe, s_phi, scores + 1, s_spent)
                    for b in range(SB):
                        k, q = (phi[b * D:b * D + D, r, kq] for kq in range(2))
                        pe.matmul(p_sc[b][:, 0:256], k[:, 0:P], q, start=True, stop=True)
                        pe.matmul(p_sc[b][:, 256:384], k[:, P:T], q[:, P:T], start=True, stop=True).then_inc(s_sc, 1)
                    for b in range(SB):
                        pause(pe, s_sm, scores * SB + b + 1, s_spent)
                        pe.matmul(out_p(r)[:, 2 * b, :], sm[:, r, b, 0:P], val[:, r, 0, b, :], start=True, stop=True)
                        pe.matmul(out_p(r)[:, 2 * b + 1, :], sm[:, r, b, P:2 * P], val[:, r, 0, b, :], start=True, stop=False)
                        mm = pe.matmul(out_p(r)[:, 2 * b + 1, :], sm[:, r, b, 2 * P:3 * P], val[:, r, 1, b, :], start=False, stop=True)
                    mm.then_inc(s_out, 1)

            staggered(pe, step, STAGES)

        @block.scalar
        def _(act):
            a = nc.scalar

            def step(slots, r):
                new, phases, scores, _ = slots
                o = 1 - r
                if phases is not None:
                    pause(act, s_hid_p, phases * 2 + 2, s_spent)
                    for kq in range(2):
                        a.activation(hid[:, o, kq], p_hid[:, kq], ACT.Tanh, bias=W("q_b1" if kq else "k_b1")).then_inc(s_hid, 1)
                if scores is not None:
                    pause(act, s_fold, scores + 1, s_spent)
                    a.activation(phi[:, r], u[:, r], ACT.Sin, scale=C("sin_scale"), bias=C("sin_bias")).then_inc(s_phi, 1)
                if new is not None:
                    pause(act, s_xt_p, new + 1, s_spent)
                    a.activation(xt[:, r], p_xt[:, 0:T], ACT.Copy).then_inc(s_xt, 1)
                if phases is not None:
                    pause(act, s_ph, phases * 2 + 2, s_spent)
                    for kq in range(2):
                        a.activation(u[:, o, kq], p_ph[:, kq], ACT.Tanh, bias=W("q_b2" if kq else "k_b2")).then_inc(s_u, 1)

            staggered(act, step, STAGES)
            ln_root(nc, mem, act, s_sums, s_root)


CH = 32
CHUNKS = ALL_COLS // CH
OH = 16


def node_table(nc, mem, table_dram):
    xc, rstd, C, W = mem["xc"], mem["rstd"], mem["C"], mem["W"]
    with ExitStack() as ctx:
        sb = lambda name, shape: ctx.enter_context(nc.sbuf_tensor("nt_" + name, shape, F32))
        ps = lambda name: [ctx.enter_context(nc.psum_tensor("nt_%s%d" % (name, r), [P, 512], F32)) for r in range(2)]
        sem = lambda name: ctx.enter_context(nc.semaphore("nt_" + name))
        x = sb("x", [P, 2, GT, D])
        xt = sb("xt", [P, 2, GB * P])
        tab = sb("tab", [P, TILES, ROW])
        att = sb("att", [P, 2, TILES, 16])
        p_xt, p_h = ps("pxt"), ps("ph")
        s_x, s_xt_p, s_xt, s_h_p, s_h, s_dve, s_tab, s_out, s_spent = (sem(n) for n in ("x", "xtp", "xt", "hp", "h", "dve", "tab", "out", "spent"))
        block = ctx.enter_context(nc.Block())

        @block.vector
        def _(dve):
            v = nc.vector
            with dve.Fori(0, GROUPS // 2) as i:
                for r in range(2):
                    g = bass.ds((i * 2 + r) * GT, GT)
                    pause(dve, s_xt_p, i * 2 + r + 1, s_spent)
                    v.tensor_tensor(x[:, r], xc[:, g], spread(rstd[:, g], D), ALU.mult).then_inc(s_x, 1)
            ch = Chain(dve, s_dve)
            dve.wait_ge(s_h, GROUPS + 2)
            for n, name in enumerate(("att_src", "att_dst")):
                ch.step(v.tensor_tensor(att[:, n], tab[:, :, 0:16], repeat(W(name), TILES), ALU.mult))
            ch.settle()
            for n in range(2):
                v.tensor_reduce(tab[:, :, 16 + 4 * n:20 + 4 * n], att[:, n].rearrange("p t (h e) -> p t h e", e=EXPERTS), AX.X, ALU.add).then_inc(s_tab, 1)

        @block.tensor
        def _(pe):
            pe.sem_inc(s_xt_p, 2)
            pe.sem_inc(s_h, 2)
            with pe.Fori(0, GROUPS // 2) as i:
                for r in range(2):
                    pause(pe, s_x, i * 2 + r + 1, s_spent)
                    for t in range(GB):
                        mm = pe.transpose(p_xt[r][:, t * P:t * P + P], x[:, r, 2 * t:2 * t + 2].rearrange("p two d -> p (two d)"), C("ident"))
                    mm.then_inc(s_xt_p, 1)
                for r in range(2):
                    pause(pe, s_xt, i * 2 + r + 1, s_spent)
                    pause(pe, s_h, i * 2 + r + 1, s_spent)
                    for t in range(GB):
                        mm = pe.matmul(p_h[r][:, t * 32:t * 32 + 32], xt[:, r, t * P:t * P + P], W("w_gat"), start=True, stop=True)
                    mm.then_inc(s_h_p, 1)

        @block.scalar
        def _(act):
            with act.Fori(0, GROUPS // 2) as i:
                for r in range(2):
                    pause(act, s_xt_p, i * 2 + r + 3, s_spent)
                    nc.scalar.activation(xt[:, r], p_xt[r][:], ACT.Copy).then_inc(s_xt, 1)
                for r in range(2):
                    pause(act, s_h_p, i * 2 + r + 1, s_spent)
                    nc.scalar.activation(tab[:, bass.ds((i * 2 + r) * GT, GT), 0:16], p_h[r][:, 0:GT * 16].rearrange("p (t f) -> p t f", f=16), ACT.Copy).then_inc(s_h, 1)

        @block.sync
        def _(sp):
            sp.wait_ge(s_tab, 2)
            sp.dma_start(table_dram.rearrange("(t p) r -> p t r", p=P), tab[:]).then_inc(s_out, 16)
            sp.wait_ge(s_out, 16)


def edge_stream(nc, mem, sorted_keys, table_dram, state_dram, y_dram):
    C = mem["C"]
    with ExitStack() as ctx:
        sb = lambda name, shape, dt: ctx.enter_context(nc.sbuf_tensor(name, shape, dt))
        sem = lambda name: ctx.enter_context(nc.semaphore("es_" + name))
        key = sb("es_key", [P, ALL_COLS], I32)
        src = sb("es_src", [P, ALL_COLS], I32)
        tmp = sb("es_tmp", [P, ALL_COLS], I32)
        keep = sb("es_keep", [P, ALL_COLS], F32)
        starts = tmp[:].bitcast(F32)
        drop = key[:].bitcast(F32)
        hi = sb("es_hi", [P, ALL_COLS], BF16)
        lo = sb("es_lo", [P, ALL_COLS], BF16)
        iota = sb("es_iota", [P, P], BF16)
        hot = sb("es_hot", [P, 2, 2, OH, P], BF16)
        now = sb("es_now", [P, 2, CH], I32)
        row0 = sb("es_row0", [P, ROW], F32)
        got = sb("es_got", [P, 2, CH, ROW], F32)
        a_self = sb("es_aself", [P, 4, CH], F32)
        a_dst = sb("es_adst", [P, 2, 4, CH], F32)
        e = sb("es_e", [P, 4, CH], F32)
        diff = sb("es_diff", [P, 2, CH, 4], F32)
        ex = sb("es_ex", [P, 2, CH, 4], F32)
        msg = sb("es_msg", [P, CH, 16], F32)
        st = sb("es_st", [P, 2, CH + 1, ROW], F32)
        counts = ctx.enter_context(nc.psum_tensor("es_counts", [P, P], F32))
        x, xt = sb("ex_x", [P, ST, D], F32), sb("ex_xt", [D, SN], F32)
        hid, y = sb("ex_hid", [P, 2, SN], F32), sb("ex_y", [P, ST, EXPERTS * D], F32)
        ps = lambda name, shape: ctx.enter_context(nc.psum_tensor("ex_" + name, shape, F32))
        p_xt, p_y = ps("pxt", [D, SN]), ps("py", [P, ST, EXPERTS * D])
        p_hid = [ps("phid0", [P, SN]), ps("phid1", [P, SN])]
        s_x, s_xt_p, s_xt, s_hid_p, s_hid, s_y_p, s_y, s_y_out = (sem(n) for n in ("x", "xtp", "xt", "hidp", "hid", "yp", "y", "yout"))
        C, W, xc, rstd = mem["C"], mem["W"], mem["xc"], mem["rstd"]
        SLOTS = TILES // ST
        s_keys, s_dve, s_pool, s_src, s_row0, s_diff, s_ex, s_state, s_stored0, s_stored1, s_spent, s_hot, s_used = (
            sem(n) for n in ("keys", "dve", "pool", "src", "row0", "diff", "ex", "state", "stored0", "stored1", "spent", "hot", "used"))
        s_landed, s_free, s_stored = [sem("landed0"), sem("landed1")], [sem("free0"), sem("free1")], [s_stored0, s_stored1]
        block = ctx.enter_context(nc.Block())
        HOTS = CH // OH

        @block.sync
        def _(sp):
            sp.dma_start(key[:], sorted_keys.rearrange("(p c) -> p c", p=P).bitcast(I32)).then_inc(s_keys, 16)
            states = state_dram.rearrange("(p c) r -> p c r", p=P)
            for r in range(2):
                sp.sem_inc(s_stored[r], 16)
            sp.sem_inc(s_y_out, 16)

            def turn(i, with_experts):
                for r in range(2):
                    pause(sp, s_state, i * 2 + r + 1, s_spent)
                    sp.dma_start(states[:, bass.ds((i * 2 + r) * CH, CH), :], st[:, r, 1:, :]).then_inc(s_stored[r], 16)
                    if r == 0 and with_experts:
                        pause(sp, s_y, i + 2, s_spent)
                        sp.dma_start(y_dram.rearrange("(s t p) f -> s p t f", p=P, t=ST)[bass.ds(i, 1)].rearrange("s p t f -> (s p) t f"), y[:]).then_inc(s_y_out, 16)

            with sp.Fori(0, SLOTS) as i:
                turn(i, True)
            with sp.Fori(SLOTS, CHUNKS // 2) as i:
                turn(i, False)
            sp.wait_ge(s_y_out, 16 * (SLOTS + 1))
            for r in range(2):
                sp.wait_ge(s_stored[r], 16 * (CHUNKS // 2 + 1))

        @block.gpsimd
        def _(pool):
            pool.wait_ge(s_src, 1)
            pool.indirect_dma_start(out=row0[:], out_offset=None, in_=table_dram,
                                    in_offset=bass.IndirectOffsetOnAxis(ap=mem["first"][:, 0:1].bitcast(U32), axis=0)).then_inc(s_row0, 16)
            for r in range(2):
                pool.sem_inc(s_free[r], 1)
            with pool.Fori(0, CHUNKS // 2) as i:
                for r in range(2):
                    pause(pool, s_free[r], i + 1, s_spent)
                    nc.gpsimd.tensor_copy(now[:, r, :], src[:, bass.ds((i * 2 + r) * CH, CH)]).then_inc(s_pool, 1)
                    pause(pool, s_pool, i * 2 + r + 1, s_spent)
                    for k in range(CH):
                        pool.indirect_dma_start(out=got[:, r, k, :], out_offset=None, in_=table_dram,
                                                in_offset=bass.IndirectOffsetOnAxis(ap=now[:, r, k:k + 1].bitcast(U32), axis=0)).then_inc(s_landed[r], 16)

        @block.scalar
        def _(act):
            def turn(i, with_experts):
                for r in range(2):
                    pause(act, s_diff, i * 2 + r + 1, s_spent)
                    nc.scalar.activation(ex[:], diff[:], ACT.Exp).then_inc(s_ex, 1)
                    if r == 0 and with_experts:
                        pause(act, s_xt_p, i + 1, s_spent)
                        nc.scalar.activation(xt[:], p_xt[:], ACT.Copy).then_inc(s_xt, 1)
                        for e in range(EXPERTS):
                            pause(act, s_hid_p, i * EXPERTS + e + 1, s_spent)
                            if e >= 2:
                                pause(act, s_y_p, i * EXPERTS + e - 1, s_spent)
                            nc.scalar.activation(hid[:, e % 2], p_hid[e % 2][:], ACT.Gelu, bias=W("e_b1")[:, e:e + 1]).then_inc(s_hid, 1)
                        pause(act, s_y_p, i * EXPERTS + EXPERTS, s_spent)
                        pause(act, s_y_out, i * 16 + 16, s_spent)
                        nc.scalar.activation(y[:], p_y[:], ACT.Copy).then_inc(s_y, 1)

            with act.Fori(0, SLOTS) as i:
                turn(i, True)
            with act.Fori(SLOTS, CHUNKS // 2) as i:
                turn(i, False)

        @block.tensor
        def _(pe):
            pe.wait_ge(s_src, 1)
            pe.matmul(counts[:], hot[:, 0, 0, 0, :], hot[:, 0, 1, 0, :], start=True, stop=False, skip_group_check=True).then_inc(s_used, 2)

            def expert(i, e):
                pe.matmul(p_hid[e % 2][:], W("e_w1")[0:D, e * HID:e * HID + HID], xt[:], start=True, stop=True).then_inc(s_hid_p, 1)

            def turn(i, with_experts):
                for n in range(2 * HOTS):
                    pause(pe, s_hot, i * (2 * HOTS) + n + 1, s_spent)
                    for k in range(OH):
                        mm = pe.matmul(counts[:], hot[:, n % 2, 0, k, :], hot[:, n % 2, 1, k, :], start=False, stop=False, skip_group_check=True)
                    mm.then_inc(s_used, 1)
                    if n == 0 and with_experts:
                        pause(pe, s_x, i + 1, s_spent)
                        for t in range(ST):
                            mm = pe.transpose(p_xt[:, t * P:t * P + P], x[:, t, :], C("ident"))
                        mm.then_inc(s_xt_p, 1)
                        pause(pe, s_xt, i + 1, s_spent)
                        expert(i, 0)
                        expert(i, 1)
                        pause(pe, s_y, i + 1, s_spent)
                        for t in range(ST):
                            pe.matmul(p_y[:, t, :], C("ones_row")[0:1], W("e_b2")[0:1], start=(t % 2 == 0), stop=False, skip_group_check=True)
                        for e in range(EXPERTS):
                            pause(pe, s_hid, i * EXPERTS + e + 1, s_spent)
                            for t in range(ST):
                                mm = pe.matmul(p_y[:, t, e * D:e * D + D], hid[:, e % 2, t * P:t * P + P], W("e_w2")[:, e * D:e * D + D], start=False, stop=True, skip_group_check=True)
                            mm.then_inc(s_y_p, 1)
                            if e + 2 < EXPERTS:
                                expert(i, e + 2)

            pe.sem_inc(s_y, 1)
            with pe.Fori(0, SLOTS) as i:
                turn(i, True)
            with pe.Fori(SLOTS, CHUNKS // 2) as i:
                turn(i, False)
            pe.matmul(counts[:], hot[:, 0, 0, 0, :], mem["zeros"][:], start=False, stop=True, skip_group_check=True).then_inc(s_used, 1)

        @block.vector
        def _(dve):
            ch = Chain(dve, s_dve)
            v = nc.vector
            dve.wait_ge(s_keys, 16)
            ch.step(v.tensor_scalar(src[:], key[:], M - 1, None, ALU.bitwise_and))
            ch.step(v.tensor_scalar(mem["first"][:], key[:, 0:1], 15, M - 1, ALU.logical_shift_right, ALU.bitwise_and))
            ch.step(v.tensor_copy(iota[:], C("iota")))
            ch.step(v.memset(mem["zeros"][:], 0.0))
            ch.step(v.memset(hot[:, 0, :, 0, :], 0.0))
            ch.settle()
            dve.sem_inc(s_src, 1)
            for to, shift in ((hi, 22), (lo, 15)):
                ch.step(v.tensor_scalar(tmp[:], key[:], shift, P - 1, ALU.logical_shift_right, ALU.bitwise_and)); ch.settle()
                ch.step(v.tensor_copy(to[:], tmp[:])); ch.settle()
            ch.step(v.tensor_scalar(tmp[:], key[:], 14, 1, ALU.logical_shift_right, ALU.bitwise_and)); ch.settle()
            ch.step(v.tensor_copy(keep[:], tmp[:])); ch.settle()
            ch.step(v.tensor_scalar(starts, keep[:], -1.0, 1.0, ALU.mult, ALU.add)); ch.settle()
            ch.step(v.tensor_scalar(drop, starts, -BIG, None, ALU.mult))
            ch.step(v.tensor_reduce(mem["has_start"][:], starts, AX.X, ALU.max))
            ch.step(v.tensor_copy(mem["first_keep"][:], keep[:, 0:1]))
            ch.step(v.memset(st[:, 1, CH, 0:4], -BIG))
            ch.step(v.memset(st[:, 1, CH, 4:ROW], 0.0))
            dve.wait_ge(s_row0, 16)
            ch.step(v.tensor_copy(a_dst[:, 1, :, CH - 1], row0[:, 20:24]))
            ch.settle()
            def turn(i, with_experts):
                if with_experts:
                    g = bass.ds(i * ST, ST)
                    v.tensor_tensor(x[:], xc[:, g], spread(rstd[:, g], D), ALU.mult).then_inc(s_x, 1)
                for r in range(2):
                    cols = bass.ds((i * 2 + r) * CH, CH)
                    for n in range(HOTS):
                        at = bass.ds((i * 2 + r) * CH + n * OH, OH)
                        pause(dve, s_used, (i * 2 + r) * HOTS + n + 1, s_spent)
                        v.tensor_tensor(hot[:, n % 2, 0], repeat(iota[:], OH), spread(hi[:, at], P), ALU.is_equal)
                        v.tensor_tensor(hot[:, n % 2, 1], repeat(iota[:], OH), spread(lo[:, at], P), ALU.is_equal).then_inc(s_hot, 1)
                    pause(dve, s_landed[r], (i + 1) * (16 * CH), s_spent)
                    g = got[:, r]
                    ch.step(v.tensor_tensor(a_self[:], g[:, :, 20:24].rearrange("p c k -> p k c"), repeat(starts[:, cols], 4), ALU.mult)); ch.settle()
                    for k in range(4):
                        ch.step(v.tensor_tensor_scan(a_dst[:, r, k], keep[:, cols], a_self[:, k], a_dst[:, 1 - r, k, CH - 1:CH], ALU.mult, ALU.add))
                    ch.settle()
                    ch.step(v.tensor_tensor(e[:], g[:, :, 16:20].rearrange("p c k -> p k c"), a_dst[:, r], ALU.add)); ch.settle()
                    ch.step(v.scalar_tensor_tensor(out=e[:], in0=e[:], scalar=0.2, in1=e[:], op0=ALU.mult, op1=ALU.max)); ch.settle()
                    pause(dve, s_stored[r], (i + 1) * 16, s_spent)
                    ch.step(v.tensor_copy(st[:, r, 0, :], st[:, 1 - r, CH, :]))
                    ch.settle()
                    for k in range(4):
                        ch.step(v.tensor_tensor_scan(st[:, r, 1:, k], drop[:, cols], e[:, k], st[:, r, 0, k:k + 1], ALU.add, ALU.max))
                    ch.settle()
                    ch.step(v.tensor_tensor(diff[:, 0], st[:, r, 0:CH, 0:4], st[:, r, 1:, 0:4], ALU.subtract))
                    ch.step(v.tensor_tensor(diff[:, 1], e[:].rearrange("p k c -> p c k"), st[:, r, 1:, 0:4], ALU.subtract))
                    ch.settle()
                    v.tensor_tensor(diff[:, 0], diff[:, 0], spread(drop[:, cols], 4), ALU.add).then_inc(s_diff, 1)
                    pause(dve, s_ex, i * 2 + r + 1, s_spent)
                    for k in range(4):
                        ch.step(v.tensor_tensor_scan(st[:, r, 1:, 4 + k], ex[:, 0, :, k], ex[:, 1, :, k], st[:, r, 0, 4 + k:5 + k], ALU.mult, ALU.add))
                    for k in range(4):
                        ch.step(v.tensor_tensor(msg[:, :, 4 * k:4 * k + 4], g[:, :, 4 * k:4 * k + 4], spread(ex[:, 1, :, k], 4), ALU.mult))
                    ch.settle()
                    dve.sem_inc(s_free[r], 1)
                    for j in range(16):
                        ch.step(v.tensor_tensor_scan(st[:, r, 1:, 8 + j], ex[:, 0, :, j // 4], msg[:, :, j], st[:, r, 0, 8 + j:9 + j], ALU.mult, ALU.add))
                    ch.settle()
                    dve.sem_inc(s_state, 1)

            PER = 2 * 38
            with dve.Fori(0, SLOTS) as i:
                ch.turn(i, PER)
                turn(i, True)
            with dve.Fori(SLOTS, CHUNKS // 2) as i:
                ch.resume(i)
                turn(i, False)
            ch.end(CHUNKS // 2)
            ch.step(v.tensor_copy(mem["last"][:], st[:, 1, CH, :]))
            dve.wait_ge(s_used, 2 + CHUNKS * HOTS + 1)
            ch.step(v.tensor_copy(mem["counts"][:], counts[:]))
            ch.settle()


def join_runs(nc, mem, state_dram, end_dram):
    C = mem["C"]
    with ExitStack() as ctx:
        sb = lambda name, shape, dt: ctx.enter_context(nc.sbuf_tensor("jr_" + name, shape, dt))
        ps = lambda name, shape: ctx.enter_context(nc.psum_tensor("jr_" + name, shape, F32))
        sem = lambda name: ctx.enter_context(nc.semaphore("jr_" + name))
        total, prefix, end_f, end_i = sb("total", [P, 1], F32), sb("prefix", [P, 1], F32), sb("endf", [P, P], F32), sb("endi", [P, P], I32)
        pos, pos_f, bad, to, row = sb("pos", [P, 1], I32), sb("posf", [P, 1], F32), sb("bad", [P, 1], F32), sb("to", [P, 1], I32), sb("row", [P, ROW], F32)
        wide = sb("wide", [P, 4, 16], F32)
        tr = sb("tr", [16, 4, P], F32)
        car = sb("car", [16, 3, P + 1], F32)
        df = sb("df", [16, 2, P], F32)
        fx = sb("fx", [16, 2, P], F32)
        ws = sb("ws", [16, 2, P], F32)
        cin = sb("cin", [P, 3, 16], F32)
        mine = sb("mine", [P, 3, 16], F32)
        d2, x2, mix, mix2, new = sb("d2", [P, 2, 16], F32), sb("x2", [P, 2, 16], F32), sb("mix", [P, 2, 16], F32), sb("mix2", [P, 2, 16], F32), sb("new", [P, ROW], F32)
        m16 = sb("m16", [P, 16], F32)
        p_pre, p_tr, p_back, p_end = ps("ppre", [P, 1]), ps("ptr", [16, 4, P]), ps("pback", [P, 3, 16]), ps("pend", [P, P])
        s_dve, s_total, s_pre, s_end, s_end_t, s_endd, s_pos, s_posok, s_row, s_wide, s_tr, s_ex, s_exd, s_car, s_back, s_ex2, s_ex2d, s_new, s_scat = (
            sem(n) for n in ("dve", "total", "pre", "end", "endt", "endd", "pos", "posok", "row", "wide", "tr", "ex", "exd", "car", "back", "ex2", "ex2d", "new", "scat"))
        block = ctx.enter_context(nc.Block())

        @block.vector
        def _(dve):
            ch = Chain(dve, s_dve)
            v = nc.vector
            counts = mem["counts"]
            v.tensor_reduce(total[:], counts[:], AX.X, ALU.add).then_inc(s_total, 1)
            dve.wait_ge(s_pre, 1)
            ch.step(v.tensor_copy(prefix[:], p_pre[:])); ch.settle()
            ch.step(v.tensor_scalar(prefix[:], prefix[:], -1.0, None, ALU.add)); ch.settle()
            ch.step(v.memset(end_f[:], 1.0)); ch.settle()
            ch.step(v.tensor_tensor_scan(end_f[:], end_f[:], counts[:], prefix[:], ALU.mult, ALU.add)); ch.settle()
            v.tensor_copy(end_i[:], end_f[:]).then_inc(s_end, 1)
            dve.wait_ge(s_end_t, 1)
            ch.step(v.tensor_copy(mem["node_end"][:], p_end[:]))
            last = mem["last"]
            ch.step(v.tensor_copy(wide[:, 0].rearrange("p (h e) -> p h e", e=4), spread(last[:, 0:4], 4)))
            ch.step(v.tensor_copy(wide[:, 1].rearrange("p (h e) -> p h e", e=4), spread(last[:, 4:8], 4)))
            ch.step(v.tensor_copy(wide[:, 2], last[:, 8:24]))
            ch.step(v.tensor_copy(wide[:, 3], mem["has_start"][:, 0:1].broadcast_to([P, 16]))); ch.settle()
            dve.sem_inc(s_wide, 1)
            dve.wait_ge(s_tr, 1)
            ch.step(v.tensor_copy(tr[:], p_tr[:]))
            ch.step(v.memset(car[:, 0, 0:1], -BIG))
            ch.step(v.memset(car[:, 1:, 0:1], 0.0)); ch.settle()
            ch.step(v.tensor_scalar(tr[:, 3], tr[:, 3], -BIG, None, ALU.mult)); ch.settle()
            ch.step(v.tensor_tensor_scan(car[:, 0, 1:], tr[:, 3], tr[:, 0], car[:, 0, 0:1], ALU.add, ALU.max)); ch.settle()
            ch.step(v.tensor_tensor(df[:, 0], car[:, 0, 0:P], car[:, 0, 1:], ALU.subtract))
            ch.step(v.tensor_tensor(df[:, 1], tr[:, 0], car[:, 0, 1:], ALU.subtract)); ch.settle()
            v.tensor_tensor(df[:, 0], df[:, 0], tr[:, 3], ALU.add).then_inc(s_ex, 1)
            dve.wait_ge(s_exd, 1)
            for k in range(2):
                ch.step(v.tensor_tensor(ws[:, k], fx[:, 1], tr[:, 1 + k], ALU.mult))
            ch.settle()
            for k in range(2):
                ch.step(v.tensor_tensor_scan(car[:, 1 + k, 1:], fx[:, 0], ws[:, k], car[:, 1 + k, 0:1], ALU.mult, ALU.add))
            ch.settle()
            dve.sem_inc(s_car, 1)
            dve.wait_ge(s_pos, 16)
            ch.step(v.tensor_copy(pos_f[:], pos[:])); ch.settle()
            ch.step(v.tensor_tensor(bad[:], pos_f[:], C("slice_end"), ALU.is_ge)); ch.settle()
            ch.step(v.tensor_tensor(bad[:], bad[:], mem["first_keep"][:], ALU.is_ge)); ch.settle()
            ch.step(v.scalar_tensor_tensor(out=pos_f[:], in0=bad[:], scalar=float(1 << 20), in1=pos_f[:], op0=ALU.mult, op1=ALU.add)); ch.settle()
            ch.step(v.tensor_copy(to[:], pos_f[:]))
            dve.wait_ge(s_back, 1)
            ch.step(v.tensor_copy(cin[:], p_back[:]))
            dve.wait_ge(s_row, 16)
            for k in range(2):
                ch.step(v.tensor_copy(mine[:, k].rearrange("p (h e) -> p h e", e=4), spread(row[:, 4 * k:4 * k + 4], 4)))
            ch.step(v.tensor_copy(mine[:, 2], row[:, 8:24])); ch.settle()
            ch.step(v.tensor_tensor(m16[:], cin[:, 0], mine[:, 0], ALU.max)); ch.settle()
            ch.step(v.tensor_tensor(d2[:, 0], cin[:, 0], m16[:], ALU.subtract))
            ch.step(v.tensor_tensor(d2[:, 1], mine[:, 0], m16[:], ALU.subtract)); ch.settle()
            dve.sem_inc(s_ex2, 1)
            dve.wait_ge(s_ex2d, 1)
            ch.step(v.tensor_tensor(mix[:], cin[:, 1:], repeat(x2[:, 0], 2), ALU.mult))
            ch.step(v.tensor_tensor(mix2[:], mine[:, 1:], repeat(x2[:, 1], 2), ALU.mult)); ch.settle()
            ch.step(v.tensor_tensor(mix[:], mix[:], mix2[:], ALU.add)); ch.settle()
            ch.step(v.tensor_copy(new[:, 0:4], m16[:].rearrange("p (h e) -> p h e", e=4)[:, :, 0]))
            ch.step(v.tensor_copy(new[:, 4:8], mix[:, 0].rearrange("p (h e) -> p h e", e=4)[:, :, 0]))
            ch.step(v.tensor_copy(new[:, 8:24], mix[:, 1])); ch.settle()
            dve.sem_inc(s_new, 1)

        @block.tensor
        def _(pe):
            pe.wait_ge(s_total, 1)
            pe.matmul(p_pre[:], C("before"), total[:], start=True, stop=True).then_inc(s_pre, 1)
            pe.wait_ge(s_end, 1)
            pe.transpose(p_end[:], end_f[:], C("ident")).then_inc(s_end_t, 1)
            pe.wait_ge(s_wide, 1)
            for k in range(4):
                mm = pe.transpose(p_tr[:, k], wide[:, k], C("ident"))
            mm.then_inc(s_tr, 1)
            pe.wait_ge(s_car, 1)
            for k in range(3):
                mm = pe.transpose(p_back[:, k], car[:, k, 0:P], C("ident")[0:16, 0:16])
            mm.then_inc(s_back, 1)

        @block.scalar
        def _(act):
            act.wait_ge(s_ex, 1)
            nc.scalar.activation(fx[:], df[:], ACT.Exp).then_inc(s_exd, 1)
            act.wait_ge(s_ex2, 1)
            nc.scalar.activation(x2[:], d2[:], ACT.Exp).then_inc(s_ex2d, 1)

        @block.gpsimd
        def _(pool):
            pool.wait_ge(s_end, 1)
            pool.dma_start(end_dram.rearrange("(p c) one -> p (c one)", p=P), end_i[:].bitcast(F32)).then_inc(s_endd, 16)
            pool.wait_ge(s_endd, 16)
            at = lambda t: bass.IndirectOffsetOnAxis(ap=t[:, 0:1].bitcast(U32), axis=0)
            pool.indirect_dma_start(out=pos[:].bitcast(F32), out_offset=None, in_=end_dram, in_offset=at(mem["first"])).then_inc(s_pos, 16)
            pool.wait_ge(s_pos, 16)
            pool.indirect_dma_start(out=row[:], out_offset=None, in_=state_dram, in_offset=at(pos)).then_inc(s_row, 16)
            pool.wait_ge(s_new, 1)
            pool.indirect_dma_start(out=state_dram, out_offset=at(to), in_=new[:], in_offset=None,
                                    bounds_check=EDGES + M - 1, oob_is_err=False).then_inc(s_scat, 16)
            pool.wait_ge(s_scat, 16)


GATE_STEPS = 37


def gate(nc, mem, state_dram, y_dram):
    h, xc, mean, rstd, C, W = mem["h"], mem["xc"], mem["mean"], mem["rstd"], mem["C"], mem["W"]
    RG = 16
    TURNS = TILES // RG // 2
    OURS = EXPERTS - 1
    with ExitStack() as ctx:
        sb = lambda name, shape, dt=F32: ctx.enter_context(nc.sbuf_tensor("gt_" + name, shape, dt))
        sem = lambda name: ctx.enter_context(nc.semaphore("gt_" + name))
        now = sb("now", [P, 2, RG], I32)
        ring = sb("ring", [P, 2, RG, ROW])
        den = sb("den", [P, RG, 4])
        agg, sq = sb("agg", [P, RG, 16]), sb("sq", [P, RG, 16])
        mu, sd = sb("mu", [P, RG]), sb("sd", [P, RG])
        sc = sb("sc", [P, RG, 4])
        best = sb("best", [P, 2, RG])
        pick = sb("pick", [P, 2, 4, RG])
        found, t, w1 = sb("found", [P, RG]), sb("t", [P, RG]), sb("w1", [P, 2, RG])
        gates = sb("gates", [P, RG, EXPERTS])
        y = [sb("y%d" % r, [P, RG, EXPERTS, D]) for r in range(2)]
        total, sq_h = sb("total", [P, RG, 2, D]), sb("sqh", [P, RG, D])
        s_pool, s_spent, s_dve, s_var, s_std, s_t, s_exp, s_gates, s_last, s_xc, s_sq, s_used, s_sums, s_root = (
            sem(n) for n in ("pool", "spent", "dve", "var", "std", "t", "exp", "gates", "last", "xc", "sq", "used", "sums", "root"))
        s_landed, s_free, s_y = ([sem(n + "0"), sem(n + "1")] for n in ("landed", "free", "y"))
        block = ctx.enter_context(nc.Block())
        at = lambda i, r: bass.ds((i * 2 + r) * RG, RG)

        @block.sync
        def _(sp):
            sp.sem_inc(s_used, 2)
            with sp.Fori(0, TURNS) as i:
                for r in range(2):
                    pause(sp, s_used, i * 2 + r + 1, s_spent)
                    sp.dma_start(y[r][:].rearrange("p t e d -> p t (e d)"),
                                 y_dram.rearrange("(s t p) f -> s p t f", p=P, t=RG)[bass.ds(i * 2 + r, 1)].rearrange("s p t f -> (s p) t f")).then_inc(s_y[r], 16)

        @block.gpsimd
        def _(pool):
            for r in range(2):
                pool.sem_inc(s_free[r], 1)
            with pool.Fori(0, TURNS) as i:
                for r in range(2):
                    pause(pool, s_free[r], i + 1, s_spent)
                    nc.gpsimd.tensor_copy(now[:, r], mem["node_end"][:, at(i, r)]).then_inc(s_pool, 1)
                    pause(pool, s_pool, i * 2 + r + 1, s_spent)
                    for k in range(RG):
                        pool.indirect_dma_start(out=ring[:, r, k, :], out_offset=None, in_=state_dram,
                                                in_offset=bass.IndirectOffsetOnAxis(ap=now[:, r, k:k + 1].bitcast(U32), axis=0)).then_inc(s_landed[r], 16)

        @block.scalar
        def _(act):
            with act.Fori(0, TURNS) as i:
                for r in range(2):
                    pause(act, s_var, i * 2 + r + 1, s_spent)
                    nc.scalar.activation(sd[:], sd[:], ACT.Sqrt, scale=1.0 / 16, bias=C("eps")).then_inc(s_std, 1)
                    pause(act, s_t, i * 2 + r + 1, s_spent)
                    nc.scalar.activation(t[:], t[:], ACT.Exp).then_inc(s_exp, 1)
                    pause(act, s_gates, i * 2 + r + 1, s_spent)
                    for k in range(RG):
                        ins = nc.scalar.activation(y[r][:, k, OURS], y[r][:, k, OURS], ACT.Copy, scale=gates[:, k, OURS:])
                    ins.then_inc(s_last, 1)
                    pause(act, s_xc, i * 2 + r + 1, s_spent)
                    nc.scalar.activation(sq_h[:], xc[:, at(i, r)], ACT.Square).then_inc(s_sq, 1)
            act.wait_ge(s_sums, 2 * TURNS)
            nc.scalar.activation(rstd[:], rstd[:], ACT.Sqrt, scale=1.0 / D, bias=C("eps")).then_inc(s_root, 1)

        @block.vector
        def _(dve):
            ch = Chain(dve, s_dve)
            v = nc.vector
            four = lambda a: a.rearrange("p t (h e) -> p t h e", e=4)

            def do(ins):
                ch.step(ins)
                ch.settle()

            with dve.Fori(0, TURNS) as i:
                ch.turn(i, 2 * GATE_STEPS)
                for r in range(2):
                    nth, g = i * 2 + r + 1, at(i, r)
                    pause(dve, s_landed[r], (i + 1) * (16 * RG), s_spent)
                    do(v.tensor_scalar(den[:], ring[:, r, :, 4:8], 1e-16, None, ALU.add))
                    do(v.reciprocal(den[:], den[:]))
                    do(v.tensor_tensor(four(agg[:]), four(ring[:, r, :, 8:24]), spread(den[:], 4), ALU.mult))
                    dve.sem_inc(s_free[r], 1)
                    do(v.tensor_tensor(agg[:], agg[:], repeat(W("b_gat"), RG), ALU.add))
                    do(v.tensor_reduce(mu[:], agg[:], AX.X, ALU.add))
                    do(v.scalar_tensor_tensor(out=agg[:], in0=spread(mu[:], 16), scalar=-1.0 / 16, in1=agg[:], op0=ALU.mult, op1=ALU.add))
                    do(v.tensor_tensor(sq[:], agg[:], agg[:], ALU.mult))
                    v.tensor_reduce(sd[:], sq[:], AX.X, ALU.add).then_inc(s_var, 1)
                    do(v.tensor_tensor(agg[:], agg[:], repeat(W("gamma"), RG), ALU.mult))
                    pause(dve, s_std, nth, s_spent)
                    do(v.reciprocal(sd[:], sd[:]))
                    do(v.tensor_tensor(agg[:], agg[:], spread(sd[:], 16), ALU.mult))
                    do(v.tensor_tensor(agg[:], agg[:], repeat(W("beta"), RG), ALU.add))
                    do(v.tensor_reduce(sc[:], agg[:].rearrange("p t (h e) -> p t e h", e=4), AX.X, ALU.add))
                    do(v.tensor_scalar(sc[:], sc[:], 0.25, None, ALU.mult))
                    for n in range(2):
                        do(v.tensor_reduce(best[:, n], sc[:], AX.X, ALU.max))
                        if n == 1:
                            v.tensor_tensor(t[:], best[:, 1], best[:, 0], ALU.subtract).then_inc(s_t, 1)
                        do(v.tensor_tensor(pick[:, n], sc[:].rearrange("p t e -> p e t"), repeat(best[:, n], 4), ALU.is_equal))
                        ch.step(v.tensor_tensor(w1[:, 0], pick[:, n, 1], pick[:, n, 0], ALU.max))
                        do(v.tensor_tensor(pick[:, n, 1], pick[:, n, 1], pick[:, n, 0], ALU.is_gt))
                        ch.step(v.tensor_tensor(w1[:, 1], pick[:, n, 2], w1[:, 0], ALU.max))
                        do(v.tensor_tensor(pick[:, n, 2], pick[:, n, 2], w1[:, 0], ALU.is_gt))
                        do(v.tensor_tensor(pick[:, n, 3], pick[:, n, 3], w1[:, 1], ALU.is_gt))
                        if n == 0:
                            do(v.scalar_tensor_tensor(out=sc[:], in0=pick[:, 0].rearrange("p e t -> p t e"), scalar=-BIG, in1=sc[:], op0=ALU.mult, op1=ALU.add))
                    pause(dve, s_exp, nth, s_spent)
                    do(v.tensor_scalar(w1[:, 0], t[:], 1.0, None, ALU.add))
                    do(v.reciprocal(w1[:, 0], w1[:, 0]))
                    do(v.tensor_tensor(w1[:, 1], t[:], w1[:, 0], ALU.mult))
                    do(v.tensor_tensor(pick[:], pick[:], w1[:].unsqueeze(2).broadcast_to([P, 2, 4, RG]), ALU.mult))
                    do(v.tensor_tensor(gates[:], pick[:, 0].rearrange("p e t -> p t e"), pick[:, 1].rearrange("p e t -> p t e"), ALU.add))
                    pause(dve, s_y[r], (i + 1) * 16, s_spent)
                    dve.sem_inc(s_gates, 1)
                    do(v.tensor_tensor(y[r][:, :, 0:OURS], y[r][:, :, 0:OURS], spread(gates[:, :, 0:OURS], D), ALU.mult))
                    pause(dve, s_last, nth, s_spent)
                    v.tensor_tensor(total[:], y[r][:, :, 0:2], y[r][:, :, 2:4], ALU.add).then_inc(s_used, 1)
                    pause(dve, s_used, i * 2 + r + 3, s_spent)
                    do(v.tensor_tensor(total[:, :, 0], total[:, :, 0], total[:, :, 1], ALU.add))
                    do(v.tensor_tensor(h[:, g], h[:, g], total[:, :, 0], ALU.add))
                    dve.sem_inc(s_spent, 1)
                    do(v.tensor_reduce(mean[:, g], h[:, g], AX.X, ALU.add))
                    v.scalar_tensor_tensor(out=xc[:, g], in0=spread(mean[:, g], D), scalar=-1.0 / D, in1=h[:, g], op0=ALU.mult, op1=ALU.add).then_inc(s_xc, 1)
                    pause(dve, s_sq, nth, s_spent)
                    v.tensor_reduce(rstd[:, g], sq_h[:], AX.X, ALU.add).then_inc(s_sums, 1)
                ch.end(TURNS)
            dve.wait_ge(s_root, 1)
            v.reciprocal(rstd[:], rstd[:])


def graph_experts(nc, mem, sorted_keys, table_dram, state_dram, end_dram, y_dram):
    with ExitStack() as ctx:
        sb = lambda name, shape, dt: ctx.enter_context(nc.sbuf_tensor(name, shape, dt))
        mem.update(zeros=sb("zeros", [P, P], BF16), first=sb("first", [P, 1], I32), has_start=sb("has_start", [P, 1], F32),
                   first_keep=sb("first_keep", [P, 1], F32), last=sb("last", [P, ROW], F32), counts=sb("counts", [P, P], F32),
                   node_end=sb("node_end", [P, TILES], I32))
        node_table(nc, mem, table_dram)
        edge_stream(nc, mem, sorted_keys, table_dram, state_dram, y_dram)
        join_runs(nc, mem, state_dram, end_dram)
        gate(nc, mem, state_dram, y_dram)


def head_attention(nc, mem):
    h, xc, rstd, C, W = mem["h"], mem["xc"], mem["rstd"], mem["C"], mem["W"]
    NG = SB * 2 * H1
    with ExitStack() as ctx:
        sb = lambda name, shape: ctx.enter_context(nc.sbuf_tensor("a1_" + name, shape, F32))
        ps = lambda name, shape: ctx.enter_context(nc.psum_tensor("a1_" + name, shape, F32))
        sem = lambda name: ctx.enter_context(nc.semaphore("a1_" + name))
        x, xt, qt, rt = sb("x", [P, 2, 2, SB, D]), sb("xt", [P, 2, T]), sb("qt", [P, 2, T]), sb("rt", [P, 2, T])
        kv, sq = sb("kv", [P, 2, 2 * NG, C1]), sb("sq", [P, 2 * NG, C1])
        mu, sd = sb("mu", [P, 2 * NG]), sb("sd", [P, 2 * NG])
        kvm = sb("kvm", [P, P])
        bias = ctx.enter_context(nc.sbuf_tensor("a1_bias", [P, SB * 2 * D + D], BF16))
        ones = ctx.enter_context(nc.sbuf_tensor("a1_ones", [P, P], BF16))
        part, rest, kept = (sb(n, [P, SB * 2 * D + D]) for n in ("part", "rest", "kept"))
        gj, sq_h = sb("gj", [P, 2, 2, SB, D]), sb("sqh", [P, ST, D])
        p_xt, p_q, p_kv, p_kvm, p_o, p_prj = (ps("p" + n, [P, 512]) for n in ("xt", "q", "kv", "kvm", "o", "prj"))
        s_bias, s_x, s_hx, s_xt_p, s_xt, s_q_p, s_q, s_kv_p, s_cent, s_sq, s_var, s_std, s_norm, s_kv, s_kvm_p, s_kvm, s_o, s_rt, s_p, s_gj, s_dve, s_pool, s_sums, s_root, s_spent = (
            sem(n) for n in ("bias", "x", "hx", "xtp", "xt", "qp", "q", "kvp", "cent", "sq", "var", "std", "norm", "kv", "kvmp", "kvm", "o", "rt", "p", "gj", "dve", "pool", "sums", "root", "spent"))
        block = ctx.enter_context(nc.Block())
        at = lambda n: bass.ds(n * ST, ST)
        by_half = lambda ap: ap.rearrange("p (b two) d -> p two b d", two=2)
        groups = p_kv[:].rearrange("p (g c) -> p g c", c=C1)
        halves = lambda r: kv[:, r].rearrange("p (two g) c -> p two (g c)", two=2)
        STAGES = 4

        @block.vector
        def _(dve):
            ch = Chain(dve, s_dve)
            v = nc.vector

            def do(ins):
                ch.step(ins)
                ch.settle()

            def step(slots, r):
                new, qkv, products, last = slots
                o = 1 - r
                if products is not None:
                    pause(dve, s_hx, products + 1, s_spent)
                if new is not None:
                    v.tensor_tensor(x[:, r], by_half(xc[:, at(new)]), by_half(spread(rstd[:, at(new)], D)), ALU.mult).then_inc(s_x, 1)
                if last is not None:
                    pause(dve, s_gj, last + 1, s_spent)
                    do(v.tensor_tensor(by_half(h[:, at(last)]), by_half(h[:, at(last)]), gj[:, o], ALU.add))
                if qkv is not None:
                    pause(dve, s_kv_p, qkv + 1, s_spent)
                    do(v.tensor_reduce(mu[:], groups, AX.X, ALU.add))
                    v.scalar_tensor_tensor(out=kv[:, o], in0=spread(mu[:], C1), scalar=-1.0 / C1, in1=groups, op0=ALU.mult, op1=ALU.add).then_inc(s_cent, 1)
                if last is not None:
                    ln_centre(do, lambda: dve.sem_inc(s_spent, 1), v, mem, at(last))
                if qkv is not None:
                    pause(dve, s_sq, qkv + 1, s_spent)
                    v.tensor_reduce(sd[:], sq[:], AX.X, ALU.add).then_inc(s_var, 1)
                if products is not None:
                    pause(dve, s_kvm_p, products + 1, s_spent)
                    v.tensor_tensor(kvm[:], p_kvm[:, 0:P], C("own_head"), ALU.mult).then_inc(s_kvm, 1)
                if last is not None:
                    ln_squares(do, lambda: dve.sem_inc(s_spent, 1), v, mem, at(last), sq_h[:])
                if products is not None:
                    pause(dve, s_o, products + 1, s_spent)
                    v.tensor_tensor(rt[:, r], p_o[:, 0:T], xt[:, r], ALU.add).then_inc(s_rt, 1)
                if qkv is not None:
                    pause(dve, s_std, qkv + 1, s_spent)
                    do(v.tensor_scalar(sd[:], sd[:], EPS, None, ALU.add))
                    do(v.reciprocal(sd[:], sd[:]))
                    v.tensor_tensor(kv[:, o], kv[:, o], spread(sd[:], C1), ALU.mult).then_inc(s_norm, 1)

            ch.step(v.memset(ones[:], 1.0))
            both = mem["w"][:, WEIGHT["kv_b"][0]:sum(WEIGHT["proj_b"])]
            exact_rows(do, v, bias[:], both, part[:], rest[:], kept[:], C)
            dve.sem_inc(s_bias, 1)
            staggered(dve, step, STAGES, ch, 2 * (4 + LN_STEPS))
            ln_finish(nc, mem, dve, s_sums, s_root)

        @block.gpsimd
        def _(pool):
            def step(slots, r):
                new, qkv, _, _ = slots
                o = 1 - r
                if new is not None:
                    pause(pool, s_x, new + 1, s_spent)
                    nc.gpsimd.tensor_tensor(by_half(h[:, at(new)]), by_half(h[:, at(new)]), x[:, r], ALU.add).then_inc(s_hx, 1)
                if qkv is not None:
                    pause(pool, s_norm, qkv + 1, s_spent)
                    nc.gpsimd.tensor_tensor(halves(o), halves(o), repeat(W("kv_ln_w"), 2), ALU.mult).then_inc(s_pool, 1)
                    pause(pool, s_pool, qkv + 1, s_spent)
                    nc.gpsimd.tensor_tensor(halves(o), halves(o), repeat(W("kv_ln_b"), 2), ALU.add).then_inc(s_kv, 1)

            staggered(pool, step, STAGES)

        @block.tensor
        def _(pe):
            def step(slots, r):
                new, qkv, products, last = slots
                o = 1 - r
                if qkv is not None:
                    pause(pe, s_xt, qkv + 1, s_spent)
                    for half in range(2):
                        mm = pe.matmul(p_kv[:, half * T:half * T + T], xt[:, o, half * P:half * P + P], W("kv_w"), start=False, stop=(half == 1))
                    mm.then_inc(s_kv_p, 1)
                if products is not None:
                    pause(pe, s_q, products + 1, s_spent)
                if qkv is not None:
                    pe.matmul(p_q[:, 0:T], W("q_w"), xt[:, o], start=True, stop=True).then_inc(s_q_p, 1)
                if products is not None:
                    pause(pe, s_kv, products + 1, s_spent)
                    for half in range(2):
                        mm = pe.matmul(p_kvm[:, 0:P], halves(r)[:, half, 0:P], halves(r)[:, half, P:2 * P], start=(half == 0), stop=(half == 1))
                    mm.then_inc(s_kvm_p, 1)
                    pause(pe, s_kvm, products + 1, s_spent)
                    pe.matmul(p_o[:, 0:T], kvm[:], qt[:, r], start=True, stop=True).then_inc(s_o, 1)
                if new is not None:
                    pause(pe, s_x, new + 1, s_spent)
                    for half in range(2):
                        mm = pe.transpose(p_xt[:, half * P:half * P + P], x[:, r, half].rearrange("p b d -> p (b d)"), C("ident"))
                    mm.then_inc(s_xt_p, 1)
                if products is not None:
                    if last is not None:
                        pause(pe, s_gj, last + 1, s_spent)
                    pe.matmul(p_prj[:, 0:ST * D], ones[0:3], repeat(bias[0:3, SB * 2 * D:], ST), start=True, stop=False)
                    pause(pe, s_rt, products + 1, s_spent)
                    for half in range(2):
                        mm = pe.matmul(p_prj[:, half * P:half * P + P], rt[:, r, half * P:half * P + P], W("proj_w"), start=False, stop=(half == 1))
                    mm.then_inc(s_p, 1)
                if new is not None:
                    if qkv is not None:
                        pause(pe, s_cent, qkv + 1, s_spent)
                    pe.matmul(p_kv[:], ones[0:3], repeat(bias[0:3, 0:SB * 2 * D], 2), start=True, stop=False)

            pe.wait_ge(s_bias, 1)
            staggered(pe, step, STAGES)

        @block.scalar
        def _(act):
            a = nc.scalar

            def step(slots, r):
                new, qkv, products, _ = slots
                o = 1 - r
                if qkv is not None:
                    pause(act, s_cent, qkv + 1, s_spent)
                    a.activation(sq[:], kv[:, o], ACT.Square).then_inc(s_sq, 1)
                    pause(act, s_q_p, qkv + 1, s_spent)
                    a.activation(qt[:, o], p_q[:, 0:T], ACT.Identity, bias=W("q_b")).then_inc(s_q, 1)
                    pause(act, s_var, qkv + 1, s_spent)
                    a.activation(sd[:], sd[:], ACT.Sqrt, scale=1.0 / (C1 - 1)).then_inc(s_std, 1)
                if new is not None:
                    if products is not None:
                        pause(act, s_rt, products + 1, s_spent)
                    pause(act, s_xt_p, new + 1, s_spent)
                    a.activation(xt[:, r], p_xt[:, 0:T], ACT.Copy).then_inc(s_xt, 1)
                if products is not None:
                    pause(act, s_p, products + 1, s_spent)
                    a.activation(gj[:, r].rearrange("p two b d -> p (two b d)"), p_prj[:, 0:ST * D], ACT.Gelu).then_inc(s_gj, 1)

            staggered(act, step, STAGES)
            ln_root(nc, mem, act, s_sums, s_root)


def route(nc, mem, route_dram):
    xc, rstd, C, W = mem["xc"], mem["rstd"], mem["C"], mem["W"]
    Q = TILES // 4
    with ExitStack() as ctx:
        sem = lambda name: ctx.enter_context(nc.semaphore("rt_" + name))
        prod = ctx.enter_context(nc.sbuf_tensor("rt_prod", [P, Q, D], F32))
        turned = ctx.enter_context(nc.sbuf_tensor("rt_turned", [P, P], F32))
        p_t = ctx.enter_context(nc.psum_tensor("rt_pt", [P, P], F32))
        s_dve, s_w, s_p, s_t, s_out = (sem(n) for n in ("dve", "w", "p", "t", "out"))
        block = ctx.enter_context(nc.Block())
        rw = mem["route"]

        @block.vector
        def _(dve):
            ch = Chain(dve, s_dve)
            v = nc.vector
            for q in range(4):
                t = slice(q * Q, q * Q + Q)
                ch.step(v.tensor_tensor(prod[:], xc[:, t], repeat(W("route_w"), Q), ALU.mult)); ch.settle()
                ch.step(v.tensor_reduce(rw[:, t], prod[:], AX.X, ALU.add)); ch.settle()
            ch.step(v.tensor_tensor(rw[:], rw[:], rstd[:], ALU.mult)); ch.settle()
            v.tensor_scalar(rw[:], rw[:], W("route_b"), None, ALU.add).then_inc(s_w, 1)
            dve.wait_ge(s_p, 1)
            v.tensor_copy(turned[:], p_t[:]).then_inc(s_t, 1)

        @block.tensor
        def _(pe):
            pe.wait_ge(s_w, 1)
            pe.transpose(p_t[:], rw[:], C("ident")).then_inc(s_p, 1)

        @block.sync
        def _(sp):
            sp.wait_ge(s_t, 1)
            sp.dma_start(route_dram.rearrange("(t p) -> t p", p=P), turned[:]).then_inc(s_out, 16)
            sp.wait_ge(s_out, 16)


def depth_mlp(nc, mem, route_dram):
    h, xc, rstd, C, W = mem["h"], mem["xc"], mem["rstd"], mem["C"], mem["W"]
    with ExitStack() as ctx:
        sb = lambda name, shape: ctx.enter_context(nc.sbuf_tensor("m_" + name, shape, F32))
        ps = lambda name, shape: ctx.enter_context(nc.psum_tensor("m_" + name, shape, F32))
        sem = lambda name: ctx.enter_context(nc.semaphore("m_" + name))
        mem["route"] = sb("route", [P, TILES])
        route(nc, mem, route_dram)
        x, xt, hid = sb("x", [P, 2, 2, SB, D]), sb("xt", [P, 2, T]), sb("hid", [P, 2, 2, SN])
        y = sb("y", [P, ST, D])
        every = sb("every", [P, 2, SB, T])
        own, cmp = sb("own", [P, ST]), sb("cmp", [P, 2, ST, T])
        rank, kept = sb("rank", [P, 2, ST]), sb("kept", [P, 2, ST])
        p_xt, p_hid, p_y = ps("pxt", [P, 512]), [ps("phid%d" % m, [P, SB, 512]) for m in range(2)], [ps("py%d" % r, [P, 512]) for r in range(2)]
        y_p = lambda r: p_y[r][:, 0:ST * D].rearrange("p (t d) -> p t d", d=D)
        s_x, s_hx, s_xt_p, s_xt, s_hid_p, s_hid, s_y_p, s_dve, s_every, s_ranked, s_taken, s_spent = (
            sem(n) for n in ("x", "hx", "xtp", "xt", "hidp", "hid", "yp", "dve", "every", "ranked", "taken", "spent"))
        block = ctx.enter_context(nc.Block())
        at = lambda n: bass.ds(n * ST, ST)
        by_half = lambda ap: ap.rearrange("p (b two) d -> p two b d", two=2)
        STAGES = 4

        @block.sync
        def _(sp):
            sp.sem_inc(s_ranked, 2)
            rows = route_dram.rearrange("(g n) -> g n", n=SN)
            with sp.Fori(0, TURNS) as i:
                for r in range(2):
                    pause(sp, s_ranked, i * 2 + r + 1, s_spent)
                    sp.dma_start(every[:, r].rearrange("p b t -> p (b t)"), rows[bass.ds(i * 2 + r, 1), :].broadcast_to([P, SN])).then_inc(s_every, 16)
                    pause(sp, s_every, (i * 2 + r + 1) * 16, s_spent)

        @block.vector
        def _(dve):
            ch = Chain(dve, s_dve)
            v = nc.vector

            def do(ins):
                ch.step(ins)
                ch.settle()

            def step(slots, r):
                new, _, ranks, last = slots
                o = 1 - r
                if ranks is not None:
                    pause(dve, s_hx, ranks + 1, s_spent)
                    pause(dve, s_xt_p, ranks + 1, s_spent)
                if new is not None:
                    v.tensor_tensor(x[:, r], by_half(xc[:, at(new)]), by_half(spread(rstd[:, at(new)], D)), ALU.mult).then_inc(s_x, 1)
                if ranks is not None:
                    do(v.tensor_copy(own[:], mem["route"][:, at(ranks)]))
                    pause(dve, s_every, (ranks + 1) * 16, s_spent)
                    for t in range(ST):
                        them = every[:, r, t // 2, :]
                        ch.step(v.tensor_scalar(cmp[:, 0, t], them, own[:, t:t + 1], None, ALU.is_gt, op1=ALU.add, accum_out=rank[:, 0, t:t + 1]))
                        ch.step(v.scalar_tensor_tensor(out=cmp[:, 1, t], in0=them, scalar=own[:, t:t + 1], in1=C("ties")[:, (t % 2) * T:(t % 2) * T + T], op0=ALU.is_equal, op1=ALU.mult, accum_out=rank[:, 1, t:t + 1]))
                    ch.settle()
                    dve.sem_inc(s_ranked, 1)
                    do(v.tensor_tensor(rank[:, 0], rank[:, 0], rank[:, 1], ALU.add))
                    do(v.tensor_scalar(rank[:, 0], rank[:, 0], KEEP - 0.5, None, ALU.is_lt))
                    do(v.tensor_tensor(kept[:, r], rank[:, 0], own[:], ALU.mult))
                if last is not None:
                    pause(dve, s_y_p, last + 1, s_spent)
                    do(v.tensor_tensor(y[:], y_p(o), repeat(W("m_b2"), ST), ALU.add))
                    dve.sem_inc(s_taken, 1)
                    do(v.tensor_tensor(y[:], y[:], spread(kept[:, o], D), ALU.mult))
                    do(v.tensor_tensor(h[:, at(last)], h[:, at(last)], y[:], ALU.add))

            staggered(dve, step, STAGES, ch, 2 * (2 * ST + 7))

        @block.gpsimd
        def _(pool):
            def step(slots, r):
                new = slots[0]
                if new is not None:
                    pause(pool, s_x, new + 1, s_spent)
                    nc.gpsimd.tensor_tensor(by_half(h[:, at(new)]), by_half(h[:, at(new)]), x[:, r], ALU.add).then_inc(s_hx, 1)

            staggered(pool, step, STAGES)

        @block.tensor
        def _(pe):
            def step(slots, r):
                new, hidden, output, last = slots
                o = 1 - r
                if hidden is not None:
                    pause(pe, s_xt, hidden + 1, s_spent)
                if output is not None:
                    pause(pe, s_hid, output * 2 + 2, s_spent)
                if hidden is not None:
                    for m in range(2):
                        for b in range(SB):
                            mm = pe.matmul(p_hid[m][:, b, 0:T], W("m_w1")[b * D:b * D + D, m * P:m * P + P], xt[b * D:b * D + D, o], start=True, stop=True)
                        mm.then_inc(s_hid_p, 1)
                if new is not None:
                    pause(pe, s_x, new + 1, s_spent)
                    for half in range(2):
                        mm = pe.transpose(p_xt[:, half * P:half * P + P], x[:, r, half].rearrange("p b d -> p (b d)"), C("ident"))
                    mm.then_inc(s_xt_p, 1)
                if output is not None:
                    if not isinstance(output, int) or output >= 2:
                        pause(pe, s_taken, output - 1, s_spent)
                    for t in range(ST):
                        for m in range(2):
                            mm = pe.matmul(y_p(r)[:, t, :], hid[:, r, m, t * P:t * P + P], W("m_w2")[:, m * D:m * D + D], start=(m == 0), stop=(m == 1))
                    mm.then_inc(s_y_p, 1)

            staggered(pe, step, STAGES)

        @block.scalar
        def _(act):
            def step(slots, r):
                new, hidden = slots[:2]
                o = 1 - r
                if hidden is not None:
                    for m in range(2):
                        pause(act, s_hid_p, hidden * 2 + m + 1, s_spent)
                        nc.scalar.activation(hid[:, o, m].rearrange("p (b t) -> p b t", b=SB), p_hid[m][:, :, 0:T], ACT.Gelu_apprx_tanh, bias=W("m_b1")[:, m:m + 1]).then_inc(s_hid, 1)
                if new is not None:
                    pause(act, s_xt_p, new + 1, s_spent)
                    nc.scalar.activation(xt[:, r], p_xt[:, 0:T], ACT.Copy).then_inc(s_xt, 1)

            staggered(act, step, STAGES)


def lm_tower_kernel(nc, ids, emb_2, emb_3, emb_4, edges, consts, weights, scratch, out):
    sorted_keys, table_dram, state_dram, top_dram, wt_dram, end_dram, y_dram = scratch
    with ExitStack() as ctx:
        sb = lambda name, shape, dt: ctx.enter_context(nc.sbuf_tensor(name, shape, dt))
        mem = {"c": sb("consts", [P, CONST_N], F32), "w": sb("weights", [P, WEIGHT_N], F32),
               "h": sb("h", [P, TILES, D], F32), "mean": sb("mean", [P, TILES], F32), "rstd": sb("rstd", [P, TILES], F32),
               "top_dram": top_dram, "s_weights": ctx.enter_context(nc.semaphore("s_weights"))}
        mem["C"] = lambda name: mem["c"][:, CONST[name][0]:sum(CONST[name])]
        mem["W"] = lambda name: mem["w"][:, WEIGHT[name][0]:sum(WEIGHT[name])]
        h = mem["h"]
        mem["xc"] = sb("xc", [P, TILES, D], F32)
        with nc.sbuf_tensor("e3", [P, TILES, D], F32) as e3:
            mem["e3"] = e3
            embed_and_sort(nc, mem, ids, (emb_2, emb_3, emb_4), edges, consts, weights, sorted_keys)
        phase_attention(nc, mem)
        graph_experts(nc, mem, sorted_keys, table_dram, state_dram, end_dram, y_dram)
        head_attention(nc, mem)
        depth_mlp(nc, mem, wt_dram)
        with nc.semaphore("s_out") as s_out, nc.Block() as block:
            @block.sync
            def _(sp):
                sp.dma_start(out.rearrange("b (two p) d -> p b two d", p=P), h[:].rearrange("p (b two) d -> p b two d", two=2)).then_inc(s_out, 16)
                sp.wait_ge(s_out, 16)


def shape_constants():
    import numpy as np
    p = np.arange(P)
    f = np.float32
    bits = [1.0 - 2.0 * ((p >> b) & 1) for b in range(7)]
    two_pi_half = np.pi
    c = {
        "ident": np.eye(P), "causal": np.concatenate([np.arange(T)[None] >= p[:, None], (p[None] >= p[:, None])], 1),
        "rnorm": 1.0 / np.sqrt(np.stack([p + 1, p + P + 1], 1) * float(K)),
        "emb_scale": np.stack([np.where((p < n + 1) & (half == 0), 0.0, 0.25) for n in range(3) for half in range(2)], 1),
        "fold": np.where(p % 64 < K, -1.0, 1.0)[:, None], "sin_scale": np.where(p % 64 < K, -two_pi_half, two_pi_half)[:, None],
        "sin_bias": np.where(p % 64 < K, two_pi_half / 2, 0.0)[:, None], "eps": np.full((P, 1), EPS),
        "iota": np.tile(p[None], (P, 1)), "bit_sign": np.stack(bits, 1),
        "flip": np.stack([-bits[0]] + [bits[b] * bits[b + 1] for b in range(6)], 1),
        "before": p[:, None] < p[None], "ties": np.concatenate([np.arange(T)[None] < p[:, None], np.arange(T)[None] < p[:, None] + P], 1),
        "own_head": np.where(p[:, None] // C1 == p[None] // C1, 1.0 / T, 0.0),
        "zero": np.zeros((P, 1)), "ones": np.ones((P, 1)), "ones_row": np.ones((P, P)),
        "all_but_last": np.tile((p[None] < P - 1), (P, 1)), "slice_end": ((p + 1) * float(ALL_COLS))[:, None],
    }
    out = np.zeros((P, CONST_N), f)
    for name, (at, width) in CONST.items():
        out[:, at:at + width] = c[name]
    return out


def lay_out_weights(a):
    import numpy as np
    row = lambda v: np.broadcast_to(np.asarray(v).reshape(1, -1), (P, np.asarray(v).size))
    col = lambda *vs: np.concatenate([np.asarray(v).reshape(-1, 1) for v in vs], 0)
    qkv_w = np.asarray(a["L1_attn_W_qkv"]).reshape(H1, 3, C1, D)
    qkv_b = np.asarray(a["L1_attn_b_qkv"]).reshape(H1, 3, C1)
    under = lambda m, bias: np.concatenate([np.asarray(m), np.asarray(bias).reshape(1, -1)], 0)
    side = lambda m: np.concatenate([np.asarray(m[e]) for e in range(m.shape[0])], 1)
    kkvv = lambda k, v: np.concatenate([np.asarray(m).reshape(-1) for m in (k, k, v, v)])

    def twice(m):
        m = np.asarray(m)
        both = np.zeros((2 * m.shape[0], 2 * m.shape[1]), m.dtype)
        both[:m.shape[0], :m.shape[1]] = m
        both[m.shape[0]:, m.shape[1]:] = m
        return both

    beside = lambda m: np.concatenate([np.asarray(m)] * 2, 1)
    w = {
        "k_w1": twice(a["L0_attn_kw1"].T), "q_w1": twice(a["L0_attn_qw1"].T),
        "k_w2": twice(beside(a["L0_attn_kw2"].T)), "q_w2": twice(beside(a["L0_attn_qw2"].T)), "v_w": twice(a["L0_attn_vw"].T),
        "k_b1": col(*[a["L0_attn_kb1"]] * 2), "q_b1": col(*[a["L0_attn_qb1"]] * 2),
        "k_b2": col(*[a["L0_attn_kb2"]] * 4), "q_b2": col(*[a["L0_attn_qb2"]] * 4),
        "v_b": row(a["L0_attn_vb"]), "w_gat": twice(a["L0_ffn_W_gat"]), "att_src": row(a["L0_ffn_att_src"]),
        "att_dst": row(a["L0_ffn_att_dst"]), "b_gat": row(a["L0_ffn_b_gat"]), "gamma": row(a["L0_ffn_ln_gamma"]),
        "beta": row(a["L0_ffn_ln_beta"]), "e_w1": side(a["L0_ffn_W1"]), "e_b1": a["L0_ffn_b1"].T,
        "e_w2": side(a["L0_ffn_W2"]), "e_b2": row(a["L0_ffn_b2"]),
        "q_w": twice(qkv_w[:, 0].reshape(D, D).T), "q_b": col(*[qkv_b[:, 0]] * 2),
        "kv_w": np.concatenate([twice(qkv_w[:, n].reshape(D, D).T) for n in (1, 2)], 1), "kv_b": row(kkvv(qkv_b[:, 1], qkv_b[:, 2])),
        "kv_ln_w": row(kkvv(a["L1_attn_kln_w"], a["L1_attn_vln_w"])), "kv_ln_b": row(kkvv(a["L1_attn_kln_b"], a["L1_attn_vln_b"])),
        "proj_w": twice(a["L1_attn_W_proj"].T), "proj_b": row(a["L1_attn_b_proj"]),
        "route_w": row(a["L1_ffn_wr"]), "route_b": row(a["L1_ffn_br"]), "m_w1": np.concatenate([a["L1_ffn_w1"]] * 2, 0),
        "m_b1": np.asarray(a["L1_ffn_b1"]).reshape(2, P).T, "m_w2": np.concatenate([a["L1_ffn_w2"][:P], a["L1_ffn_w2"][P:]], 1),
        "m_b2": row(a["L1_ffn_b2"]),
    }
    out = np.zeros((P, WEIGHT_N), np.float32)
    for name, (at, width) in WEIGHT.items():
        out[:w[name].shape[0], at:at + width] = w[name]
    return out


def kernel(**inputs):
    import numpy as _np
    import concourse.bacc as _bacc
    from concourse import mybir as _mybir
    from concourse.bass_utils import run_bass_kernel_spmd as _run

    nc = _bacc.Bacc("TRN2", target_bir_lowering=False, num_devices=1)
    a = {k: _np.asarray(v) for k, v in inputs.items()}
    arrays = {"ids": a["x"], "emb_2": a["L0_tok_emb_2"], "emb_3": a["L0_tok_emb_3"], "emb_4": a["L0_tok_emb_4"],
              "edges": a["L0_ffn_edge_index"], "consts": shape_constants(), "weights": lay_out_weights(a)}
    args = [nc.dram_tensor("in_" + n, v.shape, _mybir.dt.from_np(v.dtype), kind="ExternalInput").ap() for n, v in arrays.items()]
    scratch = [nc.dram_tensor(n, shape, F32, kind="Internal").ap() for n, shape in (
        ("sorted_keys", (EDGES + M,)), ("node_table", (M, ROW)), ("edge_states", (EDGES + M, ROW)), ("top_keys", (M,)), ("route", (B * T,)), ("node_ends", (M, 1)), ("expert_outputs", (M, EXPERTS * D)))]
    out = nc.dram_tensor("out_0_dram", (B, T, D), F32, kind="ExternalOutput").ap()
    lm_tower_kernel(nc, *args, scratch, out)
    r = _run(nc, [{"in_" + n: _np.ascontiguousarray(v) for n, v in arrays.items()}], core_ids=[0])
    return r.results[0]["out_0_dram"]
```
